# Optimizing a Trainium2 kernel written in Bass

```python
import numpy as np
import jax
import jax.numpy as jnp

def _softmax(x, axis=-1):
    return jax.nn.softmax(x, axis=axis)

def _gelu(x):
    return jax.nn.gelu(x, approximate=True)

def _silu(x):
    return jax.nn.silu(x)

def _sigmoid(x):
    return jax.nn.sigmoid(x)

def _layernorm(x, axis=-1, eps=1e-05):
    m = jnp.mean(x, axis=axis, keepdims=True)
    v = jnp.var(x, axis=axis, keepdims=True)
    return (x - m) / jnp.sqrt(v + eps)

def _scatter_add(tgt, idx, src, axis=0):
    return tgt.at[idx].add(src)

def _segment_sum(src, seg, n):
    return jax.ops.segment_sum(src, seg, n)
kernel_name = 'mk_hybrid_d1_jaxref_r8_8ee5cd'

def setup_inputs(seed: int=0):
    np.random.seed(seed)
    _w = jnp.asarray

    def _L0_attn_a_setup():
        import jax, jax.numpy as jnp
        import numpy as np
        BLOCK = 32
        NUM_HEADS = 16
        HEAD_DIM = 128
        FP4_GRID = jnp.array([0.0, 0.5, 1.0, 1.5, 2.0, 3.0, 4.0, 6.0], dtype=jnp.float32)

        def quantize_to_mxfp4(w, block_size=BLOCK):
            D, F = w.shape
            blocks = w.reshape(D // block_size, block_size, F)
            amax = jnp.max(jnp.abs(blocks), axis=1)
            e = jnp.floor(jnp.log2(jnp.maximum(amax, 1e-12) / 6.0))
            scale = jnp.exp2(e)
            v = blocks / scale[:, None, :]
            idx = jnp.argmin(jnp.abs(jnp.abs(v)[..., None] - FP4_GRID), axis=-1)
            codes = jnp.sign(v) * FP4_GRID[idx]
            return (codes.reshape(D, F).astype(jnp.float32), scale.astype(jnp.float32))

        def _mxfp4_matmul(x, codes, scales, block_size=BLOCK):
            w = codes * jnp.repeat(scales, block_size, axis=0)
            return x @ w
        key = jax.random.key(seed)
        ks = jax.random.split(key, 9)
        B, S, D = (2, 256, 256)
        feat = NUM_HEADS * HEAD_DIM
        x = jax.random.normal(ks[0], (B, S, D), dtype=jnp.float32)

        def make_w(k, din, dout):
            w = jax.random.normal(k, (din, dout), dtype=jnp.float32) * (1.0 / np.sqrt(din))
            return quantize_to_mxfp4(w, BLOCK)
        wq_codes, wq_scales = make_w(ks[1], D, feat)
        wk_codes, wk_scales = make_w(ks[2], D, feat)
        wv_codes, wv_scales = make_w(ks[3], D, feat)
        wo_codes, wo_scales = make_w(ks[4], feat, D)
        bq = jnp.zeros((feat,), jnp.float32)
        bk = jnp.zeros((feat,), jnp.float32)
        bv = jnp.zeros((feat,), jnp.float32)
        bo = jnp.zeros((D,), jnp.float32)
        return {'x': x, 'wq_codes': wq_codes, 'wq_scales': wq_scales, 'bq': bq, 'wk_codes': wk_codes, 'wk_scales': wk_scales, 'bk': bk, 'wv_codes': wv_codes, 'wv_scales': wv_scales, 'bv': bv, 'wo_codes': wo_codes, 'wo_scales': wo_scales, 'bo': bo}
    _L0_attn_a_in = _L0_attn_a_setup()

    def _L0_attn_b_setup():
        import math
        import jax, jax.numpy as jnp
        import numpy as np
        HID = 256
        H = 16
        HKV = 8
        D = HID // H
        F = D
        SEQ = 256
        BATCH = 2
        THETA = 10000.0

        def _rotate_half(x):
            x1, x2 = (x[..., :x.shape[-1] // 2], x[..., x.shape[-1] // 2:])
            return jnp.concatenate((-x2, x1), axis=-1)

        def _softmax_kernel(x, R):
            n = jnp.sqrt(jnp.sum(x * x, axis=-1, keepdims=True))
            x = x / jnp.maximum(n, 1e-06)
            p = jnp.einsum('...d,ed->...e', x, R)
            feats = jnp.concatenate([jnp.sin(p), jnp.cos(p)], axis=-1)
            return feats / math.sqrt(F)
        key = jax.random.key(seed)
        ks = jax.random.split(key, 10)
        s = lambda k, shape, scale=0.02: jax.random.normal(k, shape, dtype=jnp.float32) * scale
        return {'hidden_states': jax.random.normal(ks[0], (BATCH, SEQ, HID), dtype=jnp.float32), 'Wq': s(ks[1], (HID, HID)), 'bq': s(ks[2], (HID,)), 'Wk': s(ks[3], (HKV * D, HID)), 'bk': s(ks[4], (HKV * D,)), 'Wv': s(ks[5], (HKV * D, HID)), 'bv': s(ks[6], (HKV * D,)), 'Wo': s(ks[7], (HID, HID)), 'bo': s(ks[8], (HID,)), 'rand_matrix': jax.random.normal(ks[9], (F // 2, D), dtype=jnp.float32)}
    _L0_attn_b_in = _L0_attn_b_setup()

    def _L0_ffn_setup():
        import jax, jax.numpy as jnp
        import numpy as np
        NUM_EXPERTS = 32
        TOP_K = 8
        SELECT_TOP_K = 4
        THRESHOLD = 0.5
        HIDDEN = 256
        D_FF = 96

        def _moe_forward(hidden_states, gate_weight, gate_up_proj, down_proj, similarity):
            B, S_len, H = hidden_states.shape
            E, K, Ssel = (NUM_EXPERTS, TOP_K, SELECT_TOP_K)
            x = hidden_states.reshape(-1, H)
            router_logits = x @ gate_weight.T
            router_probs = jax.nn.softmax(router_logits.astype(jnp.float32), axis=-1).astype(router_logits.dtype)
            router_top_value, router_indices = jax.lax.top_k(router_probs, K)
            routing_weights = router_top_value / jnp.clip(jnp.sum(router_top_value, axis=-1, keepdims=True), 1e-12, None)
            sim = similarity.astype(jnp.float32)
            sim = sim.at[jnp.arange(E), jnp.arange(E)].set(1.0)
            prim = router_indices[:, :Ssel]
            sec = router_indices[:, Ssel:]
            sim_cand = sim[sec[:, :, None], prim[:, None, :]]
            best_sim = jnp.max(sim_cand, axis=-1)
            best_i = jnp.argmax(sim_cand, axis=-1)
            prim_rep = jnp.broadcast_to(prim[:, None, :], sim_cand.shape)
            best_primary = jnp.take_along_axis(prim_rep, best_i[..., None], axis=-1)[..., 0]
            new_sec = jnp.where(best_sim < THRESHOLD, sec, best_primary) if THRESHOLD > 0.0 else best_primary
            rerouted_indices = jnp.concatenate([prim, new_sec], axis=1)
            combine = jnp.sum(jax.nn.one_hot(rerouted_indices, E, dtype=routing_weights.dtype) * routing_weights[..., None], axis=1)

            def expert_step(y, params):
                wgu, wd, cw = params
                gu = x @ wgu.T
                g, u = jnp.split(gu, 2, axis=-1)
                h = jax.nn.silu(g) * u
                y = y + h @ wd.T * cw[:, None]
                return (y, None)
            y0 = jnp.zeros_like(x)
            y, _ = jax.lax.scan(expert_step, y0, (gate_up_proj, down_proj, combine.T))
            return y.reshape(B, S_len, H)
        key = jax.random.key(seed)
        ks = jax.random.split(key, 5)
        hidden_states = jax.random.normal(ks[0], (4, 256, HIDDEN), dtype=jnp.float32)
        gate_weight = jax.random.normal(ks[1], (NUM_EXPERTS, HIDDEN), dtype=jnp.float32) * 0.02
        gate_up_proj = jax.random.normal(ks[2], (NUM_EXPERTS, 2 * D_FF, HIDDEN), dtype=jnp.float32) * 0.02
        down_proj = jax.random.normal(ks[3], (NUM_EXPERTS, HIDDEN, D_FF), dtype=jnp.float32) * 0.02
        similarity = jax.random.uniform(ks[4], (NUM_EXPERTS, NUM_EXPERTS), dtype=jnp.float32)
        return {'hidden_states': hidden_states, 'gate_weight': gate_weight, 'gate_up_proj': gate_up_proj, 'down_proj': down_proj, 'similarity': similarity}
    _L0_ffn_in = _L0_ffn_setup()
    _d = {'L0_attn_a_x': _L0_attn_a_in['x'], 'L0_attn_a_wq_codes': _L0_attn_a_in['wq_codes'], 'L0_attn_a_wq_scales': _L0_attn_a_in['wq_scales'], 'L0_attn_a_bq': _L0_attn_a_in['bq'], 'L0_attn_a_wk_codes': _L0_attn_a_in['wk_codes'], 'L0_attn_a_wk_scales': _L0_attn_a_in['wk_scales'], 'L0_attn_a_bk': _L0_attn_a_in['bk'], 'L0_attn_a_wv_codes': _L0_attn_a_in['wv_codes'], 'L0_attn_a_wv_scales': _L0_attn_a_in['wv_scales'], 'L0_attn_a_bv': _L0_attn_a_in['bv'], 'L0_attn_a_wo_codes': _L0_attn_a_in['wo_codes'], 'L0_attn_a_wo_scales': _L0_attn_a_in['wo_scales'], 'L0_attn_a_bo': _L0_attn_a_in['bo'], 'L0_attn_b_Wq': _L0_attn_b_in['Wq'], 'L0_attn_b_bq': _L0_attn_b_in['bq'], 'L0_attn_b_Wk': _L0_attn_b_in['Wk'], 'L0_attn_b_bk': _L0_attn_b_in['bk'], 'L0_attn_b_Wv': _L0_attn_b_in['Wv'], 'L0_attn_b_bv': _L0_attn_b_in['bv'], 'L0_attn_b_Wo': _L0_attn_b_in['Wo'], 'L0_attn_b_bo': _L0_attn_b_in['bo'], 'L0_attn_b_rand_matrix': _L0_attn_b_in['rand_matrix'], 'L0_ffn_gate_weight': _L0_ffn_in['gate_weight'], 'L0_ffn_gate_up_proj': _L0_ffn_in['gate_up_proj'], 'L0_ffn_down_proj': _L0_ffn_in['down_proj'], 'L0_ffn_similarity': _L0_ffn_in['similarity']}
    _x0 = _d['L0_attn_a_x']
    _d['L0_attn_a_x'] = jax.random.normal(jax.random.fold_in(jax.random.key(seed), 1), (1, 2048, 256), dtype=_x0.dtype)
    del _x0
    return _d

def reference(L0_attn_a_x, L0_attn_a_wq_codes, L0_attn_a_wq_scales, L0_attn_a_bq, L0_attn_a_wk_codes, L0_attn_a_wk_scales, L0_attn_a_bk, L0_attn_a_wv_codes, L0_attn_a_wv_scales, L0_attn_a_bv, L0_attn_a_wo_codes, L0_attn_a_wo_scales, L0_attn_a_bo, L0_attn_b_Wq, L0_attn_b_bq, L0_attn_b_Wk, L0_attn_b_bk, L0_attn_b_Wv, L0_attn_b_bv, L0_attn_b_Wo, L0_attn_b_bo, L0_attn_b_rand_matrix, L0_ffn_gate_weight, L0_ffn_gate_up_proj, L0_ffn_down_proj, L0_ffn_similarity):

    def _L0_attn_a_ref(x, wq_codes, wq_scales, bq, wk_codes, wk_scales, bk, wv_codes, wv_scales, bv, wo_codes, wo_scales, bo):
        import jax, jax.numpy as jnp
        import numpy as np
        BLOCK = 32
        NUM_HEADS = 16
        HEAD_DIM = 128
        FP4_GRID = jnp.array([0.0, 0.5, 1.0, 1.5, 2.0, 3.0, 4.0, 6.0], dtype=jnp.float32)

        def quantize_to_mxfp4(w, block_size=BLOCK):
            D, F = w.shape
            blocks = w.reshape(D // block_size, block_size, F)
            amax = jnp.max(jnp.abs(blocks), axis=1)
            e = jnp.floor(jnp.log2(jnp.maximum(amax, 1e-12) / 6.0))
            scale = jnp.exp2(e)
            v = blocks / scale[:, None, :]
            idx = jnp.argmin(jnp.abs(jnp.abs(v)[..., None] - FP4_GRID), axis=-1)
            codes = jnp.sign(v) * FP4_GRID[idx]
            return (codes.reshape(D, F).astype(jnp.float32), scale.astype(jnp.float32))

        def _mxfp4_matmul(x, codes, scales, block_size=BLOCK):
            w = codes * jnp.repeat(scales, block_size, axis=0)
            return x @ w
        B, S, D = x.shape
        q = _mxfp4_matmul(x, wq_codes, wq_scales) + bq
        k = _mxfp4_matmul(x, wk_codes, wk_scales) + bk
        v = _mxfp4_matmul(x, wv_codes, wv_scales) + bv
        q = q.reshape(B, S, NUM_HEADS, HEAD_DIM)
        k = k.reshape(B, S, NUM_HEADS, HEAD_DIM)
        v = v.reshape(B, S, NUM_HEADS, HEAD_DIM)
        scores = jnp.einsum('bqhd,bkhd->bhqk', q, k) / jnp.sqrt(jnp.float32(HEAD_DIM))
        attn = jax.nn.softmax(scores, axis=-1)
        out = jnp.einsum('bhqk,bkhd->bqhd', attn, v).reshape(B, S, NUM_HEADS * HEAD_DIM)
        return _mxfp4_matmul(out, wo_codes, wo_scales) + bo

    def _L0_attn_b_ref(hidden_states, Wq, bq, Wk, bk, Wv, bv, Wo, bo, rand_matrix):
        import math
        import jax, jax.numpy as jnp
        import numpy as np
        HID = 256
        H = 16
        HKV = 8
        D = HID // H
        F = D
        SEQ = 256
        BATCH = 2
        THETA = 10000.0

        def _rotate_half(x):
            x1, x2 = (x[..., :x.shape[-1] // 2], x[..., x.shape[-1] // 2:])
            return jnp.concatenate((-x2, x1), axis=-1)

        def _softmax_kernel(x, R):
            n = jnp.sqrt(jnp.sum(x * x, axis=-1, keepdims=True))
            x = x / jnp.maximum(n, 1e-06)
            p = jnp.einsum('...d,ed->...e', x, R)
            feats = jnp.concatenate([jnp.sin(p), jnp.cos(p)], axis=-1)
            return feats / math.sqrt(F)
        b, s, _ = hidden_states.shape
        q = (hidden_states @ Wq.T + bq).reshape(b, s, H, D).transpose(0, 2, 1, 3)
        k = (hidden_states @ Wk.T + bk).reshape(b, s, HKV, D).transpose(0, 2, 1, 3)
        v = (hidden_states @ Wv.T + bv).reshape(b, s, HKV, D).transpose(0, 2, 1, 3)
        inv_freq = 1.0 / THETA ** (jnp.arange(0, D, 2, dtype=jnp.float32) / D)
        freqs = jnp.arange(s, dtype=jnp.float32)[:, None] * inv_freq[None, :]
        emb = jnp.concatenate((freqs, freqs), axis=-1)
        cos = jnp.cos(emb)[None, None, :, :]
        sin = jnp.sin(emb)[None, None, :, :]
        q = q * cos + _rotate_half(q) * sin
        k = k * cos + _rotate_half(k) * sin
        rep = H // HKV
        k = jnp.repeat(k, rep, axis=1)
        v = jnp.repeat(v, rep, axis=1)
        qp = _softmax_kernel(q, rand_matrix)
        kp = _softmax_kernel(k, rand_matrix)
        kv = jnp.einsum('bhsf,bhsd->bsfd', kp, v)
        out = jnp.einsum('bhsf,bsfd->bhsd', qp, kv)
        out = out.reshape(b, s, HID)
        return out @ Wo.T + bo

    def _L0_ffn_ref(hidden_states, gate_weight, gate_up_proj, down_proj, similarity):
        import jax, jax.numpy as jnp
        import numpy as np
        NUM_EXPERTS = 32
        TOP_K = 8
        SELECT_TOP_K = 4
        THRESHOLD = 0.5
        HIDDEN = 256
        D_FF = 96

        def _moe_forward(hidden_states, gate_weight, gate_up_proj, down_proj, similarity):
            B, S_len, H = hidden_states.shape
            E, K, Ssel = (NUM_EXPERTS, TOP_K, SELECT_TOP_K)
            x = hidden_states.reshape(-1, H)
            router_logits = x @ gate_weight.T
            router_probs = jax.nn.softmax(router_logits.astype(jnp.float32), axis=-1).astype(router_logits.dtype)
            router_top_value, router_indices = jax.lax.top_k(router_probs, K)
            routing_weights = router_top_value / jnp.clip(jnp.sum(router_top_value, axis=-1, keepdims=True), 1e-12, None)
            sim = similarity.astype(jnp.float32)
            sim = sim.at[jnp.arange(E), jnp.arange(E)].set(1.0)
            prim = router_indices[:, :Ssel]
            sec = router_indices[:, Ssel:]
            sim_cand = sim[sec[:, :, None], prim[:, None, :]]
            best_sim = jnp.max(sim_cand, axis=-1)
            best_i = jnp.argmax(sim_cand, axis=-1)
            prim_rep = jnp.broadcast_to(prim[:, None, :], sim_cand.shape)
            best_primary = jnp.take_along_axis(prim_rep, best_i[..., None], axis=-1)[..., 0]
            new_sec = jnp.where(best_sim < THRESHOLD, sec, best_primary) if THRESHOLD > 0.0 else best_primary
            rerouted_indices = jnp.concatenate([prim, new_sec], axis=1)
            combine = jnp.sum(jax.nn.one_hot(rerouted_indices, E, dtype=routing_weights.dtype) * routing_weights[..., None], axis=1)

            def expert_step(y, params):
                wgu, wd, cw = params
                gu = x @ wgu.T
                g, u = jnp.split(gu, 2, axis=-1)
                h = jax.nn.silu(g) * u
                y = y + h @ wd.T * cw[:, None]
                return (y, None)
            y0 = jnp.zeros_like(x)
            y, _ = jax.lax.scan(expert_step, y0, (gate_up_proj, down_proj, combine.T))
            return y.reshape(B, S_len, H)
        return _moe_forward(hidden_states, gate_weight, gate_up_proj, down_proj, similarity)
    x = L0_attn_a_x
    x = x + _L0_attn_a_ref(_layernorm(x, axis=-1), L0_attn_a_wq_codes, L0_attn_a_wq_scales, L0_attn_a_bq, L0_attn_a_wk_codes, L0_attn_a_wk_scales, L0_attn_a_bk, L0_attn_a_wv_codes, L0_attn_a_wv_scales, L0_attn_a_bv, L0_attn_a_wo_codes, L0_attn_a_wo_scales, L0_attn_a_bo)
    x = x + _L0_ffn_ref(_layernorm(x, axis=-1), L0_ffn_gate_weight, L0_ffn_gate_up_proj, L0_ffn_down_proj, L0_ffn_similarity)
    x = x + _L0_attn_b_ref(_layernorm(x, axis=-1), L0_attn_b_Wq, L0_attn_b_bq, L0_attn_b_Wk, L0_attn_b_bk, L0_attn_b_Wv, L0_attn_b_bv, L0_attn_b_Wo, L0_attn_b_bo, L0_attn_b_rand_matrix)
    x = x + _L0_ffn_ref(_layernorm(x, axis=-1), L0_ffn_gate_weight, L0_ffn_gate_up_proj, L0_ffn_down_proj, L0_ffn_similarity)
    return x

_drawn_inputs = setup_inputs


def setup_inputs(seed=0):
    import zlib

    import numpy as np

    out = dict(_drawn_inputs(seed))
    spreads = {'L0_attn_a_bq': (0.0, 0.8),
     'L0_attn_a_bk': (0.0, 2.0),
     'L0_attn_a_bv': (0.0, 0.1),
     'L0_attn_a_bo': (0.0, 0.1)}
    factors = {'L0_attn_a_wq_scales': 5.069,
     'L0_attn_a_wk_scales': 5.078,
     'L0_attn_a_wv_scales': 4.934,
     'L0_attn_b_bq': 22.889,
     'L0_attn_b_bk': 22.894,
     'L0_attn_b_bv': 8.0,
     'L0_attn_b_bo': 2.993,
     'L0_ffn_gate_weight': 5.72,
     'L0_ffn_gate_up_proj': 5.333,
     'L0_ffn_down_proj': 5.303,
     'L0_ffn_similarity': 8.0}
    for name, (base, spread) in spreads.items():
        noise = np.random.default_rng([zlib.crc32(name.encode()), seed]).standard_normal(out[name].shape)
        drawn = base * np.exp(spread * noise) if base else spread * noise
        out[name] = jnp.asarray(drawn.astype(out[name].dtype))
    for name, factor in factors.items():
        out[name] = (out[name] * factor).astype(out[name].dtype)
    return out
```

```python
import math
from contextlib import ExitStack

import numpy as np

import concourse.bass as bass
from concourse import mybir

FP32 = mybir.dt.float32
F32R = mybir.dt.float32r
FP16 = mybir.dt.float16
BF16 = mybir.dt.bfloat16
U32 = mybir.dt.uint32
ALU = mybir.AluOpType
ACT = mybir.ActivationFunctionType
AX = mybir.AxisListType

P = 128
TOK = 2048
DM = 256
NT = TOK // P
NB = 4
TB = TOK // NB
TPB = NT // NB
KC = DM // P
NH = 16
HD = 128
EPS = 1e-5


def fp(ap):
    return ap.bitcast(FP32)


def block_of(b):
    return bass.ds(b * TB, TB)


class Shared:

    def __init__(self, nc, ctx):
        self.made = {}
        self.new_sem = lambda name: ctx.enter_context(nc.semaphore(name))
        sb = lambda name, shape, dt: ctx.enter_context(nc.sbuf_tensor(name, shape, dt))
        self.x = sb("residual", [P, NT, DM], FP32)
        self.xh = sb("normed_hi", [P, KC, TOK], F32R)
        self.xl = sb("normed_lo", [P, KC, TOK], F32R)
        self.ident = sb("identity_sb", [P, P], FP32)


    def sem(self, name):
        if name not in self.made:
            self.made[name] = self.new_sem(name)
        return self.made[name]


def clear_stage(nc, S, prefixes):
    block_ctx = ExitStack()
    with block_ctx:
        block = block_ctx.enter_context(nc.Block())

        @block.gpsimd
        def _(pool):
            for name, sem in S.made.items():
                if name.split("_")[0] in prefixes:
                    pool.sem_clear(sem)


def load_stage(nc, S, x_in, ident_in):
    with ExitStack() as ctx:
        loaded = S.sem("x_loaded")
        ident_loaded = S.sem("ident_loaded")
        block = ctx.enter_context(nc.Block())

        @block.sync
        def _(sp):
            sp.dma_start(S.x[:, :, :], x_in.rearrange("(t p) d -> p t d", p=P)).then_inc(loaded, 16)
            sp.dma_start(S.ident[:, :], ident_in).then_inc(ident_loaded, 16)
            sp.wait_ge(loaded, 16)
            sp.wait_ge(ident_loaded, 16)


def norm_stage(nc, S, name, places=None):
    places = places or name
    with ExitStack() as ctx:
        sb = lambda n, shape, dt: ctx.enter_context(nc.sbuf_tensor(f"{places}_{n}", shape, dt))
        sem = lambda n: S.sem(f"{name}_{n}")
        stats = sb("stats", [P, NT, 6], FP32)
        mv = sb("mean_var", [P, NT, 2], FP32)
        ve = sb("var_eps", [P, NT], FP32)
        sd = sb("sd", [P, NT], FP32)
        r = sb("rsd", [P, NT], FP32)
        r2 = sb("rsd_square", [P, NT], FP32)
        fix = sb("newton", [P, NT], FP32)
        xn = sb("normed", [P, NT, DM], FP32)
        turned = [ctx.enter_context(nc.psum_tensor(f"{places}_turned{i}", [P, TB], FP32)) for i in range(4)]
        stats_done, var_ready, sd_ready = sem("stats_done"), sem("var_ready"), sem("sd_ready")
        small, normed = sem("small"), sem("normed")
        turned_ready, hi_ready, lo_ready = sem("turned_ready"), sem("hi_ready"), sem("lo_ready")
        block = ctx.enter_context(nc.Block())

        @block.vector
        def _(dve):
            for t in range(NT):
                dve.bn_stats(stats[:, t, :], S.x[:, t, :]).then_inc(stats_done, 1)
            for t in range(NT):
                dve.wait_ge(stats_done, t + 1)
                dve.bn_aggr(mv[:, t, :], stats[:, t, :]).then_inc(small, 1)
            dve.wait_ge(small, NT)
            dve.tensor_scalar(ve[:, :], mv[:, :, 1], EPS, None, ALU.add).then_inc(var_ready, 1)
            dve.wait_ge(sd_ready, 1)
            dve.reciprocal(r[:, :], sd[:, :]).then_inc(small, 1)
            dve.wait_ge(small, NT + 1)
            dve.tensor_tensor(r2[:, :], r[:, :], r[:, :], ALU.mult).then_inc(small, 1)
            dve.wait_ge(small, NT + 2)
            dve.tensor_tensor(r2[:, :], r2[:, :], ve[:, :], ALU.mult).then_inc(small, 1)
            dve.wait_ge(small, NT + 3)
            dve.tensor_scalar(fix[:, :], r2[:, :], -0.5, 1.5, ALU.mult, ALU.add).then_inc(small, 1)
            dve.wait_ge(small, NT + 4)
            dve.tensor_tensor(r[:, :], r[:, :], fix[:, :], ALU.mult).then_inc(small, 1)
            dve.wait_ge(small, NT + 5)

            def lows(n):
                b, c = n // KC, n % KC
                dve.wait_ge(hi_ready, n + 1)
                dve.tensor_tensor(S.xl[:, c, block_of(b)], turned[n % 4][:, :],
                                  fp(S.xh[:, c, block_of(b)]), ALU.subtract).then_inc(lo_ready, 1)

            for t in range(NT):
                dve.tensor_scalar(xn[:, t, :], S.x[:, t, :], mv[:, t, 0:1], r[:, t:t + 1],
                                  ALU.subtract, ALU.mult).then_inc(normed, 1)
                if t % TPB == TPB - 1 and t >= 2 * TPB - 1:
                    lows(KC * (t // TPB) - 2)
                    lows(KC * (t // TPB) - 1)
            lows(KC * NB - 2)
            lows(KC * NB - 1)

        @block.tensor
        def _(pe):
            for b in range(NB):
                pe.wait_ge(normed, TPB * (b + 1))
                for c in range(KC):
                    n = b * KC + c
                    if n >= 4:
                        pe.wait_ge(lo_ready, n - 3)
                    for i in range(TPB):
                        mm = pe.transpose(turned[n % 4][:, i * P:(i + 1) * P],
                                          xn[:, b * TPB + i, c * P:(c + 1) * P], S.ident[:, :])
                    mm.then_inc(turned_ready, 1)

        @block.scalar
        def _(act):
            act.wait_ge(var_ready, 1)
            act.activation(sd[:, :], ve[:, :], ACT.Sqrt).then_inc(sd_ready, 1)
            for n in range(KC * NB):
                b, c = n // KC, n % KC
                act.wait_ge(turned_ready, n + 1)
                act.activation(S.xh[:, c, block_of(b)], turned[n % 4][:, :], ACT.Copy).then_inc(hi_ready, 1)


def attention_stage(nc, S, wqkv_codes, wqkv_scales, wo_codes, wo_scales, bo):
    SCALE = 1.0 / math.sqrt(HD)
    KT = TOK // P
    GK = 4
    NG = KT // GK
    PV_CUT = [0, 5, 11, 16]
    with ExitStack() as ctx:
        sb = lambda n, shape, dt: ctx.enter_context(nc.sbuf_tensor(f"a_{n}", shape, dt))
        sem = lambda n: S.sem(f"a_{n}")
        Kh = [sb(f"keys_hi{i}", [P, TOK], FP16) for i in range(2)]
        Kl = [sb(f"keys_lo{i}", [P, TOK], FP16) for i in range(2)]
        Vh = [sb(f"values_hi{i}", [P, KT, HD], FP16) for i in range(2)]
        Vl = [sb(f"values_lo{i}", [P, KT, HD], FP16) for i in range(2)]
        Qh = [sb(f"queries_hi{i}", [P, TB], FP16) for i in range(2)]
        Ql = [sb(f"queries_lo{i}", [P, TB], FP16) for i in range(2)]
        vft = sb("values_by_feature", [P, TB], FP32)
        E = sb("exponentials", [P, TOK], FP32)
        Th = [sb(f"turned_hi{i}", [P, KT, TB], FP16) for i in range(2)]
        Tl = [sb(f"turned_lo{i}", [P, KT, TB], FP16) for i in range(2)]
        Oh = sb("out_hi", [P, TB], F32R)
        Ol = sb("out_lo", [P, TB], F32R)
        Wh = [sb(f"wqkv_hi{i}", [P, 3, KC, HD], F32R) for i in range(2)]
        Wl = [sb(f"wqkv_lo{i}", [P, 3, KC, HD], F32R) for i in range(2)]
        WOh = [sb(f"wo_hi{i}", [P, DM], F32R) for i in range(2)]
        WOl = [sb(f"wo_lo{i}", [P, DM], F32R) for i in range(2)]
        bias = [sb(f"bias{i}", [P, 3], FP32) for i in range(2)]
        NW = 3 * KC * HD
        codes = sb("codes", [P, NW + 3], FP32)
        scales = sb("scales", [P, NW], FP32)
        ocodes = sb("out_codes", [P, DM], FP32)
        oscales = sb("out_scales", [P, DM], FP32)
        bo_sb = sb("bo", [P, DM], FP32)
        halfmax = sb("halfmax", [P, TPB, 2], FP32)
        negmax = sb("negmax", [P, TPB], FP32)
        rowsum = [sb(f"rowsum{i}", [P, TPB], FP32) for i in range(2)]
        rinv = sb("rowsum_inverse", [P, TPB], FP32)

        scores = ctx.enter_context(nc.psum_tensor("a_scores", [P, TOK], FP32))
        turned = [ctx.enter_context(nc.psum_tensor(f"a_turned{i}", [P, GK, P], FP32)) for i in range(2)]
        obank = ctx.enter_context(nc.psum_tensor("a_out", [P, TB], FP32))
        mbank = ctx.enter_context(nc.psum_tensor("a_proj", [P, TB], FP32))

        scores_half, exps_turned, pv_done = sem("scores_half"), sem("exps_turned"), sem("pv_done")
        v_made, v_turned, q_made, k_made = sem("v_made"), sem("v_turned"), sem("q_made"), sem("k_made")
        ya_made, yb_made = sem("ya_made"), sem("yb_made")
        exps_ready, turned_hi, v_stored = sem("exps_ready"), sem("turned_hi"), sem("v_stored")
        v_hi, q_hi, k_hi, o_hi = sem("v_hi"), sem("q_hi"), sem("k_hi"), sem("o_hi")
        half_ready, negmax_ready, turned_lo = sem("half_ready"), sem("negmax_ready"), sem("turned_lo")
        v_lo, q_lo, k_lo, o_lo = sem("v_lo"), sem("q_lo"), sem("k_lo"), sem("o_lo")
        ya_added, yb_added, rinv_ready = sem("ya_added"), sem("yb_added"), sem("rinv_ready")
        w_raw, wo_raw, bo_raw = sem("w_raw"), sem("wo_raw"), sem("bo_raw")
        wqkv_step, wo_step = sem("wqkv_step"), sem("wo_step")
        w_split, wo_split = sem("w_split"), sem("wo_split")
        block = ctx.enter_context(nc.Block())
        Q, K, V = range(3)
        SPP = 2 * NB
        GS = TPB * NG
        CREDIT = 2

        def at(m):
            m %= SPP
            return m // NB, m % NB, m % 2

        @block.sync
        def _(sp):
            sp.dma_start(bo_sb[:, :], bo).then_inc(bo_raw, 16)

            def load_qkv(h):
                sp.dma_start(codes[:, :], wqkv_codes[bass.ds(h, 1), :, :].rearrange("h p n -> (h p) n")).then_inc(w_raw, 16)
                sp.dma_start(scales[:, :], wqkv_scales[bass.ds(h, 1), :, :].rearrange("h p n -> (h p) n")).then_inc(w_raw, 16)

            def load_o(h):
                sp.dma_start(ocodes[:, :], wo_codes[bass.ds(h, 1), :, :].rearrange("h p n -> (h p) n")).then_inc(wo_raw, 16)
                sp.dma_start(oscales[:, :], wo_scales[bass.ds(h, 1), :, :].rearrange("h p n -> (h p) n")).then_inc(wo_raw, 16)

            load_qkv(0)
            load_o(0)
            sp.wait_ge(w_split, 1)
            load_qkv(1)
            with sp.Fori(0, NH) as h:
                sp.wait_ge(wo_split, h + 1)
                load_o(h + 1)
                sp.wait_ge(w_split, h + 2)
                load_qkv(h + 2)

        @block.gpsimd
        def _(pool):
            flat = lambda w: w[:, :, :, :].rearrange("p m c f -> p (m c f)")

            def split_qkv(h, i):
                pool.wait_ge(w_raw, h * 32 + 32)
                pool.tensor_tensor(flat(Wh[i]), codes[:, 0:NW], scales[:, :], ALU.mult)
                pool.tensor_tensor(codes[:, 0:NW], codes[:, 0:NW], scales[:, :], ALU.mult).then_inc(wqkv_step, 1)
                pool.tensor_copy(bias[i][:, :], codes[:, NW:NW + 3])
                pool.wait_ge(wqkv_step, h + 1)
                pool.tensor_tensor(flat(Wl[i]), codes[:, 0:NW], fp(flat(Wh[i])), ALU.subtract).then_inc(w_split, 1)

            def split_o(h, i):
                pool.wait_ge(wo_raw, h * 32 + 32)
                pool.tensor_tensor(WOh[i][:, :], ocodes[:, :], oscales[:, :], ALU.mult)
                pool.tensor_tensor(ocodes[:, :], ocodes[:, :], oscales[:, :], ALU.mult).then_inc(wo_step, 1)
                pool.wait_ge(wo_step, h + 1)
                pool.tensor_tensor(WOl[i][:, :], ocodes[:, :], fp(WOh[i][:, :]), ALU.subtract).then_inc(wo_split, 1)

            split_qkv(0, 0)
            split_o(0, 0)
            split_qkv(1, 1)
            with pool.Fori(0, NH // 2) as pair:
                for hh in range(2):
                    h = pair * 2 + hh
                    pool.wait_ge(yb_added, pair * SPP + (hh * NB + 2))
                    split_o(h + 1, 1 - hh)
                    pool.wait_ge(q_lo, pair * SPP + (hh * NB + 4))
                    split_qkv(h + 2, hh)

        @block.tensor
        def _(pe):
            def project(what, i, b, made):
                for c in range(KC):
                    for k, (w, x) in enumerate(((Wh, S.xh), (Wh, S.xl), (Wl, S.xh))):
                        mm = pe.matmul(mbank[:, :], w[i][:, what, c, :], x[:, c, block_of(b)],
                                       start=(c == 0 and k == 0), stop=(c == KC - 1 and k == 2))
                mm.then_inc(made, 1)

            def turn_values():
                for i in range(TPB):
                    mm = pe.transpose(mbank[:, i * P:(i + 1) * P], vft[:, i * P:(i + 1) * P], S.ident[:, :])
                mm.then_inc(v_turned, 1)

            def score(t, hh, qq):
                for half in range(2):
                    for c in range(2 * half, 2 * half + 2):
                        for q, k in ((Qh, Kh), (Qh, Kl), (Ql, Kh)):
                            mm = pe.matmul(scores[:, block_of(c)], q[qq][:, t * P:(t + 1) * P],
                                           k[hh][:, block_of(c)], start=(q is Qh and k is Kh), stop=(q is Ql))
                    mm.then_inc(scores_half, 1)

            def values(t, hv, qv):
                for kt in range(PV_CUT[t], PV_CUT[t + 1]):
                    for v, e in ((Vh, Th), (Vh, Tl), (Vl, Th)):
                        mm = pe.matmul(obank[:, :], v[hv][:, kt, :], e[qv][:, kt, :],
                                       start=(kt == 0 and v is Vh and e is Th), stop=(kt == KT - 1 and v is Vl))
                if t == 2:
                    mm.then_inc(pv_done, 1)

            def turn(n, t):
                pe.wait_ge(exps_ready, n * TPB + (t + 1))
                for g in range(NG):
                    pe.wait_ge(turned_lo, n * GS + (t * NG + g - 1 + CREDIT))
                    for i in range(GK):
                        kt = g * GK + i
                        mm = pe.transpose(turned[g % 2][:, i, :], E[:, kt * P:(kt + 1) * P], S.ident[:, :])
                    mm.then_inc(exps_turned, 1)

            def outputs(bank, a, ho, made):
                for i in range(2):
                    cols = slice((a + i) * P, (a + i + 1) * P)
                    for k, (o, w) in enumerate(((Oh, WOh), (Oh, WOl), (Ol, WOh))):
                        mm = pe.matmul(bank[:, i * DM:(i + 1) * DM], o[:, cols], w[ho][:, :],
                                       start=(k == 0), stop=(k == 2))
                mm.then_inc(made, 1)

            pe.wait_ge(w_split, 1)
            for b in range(NB):
                if b:
                    pe.wait_ge(k_lo, b)
                project(V, 0, b, v_made)
                pe.wait_ge(v_stored, b + 1)
                turn_values()
                pe.wait_ge(v_lo, b + 1)
                project(K, 0, b, k_made)
            pe.wait_ge(k_lo, NB)
            project(Q, 0, 0, q_made)

            def step(n, pair, m):
                hh, b, qq = at(m)
                h1, _, q1 = at(m - 1)
                if b == 0:
                    pe.wait_ge(w_split, pair * 2 + (hh + 2))
                if b == 1:
                    pe.wait_ge(wo_split, pair * 2 + (hh + 1))
                pe.wait_ge(q_lo, n + 1)
                pe.wait_ge(k_lo, n + NB)
                for t in range(TPB):
                    score(t, hh, qq)
                    if t == 0:
                        pe.wait_ge(yb_added, n + 1)
                        project(V, 1 - hh, b, v_made)
                        pe.wait_ge(ya_added, n + 1)
                        pe.wait_ge(turned_lo, n * GS + CREDIT)
                    if t == 1:
                        pe.wait_ge(v_stored, n + NB + 1)
                        turn_values()
                    if t == 2:
                        pe.wait_ge(v_lo, n + NB + 1)
                        h2, b2, _ = at(m + 1)
                        project(Q, h2, b2, q_made)
                    if t < 3:
                        values(t, h1, q1)
                    else:
                        pe.wait_ge(q_lo, n + 2)
                        project(K, 1 - hh, b, k_made)
                        pe.wait_ge(o_lo, n + 1)
                        outputs(obank, 0, h1, ya_made)
                        pe.wait_ge(k_lo, n + NB + 1)
                        outputs(mbank, 2, h1, yb_made)
                    turn(n, t)

            with pe.Fori(0, NH // 2) as pair:
                for m in range(SPP):
                    step(pair * SPP + m, pair, m)

            N = NH * NB
            hh, _, qq = at(SPP - 1)
            pe.wait_ge(ya_added, N + 1)
            pe.wait_ge(turned_lo, N * GS + CREDIT)
            for t in range(3):
                values(t, hh, qq)
            pe.wait_ge(o_lo, N + 1)
            outputs(obank, 0, hh, ya_made)
            pe.wait_ge(yb_added, N + 1)
            outputs(mbank, 2, hh, yb_made)

        @block.scalar
        def _(act):
            def store_values(i, count):
                act.wait_ge(v_made, count)
                act.activation(vft[:, :], mbank[:, :], ACT.Identity, bias=bias[i][:, V:V + 1]).then_inc(v_stored, 1)

            def values_hi(i, b, count):
                act.wait_ge(v_turned, count)
                act.activation(Vh[i][:, b * TPB:(b + 1) * TPB, :].rearrange("p t d -> p (t d)"), mbank[:, :],
                               ACT.Copy).then_inc(v_hi, 1)

            def keys_hi(i, b, count):
                act.wait_ge(k_made, count)
                act.activation(Kh[i][:, block_of(b)], mbank[:, :], ACT.Identity, bias=bias[i][:, K:K + 1]).then_inc(k_hi, 1)

            def queries_hi(i, q, count):
                act.wait_ge(q_made, count)
                act.activation(Qh[q][:, :], mbank[:, :], ACT.Identity, bias=bias[i][:, Q:Q + 1]).then_inc(q_hi, 1)

            def out_hi(count):
                act.wait_ge(pv_done, count)
                act.activation(Oh[:, :], obank[:, :], ACT.Copy).then_inc(o_hi, 1)

            for b in range(NB):
                store_values(0, b + 1)
                values_hi(0, b, b + 1)
                keys_hi(0, b, b + 1)
            queries_hi(0, 0, 1)

            def step(n, pair, m):
                hh, b, qq = at(m)
                h2, _, q2 = at(m + 1)
                for t in range(TPB):
                    if t == 0:
                        store_values(1 - hh, n + NB + 1)
                    if t == 1:
                        values_hi(1 - hh, b, n + NB + 1)
                    if t == 2:
                        queries_hi(h2, q2, n + 2)
                    if t == 3:
                        keys_hi(1 - hh, b, n + NB + 1)
                    act.wait_ge(negmax_ready, n * TPB + (t + 1))
                    act.activation(E[:, :], scores[:, :], ACT.Exp, bias=negmax[:, t:t + 1], scale=SCALE,
                                   accum_out=rowsum[qq][:, t:t + 1]).then_inc(exps_ready, 1)
                    if t == 2:
                        out_hi(n + 1)
                    for g in range(NG):
                        act.wait_ge(exps_turned, n * GS + (t * NG + g + 1))
                        act.activation(Th[qq][:, g * GK:(g + 1) * GK, t * P:(t + 1) * P], turned[g % 2][:, :, :],
                                       ACT.Copy).then_inc(turned_hi, 1)

            with act.Fori(0, NH // 2) as pair:
                for m in range(SPP):
                    step(pair * SPP + m, pair, m)
            out_hi(NH * NB + 1)

        @block.vector
        def _(dve):
            def values_lo(i, b, count):
                tiles = lambda v: v[i][:, b * TPB:(b + 1) * TPB, :].rearrange("p t d -> p (t d)")
                dve.wait_ge(v_hi, count)
                dve.tensor_tensor(tiles(Vl), mbank[:, :], tiles(Vh), ALU.subtract).then_inc(v_lo, 1)

            def keys_lo(i, b, count):
                dve.wait_ge(k_hi, count)
                dve.scalar_tensor_tensor(out=Kl[i][:, block_of(b)], in0=mbank[:, :], scalar=bias[i][:, K:K + 1],
                                         in1=Kh[i][:, block_of(b)], op0=ALU.add, op1=ALU.subtract).then_inc(k_lo, 1)

            def queries_lo(i, q, count):
                dve.wait_ge(q_hi, count)
                dve.scalar_tensor_tensor(out=Ql[q][:, :], in0=mbank[:, :], scalar=bias[i][:, Q:Q + 1],
                                         in1=Qh[q][:, :], op0=ALU.add, op1=ALU.subtract).then_inc(q_lo, 1)

            def out_lo(count):
                dve.wait_ge(o_hi, count)
                dve.tensor_tensor(Ol[:, :], obank[:, :], fp(Oh[:, :]), ALU.subtract).then_inc(o_lo, 1)

            def invert_sums(q, count):
                dve.reciprocal(rinv[:, :], rowsum[q][:, :]).then_inc(rinv_ready, 1)
                dve.wait_ge(rinv_ready, count)

            def add(bank, b, a):
                for i in range(2):
                    t = b * TPB + a + i
                    ins = dve.scalar_tensor_tensor(out=S.x[:, t, :], in0=bank[:, i * DM:(i + 1) * DM],
                                                   scalar=rinv[:, a + i:a + i + 1], in1=S.x[:, t, :],
                                                   op0=ALU.mult, op1=ALU.add)
                return ins

            for z in (Th[1], Tl[1], Vh[1], Vl[1]):
                dve.memset(z[:, :, :].bitcast(FP32), 0.0)
            dve.memset(rowsum[1][:, :], 1.0)
            for z in (WOh[1], WOl[1]):
                ins = dve.memset(fp(z[:, :]), 0.0)
            ins.then_inc(turned_lo, CREDIT)
            dve.wait_ge(bo_raw, 16)
            for t in range(NT):
                ins = dve.tensor_tensor(S.x[:, t, :], S.x[:, t, :], bo_sb[:, :], ALU.add)
            ins.then_inc(ya_added, 1)
            dve.wait_ge(ya_added, 1)
            dve.sem_inc(yb_added, 1)

            for b in range(NB):
                values_lo(0, b, b + 1)
                keys_lo(0, b, b + 1)
            queries_lo(0, 0, 1)

            def step(n, pair, m):
                hh, b, qq = at(m)
                h2, _, q2 = at(m + 1)
                _, b1, q1 = at(m - 1)
                for t in range(TPB):
                    for half in range(2):
                        dve.wait_ge(scores_half, n * (2 * TPB) + (2 * t + half + 1))
                        dve.tensor_reduce(halfmax[:, t, half:half + 1], scores[:, half * 2 * TB:(half + 1) * 2 * TB],
                                          AX.X, ALU.max).then_inc(half_ready, 1)
                    dve.wait_ge(half_ready, n * (2 * TPB) + (2 * t + 2))
                    dve.tensor_scalar(negmax[:, t:t + 1], halfmax[:, t, 0:1], halfmax[:, t, 1:2], -SCALE,
                                      ALU.max, ALU.mult).then_inc(negmax_ready, 1)
                    if t == 1:
                        values_lo(1 - hh, b, n + NB + 1)
                    if t == 2:
                        queries_lo(h2, q2, n + 2)
                        out_lo(n + 1)
                    if t == 3:
                        keys_lo(1 - hh, b, n + NB + 1)
                        invert_sums(q1, n + 1)
                        dve.wait_ge(ya_made, n + 1)
                        add(obank, b1, 0).then_inc(ya_added, 1)
                        dve.wait_ge(yb_made, n + 1)
                        add(mbank, b1, 2).then_inc(yb_added, 1)
                    for g in range(NG):
                        dve.wait_ge(turned_hi, n * GS + (t * NG + g + 1))
                        dve.tensor_tensor(Tl[qq][:, g * GK:(g + 1) * GK, t * P:(t + 1) * P], turned[g % 2][:, :, :],
                                          Th[qq][:, g * GK:(g + 1) * GK, t * P:(t + 1) * P],
                                          ALU.subtract).then_inc(turned_lo, 1)

            with dve.Fori(0, NH // 2) as pair:
                for m in range(SPP):
                    step(pair * SPP + m, pair, m)

            N = NH * NB
            out_lo(N + 1)
            invert_sums(at(SPP - 1)[2], N + 1)
            dve.wait_ge(ya_made, N + 1)
            add(obank, NB - 1, 0).then_inc(ya_added, 1)
            dve.wait_ge(yb_made, N + 1)
            add(mbank, NB - 1, 2).then_inc(yb_added, 1)


NE = 32
TOPK = 8
PRIM = 4
SEC = TOPK - PRIM
THRESHOLD = 0.5
FF = 96
NF = NE * FF
JT = NF // P
NC = 3


def route_stage(nc, S, name, places, gate_w, sim_in, notdiag_in, iota_in, combine):
    with ExitStack() as ctx:
        sb = lambda n, shape, dt: ctx.enter_context(nc.sbuf_tensor(f"{places}_{n}", shape, dt))
        sem = lambda n: S.sem(f"{name}_{n}")
        gate = sb("gate", [P, KC, NE], FP32)
        gh, gl = sb("gate_hi", [P, KC, NE], F32R), sb("gate_lo", [P, KC, NE], F32R)
        sim = sb("similarity", [P, P], FP32)
        notdiag = sb("notdiag", [P, P], FP32)
        iota = sb("iota", [P, NE], FP32)
        expo = sb("expo", [P, NT, NE], FP32)
        shifted = sb("shifted", [P, NT, NE], FP32)
        top_logit = sb("top_logit", [P, NT], FP32)
        total = sb("total", [P, NT], FP32)
        top = sb("top", [P, NT, TOPK], FP32)
        index = sb("index", [P, NT, TOPK], U32)
        indexf = sb("indexf", [P, NT, TOPK], FP32)
        topsum = sb("topsum", [P, NT], FP32)
        hot = sb("onehot", [P, NT, TOPK, NE], FP32)
        hotT = sb("onehot_turned", [P, TOK], FP32)
        product = sb("product", [P, NT, TOPK, NE], FP32)
        cand = sb("candidates", [P, NT, SEC, PRIM], FP32)
        best = sb("best", [P, NT, SEC], FP32)
        isbest = sb("isbest", [P, NT, SEC, PRIM], FP32)
        seen = sb("seen", [P, NT, SEC], FP32)
        reroute = sb("reroute", [P, NT, SEC], FP32)
        moved = sb("moved", [P, NT, SEC], FP32)
        gained = sb("gained", [P, NT, PRIM], FP32)
        coef = sb("coef", [P, NT, TOPK], FP32)
        comb = sb("comb", [P, NT, NE], FP32)
        parts = sb("comb_parts", [P, NT, NC, NE], BF16)
        identb = sb("identity_bf16", [P, P], BF16)
        logits = ctx.enter_context(nc.psum_tensor(f"{places}_logits", [P, NT, NE], FP32))
        hot_ps = ctx.enter_context(nc.psum_tensor(f"{places}_hot_ps", [P, TB], FP32))
        rows = ctx.enter_context(nc.psum_tensor(f"{places}_sim_rows", [P, NT, SEC, NE], FP32))
        comb_ps = ctx.enter_context(nc.psum_tensor(f"{places}_comb_ps", [P, TOK], BF16))
        loaded = sem("loaded")
        step = sem("dve_step")
        gate_ready, logits_ready, shifted_ready, expo_ready = sem("gate_ready"), sem("logits_ready"), sem("shifted_ready"), sem("expo_ready")
        hot_ready, hot_turned, hot_stored, rows_ready = sem("hot_ready"), sem("hot_turned"), sem("hot_stored"), sem("rows_ready")
        parts_ready, comb_turned, comb_stored = sem("parts_ready"), sem("comb_turned"), sem("comb_stored")
        block = ctx.enter_context(nc.Block())

        @block.sync
        def _(sp):
            sp.dma_start(gate[:, :, :], gate_w).then_inc(loaded, 16)
            sp.dma_start(sim[:, :], sim_in).then_inc(loaded, 16)
            sp.dma_start(notdiag[:, :], notdiag_in).then_inc(loaded, 16)
            sp.dma_start(iota[:, :], iota_in).then_inc(loaded, 16)

        @block.tensor
        def _(pe):
            pe.wait_ge(gate_ready, 1)
            for t in range(NT):
                for c in range(KC):
                    for k, (x, g) in enumerate(((S.xh, gh), (S.xh, gl), (S.xl, gh))):
                        mm = pe.matmul(logits[:, t, :], x[:, c, t * P:(t + 1) * P], g[:, c, :],
                                       start=(c == 0 and k == 0), stop=(c == KC - 1 and k == 2))
            mm.then_inc(logits_ready, 1)
            pe.wait_ge(hot_ready, 1)
            for b in range(NB):
                if b:
                    pe.wait_ge(hot_stored, b)
                for i in range(TPB):
                    mm = pe.transpose(hot_ps[:, i * P:(i + 1) * P],
                                      hot[:, b * TPB + i, PRIM:TOPK, :].rearrange("p s e -> p (s e)"), S.ident[:, :])
                mm.then_inc(hot_turned, 1)
            pe.wait_ge(hot_stored, NB)
            for t in range(NT):
                mm = pe.matmul(rows[:, t, :, :].rearrange("p s e -> p (s e)"), hotT[:, t * P:(t + 1) * P], sim[:, :],
                               start=True, stop=True)
            mm.then_inc(rows_ready, 1)
            pe.wait_ge(parts_ready, 1)
            for t in range(NT):
                mm = pe.transpose(comb_ps[0:NC * NE, t * P:(t + 1) * P],
                                  parts[:, t, :, :].rearrange("p c e -> p (c e)"), identb[:, :])
            mm.then_inc(comb_turned, 1)

        @block.scalar
        def _(act):
            act.wait_ge(shifted_ready, 1)
            act.activation(expo[:, :, :], shifted[:, :, :], ACT.Exp).then_inc(expo_ready, 1)
            for b in range(NB):
                act.wait_ge(hot_turned, b + 1)
                act.activation(hotT[:, block_of(b)], hot_ps[:, :], ACT.Copy).then_inc(hot_stored, 1)
            act.wait_ge(comb_turned, 1)
            act.activation(combine[:, :], comb_ps[0:NC * NE, :], ACT.Copy).then_inc(comb_stored, 1)

        @block.vector
        def _(dve):
            done = 0

            def after(ins):
                nonlocal done
                done += 1
                ins.then_inc(step, 1)
                dve.wait_ge(step, done)

            def over(ap, n, dim):
                a = ap.unsqueeze(dim)
                shape = list(a.shape)
                shape[dim] = n
                return a.broadcast_to(shape)

            dve.tensor_copy(identb[:, :], S.ident[:, :])
            dve.wait_ge(loaded, 64)
            dve.tensor_copy(gh[:, :, :], gate[:, :, :]).then_inc(step, 1)
            dve.wait_ge(step, 1)
            dve.tensor_tensor(gl[:, :, :], gate[:, :, :], fp(gh[:, :, :]), ALU.subtract).then_inc(gate_ready, 1)
            done = 1
            after(dve.tensor_tensor(sim[:, :], sim[:, :], notdiag[:, :], ALU.mult))
            after(dve.tensor_tensor(sim[:, :], sim[:, :], S.ident[:, :], ALU.add))

            dve.wait_ge(logits_ready, 1)
            after(dve.tensor_reduce(top_logit[:, :], logits[:, :, :], AX.X, ALU.max))
            dve.tensor_tensor(shifted[:, :, :], logits[:, :, :], over(top_logit[:, :], NE, 2), ALU.subtract).then_inc(shifted_ready, 1)
            dve.wait_ge(expo_ready, 1)
            after(dve.tensor_reduce(total[:, :], expo[:, :, :], AX.X, ALU.add))
            after(dve.reciprocal(total[:, :], total[:, :]))
            after(dve.tensor_tensor(expo[:, :, :], expo[:, :, :], over(total[:, :], NE, 2), ALU.mult))

            for t in range(NT):
                ins = dve.max(top[:, t, :], expo[:, t, :])
            after(ins)
            for t in range(NT):
                ins = dve.max_index(index[:, t, :], top[:, t, :], expo[:, t, :])
            after(ins)
            after(dve.tensor_copy(indexf[:, :, :], index[:, :, :]))
            dve.tensor_tensor(hot[:, :, :, :].rearrange("p t k e -> p (t k) e"),
                              over(indexf[:, :, :].rearrange("p t k -> p (t k)"), NE, 2),
                              over(iota[:, :], NT * TOPK, 1), ALU.is_equal).then_inc(hot_ready, 1)
            after(dve.tensor_reduce(topsum[:, :], top[:, :, :], AX.X, ALU.add))
            after(dve.tensor_scalar(topsum[:, :], topsum[:, :], 1e-12, None, ALU.max))
            after(dve.reciprocal(topsum[:, :], topsum[:, :]))
            after(dve.tensor_tensor(coef[:, :, :], top[:, :, :], over(topsum[:, :], TOPK, 2), ALU.mult))

            dve.wait_ge(rows_ready, 1)
            flat = product[:, :, :, :].rearrange("p t k e -> p (t k e)")
            for s in range(SEC):
                part = flat[:, (s % 2) * NT * PRIM * NE:(s % 2 + 1) * NT * PRIM * NE].rearrange(
                    "p (t k e) -> p t k e", k=PRIM, e=NE)
                after(dve.tensor_tensor(part, over(rows[:, :, s, :], PRIM, 2), hot[:, :, 0:PRIM, :], ALU.mult))
                ins = dve.tensor_reduce(cand[:, :, s, :], part, AX.X, ALU.add)
            after(ins)
            after(dve.tensor_reduce(best[:, :, :], cand[:, :, :, :], AX.X, ALU.max))
            after(dve.tensor_tensor(isbest[:, :, :, :], cand[:, :, :, :], over(best[:, :, :], PRIM, 3), ALU.is_equal))
            after(dve.tensor_copy(seen[:, :, :], isbest[:, :, :, 0]))
            for q in range(1, PRIM):
                after(dve.tensor_tensor(isbest[:, :, :, q], isbest[:, :, :, q], seen[:, :, :], ALU.is_gt))
                after(dve.tensor_tensor(seen[:, :, :], isbest[:, :, :, q], seen[:, :, :], ALU.max))
            after(dve.tensor_scalar(reroute[:, :, :], best[:, :, :], THRESHOLD, None, ALU.is_ge))
            after(dve.tensor_tensor(moved[:, :, :], coef[:, :, PRIM:TOPK], reroute[:, :, :], ALU.mult))
            after(dve.tensor_tensor(coef[:, :, PRIM:TOPK], coef[:, :, PRIM:TOPK], moved[:, :, :], ALU.subtract))
            after(dve.tensor_tensor(isbest[:, :, :, :], isbest[:, :, :, :], over(moved[:, :, :], PRIM, 3), ALU.mult))
            after(dve.tensor_reduce(gained[:, :, :], isbest[:, :, :, :].rearrange("p t s q -> p t q s"), AX.X, ALU.add))
            after(dve.tensor_tensor(coef[:, :, 0:PRIM], coef[:, :, 0:PRIM], gained[:, :, :], ALU.add))
            after(dve.tensor_tensor(product[:, :, :, :].rearrange("p t k e -> p (t k) e"),
                                    hot[:, :, :, :].rearrange("p t k e -> p (t k) e"),
                                    over(coef[:, :, :].rearrange("p t k -> p (t k)"), NE, 2), ALU.mult))
            after(dve.tensor_reduce(comb[:, :, :], product[:, :, :, :].rearrange("p t k e -> p t e k"), AX.X, ALU.add))
            for c in range(NC):
                ins = dve.tensor_copy(parts[:, :, c, :], comb[:, :, :])
                if c < NC - 1:
                    after(ins)
                    after(dve.tensor_tensor(comb[:, :, :], comb[:, :, :], parts[:, :, c, :], ALU.subtract))
            ins.then_inc(parts_ready, 1)


def experts_stage(nc, S, name, places, w_in, sel_in, combine):
    NWJ = 2 * KC * P + DM
    with ExitStack() as ctx:
        sb = lambda n, shape, dt: ctx.enter_context(nc.sbuf_tensor(f"{places}_{n}", shape, dt))
        sem = lambda n: S.sem(f"{name}_{n}")
        ps = lambda n, shape: ctx.enter_context(nc.psum_tensor(f"{places}_{n}", shape, FP32))
        raw = [sb(f"raw{i}", [P, NWJ], FP32) for i in range(2)]
        Wh = [sb(f"w_hi{i}", [P, NWJ], F32R) for i in range(2)]
        Wl = [sb(f"w_lo{i}", [P, NWJ], F32R) for i in range(2)]
        zeros = sb("zeros", [P, KC * P], FP32)
        sel = [sb(f"select{i}", [NC * NE, P], BF16) for i in range(2)]
        a = [sb(f"silu{i}", [P, TB], FP32) for i in range(2)]
        au = [sb(f"silu_up{i}", [P, TB], FP32) for i in range(2)]
        h = [sb(f"inner{i}", [P, TB], FP32) for i in range(2)]
        Hh = [sb(f"inner_hi{i}", [P, TB], F32R) for i in range(2)]
        Hl = [sb(f"inner_lo{i}", [P, TB], F32R) for i in range(2)]
        gate_ps = [ps(f"gate{i}", [P, TB]) for i in range(2)]
        up_ps = [ps(f"up{i}", [P, TB]) for i in range(2)]
        comb_ps = [ps(f"weight{i}", [P, TB]) for i in range(2)]
        out_ps = ps("out", [P, TPB, DM])
        raw_loaded = [sem(f"raw_loaded{i}") for i in range(2)]
        sel_loaded = [sem(f"select_loaded{i}") for i in range(2)]
        piece_hi, w_split, inner_lo = sem("piece_hi"), sem("w_split"), sem("inner_lo")
        gate_made, up_made, comb_made, out_made = sem("gate_made"), sem("up_made"), sem("weight_made"), sem("out_made")
        silu_ready, inner_hi = sem("silu_ready"), sem("inner_hi")
        up_used, inner_ready, out_added = sem("up_used"), sem("inner_ready"), sem("out_added")
        block = ctx.enter_context(nc.Block())
        SPL = 2 * NB
        LOOPS = JT // 2
        PIECES = 3
        DOWN = slice(2 * KC * P, NWJ)

        @block.sync
        def _(sp):
            def load(j, i):
                sp.dma_start(raw[i][:, :], w_in[bass.ds(j, 1), :, :].rearrange("j p n -> (j p) n")).then_inc(raw_loaded[i], 16)

            def load_sel(j, i):
                sp.dma_start(sel[i][:, :], sel_in[bass.ds(j, 1), :, :].rearrange("j p n -> (j p) n")).then_inc(sel_loaded[i], 16)

            for i in range(2):
                load(i, i)
                load_sel(i, i)
            with sp.Fori(0, LOOPS - 1) as l:
                for i in range(2):
                    sp.wait_ge(w_split, l * (2 * PIECES) + PIECES * (i + 1))
                    load(l * 2 + (i + 2), i)
                    sp.wait_ge(comb_made, l * SPL + NB * (i + 1))
                    load_sel(l * 2 + (i + 2), i)

        @block.gpsimd
        def _(pool):
            def split(piece, l, i):
                cols = slice(piece * KC * P, (piece + 1) * KC * P)
                count = l * (2 * PIECES) + (PIECES * i + piece + 1)
                if piece == 0:
                    pool.wait_ge(raw_loaded[i], l * 16 + 16)
                pool.tensor_tensor(Wh[i][:, cols], raw[i][:, cols], zeros[:, :], ALU.add).then_inc(piece_hi, 1)
                pool.wait_ge(piece_hi, count)
                pool.tensor_tensor(Wl[i][:, cols], raw[i][:, cols], fp(Wh[i][:, cols]), ALU.subtract).then_inc(w_split, 1)

            def low(n, q):
                pool.wait_ge(inner_hi, n + 1)
                pool.tensor_tensor(Hl[q][:, :], h[q][:, :], fp(Hh[q][:, :]), ALU.subtract).then_inc(inner_lo, 1)

            pool.memset(zeros[:, :], 0.0)
            for z in (Hh[1], Hl[1], Wh[1], Wl[1]):
                ins = pool.memset(fp(z[:, :]), 0.0)
            ins.then_inc(inner_lo, 1)
            pool.wait_ge(inner_lo, 1)
            for piece in range(PIECES):
                split(piece, 0, 0)

            def round_(l, last):
                for m in range(SPL):
                    i, b = m // NB, m % NB
                    low(l * SPL + m, m % 2)
                    if b < PIECES and not (last and i == 1):
                        if b == 0:
                            pool.wait_ge(out_made, l * SPL + (m + 1))
                        split(b, l + i, 1 - i)

            with pool.Fori(0, LOOPS - 1) as l:
                round_(l, False)
            round_(LOOPS - 1, True)

        @block.tensor
        def _(pe):
            def inner(n, l, m):
                i, b, q = m // NB, m % NB, m % 2
                if b == 0:
                    pe.wait_ge(w_split, l * (2 * PIECES) + (PIECES * i + 2))
                    pe.wait_ge(sel_loaded[i], l * 16 + 16)
                for half, bank, made in ((0, gate_ps, gate_made), (1, up_ps, up_made)):
                    for c in range(KC):
                        cols = slice((half * KC + c) * P, (half * KC + c + 1) * P)
                        for k, (w, x) in enumerate(((Wh, S.xh), (Wh, S.xl), (Wl, S.xh))):
                            mm = pe.matmul(bank[q][:, :], w[i][:, cols], x[:, c, block_of(b)],
                                           start=(c == 0 and k == 0), stop=(c == KC - 1 and k == 2))
                    mm.then_inc(made, 1)
                pe.matmul(comb_ps[q][:, :], sel[i][:, :], combine[:, block_of(b)], start=True, stop=True).then_inc(comb_made, 1)

            def outputs(n, m):
                m1 = (m - 1) % SPL
                i, q = m1 // NB, m1 % 2
                pe.wait_ge(inner_lo, n + 1)
                pe.wait_ge(out_added, n + 1)
                for t in range(TPB):
                    cols = slice(t * P, (t + 1) * P)
                    for k, (g, w) in enumerate(((Hh, Wh), (Hh, Wl), (Hl, Wh))):
                        mm = pe.matmul(out_ps[:, t, :], g[q][:, cols], w[i][:, DOWN], start=(k == 0), stop=(k == 2))
                mm.then_inc(out_made, 1)

            with pe.Fori(0, LOOPS) as l:
                for m in range(SPL):
                    n = l * SPL + m
                    inner(n, l, m)
                    if m % NB == 1:
                        pe.wait_ge(w_split, l * (2 * PIECES) + PIECES * (m // NB + 1))
                    outputs(n, m)
            outputs(LOOPS * SPL, 0)

        @block.scalar
        def _(act):
            with act.Fori(0, LOOPS) as l:
                for m in range(SPL):
                    n, q = l * SPL + m, m % 2
                    act.wait_ge(gate_made, n + 1)
                    act.activation(a[q][:, :], gate_ps[q][:, :], ACT.Silu).then_inc(silu_ready, 1)
                    act.wait_ge(inner_ready, n + 1)
                    act.activation(Hh[q][:, :], h[q][:, :], ACT.Copy).then_inc(inner_hi, 1)

        @block.vector
        def _(dve):
            def add(n, m):
                b = (m - 1) % NB
                dve.wait_ge(out_made, n + 1)
                x = S.x[:, b * TPB:(b + 1) * TPB, :]
                dve.tensor_tensor(x, x, out_ps[:, :, :], ALU.add).then_inc(out_added, 1)

            dve.sem_inc(out_added, 1)
            with dve.Fori(0, LOOPS) as l:
                for m in range(SPL):
                    n, q = l * SPL + m, m % 2
                    dve.wait_ge(silu_ready, n + 1)
                    dve.wait_ge(up_made, n + 1)
                    dve.tensor_tensor(au[q][:, :], a[q][:, :], up_ps[q][:, :], ALU.mult).then_inc(up_used, 1)
                    dve.wait_ge(up_used, n + 1)
                    dve.wait_ge(comb_made, n + 1)
                    dve.tensor_tensor(h[q][:, :], au[q][:, :], comb_ps[q][:, :], ALU.mult).then_inc(inner_ready, 1)
                    add(n, m)
            add(LOOPS * SPL, 0)


LH, LKV, LD = 16, 8, 16
LF = LD
LE = LF // 2
TWO_PI_HI = 6.28125
TWO_PI_LO = 2 * math.pi - TWO_PI_HI
ROUND = 1.5 * 2.0 ** 23


def linear_stage(nc, S, w_in, bias_in, bv_in, wo_in, bo_in, cos_in, sin_in, rand_in, ones_in, scratch):
    HT = 8
    NU = LH // HT + LKV // HT
    NHD = NU * HT
    COLS = LE + 1
    MID = HT * LE
    OUT = 7
    VT = 3
    with ExitStack() as ctx:
        sb = lambda n, shape, dt=FP32: ctx.enter_context(nc.sbuf_tensor(f"l_{n}", shape, dt))
        sem = lambda n: S.sem(f"l_{n}")
        ps = lambda n, shape: ctx.enter_context(nc.psum_tensor(f"l_{n}", shape, FP32))

        w = sb("w", [P, KC, OUT, P])
        wh, wl = sb("w_hi", [P, KC, OUT, P], F32R), sb("w_lo", [P, KC, OUT, P], F32R)
        wo = sb("wo", [P, KC, DM])
        woh, wol = sb("wo_hi", [P, KC, DM], F32R), sb("wo_lo", [P, KC, DM], F32R)
        bias = sb("bias", [P, OUT])
        bv = sb("bv", [P, P])
        bo = sb("bo", [P, DM])
        tables = sb("tables", [P, 2 * TOK])
        cos, sin = tables[:, 0:TOK], tables[:, TOK:2 * TOK]
        rand = sb("rand", [P, MID])
        ones = sb("ones", [P, HT])
        by_cos = [sb(f"by_cos{i}", [P, TB]) for i in range(2)]
        by_sin = [sb(f"by_sin{i}", [P, TB]) for i in range(2)]
        rot = [sb(f"rotated{i}", [P, TB]) for i in range(2)]
        square = [sb(f"square{i}", [P, TB]) for i in range(2)]
        proj = sb("projected", [P, NT, NHD * LE])
        norm = sb("square_norm", [P, NT, NHD])
        v = sb("values", [P, NT, LKV * LD])
        sd, r2 = sb("norm", [P, NT, NHD]), sb("newton", [P, NT, NHD])
        turns = sb("turns", [P, NT, NHD * LE])
        feat = sb("features", [P, NT, NHD, 2, LE])
        half_pi = sb("half_pi", [P, 1])
        pairs = [sb(f"pair_products{i}", [P, LH, LKV, LF]) for i in range(2)]
        att = sb("pair_sums", [P, LH, LKV])
        outs = sb("out_products", [P, LH, LD, LKV])
        o = tables[:, :].rearrange("p (t h d) -> p t h d", t=NT, h=LH)
        z = o
        zz = feat[:, :, :, :, :].rearrange("p t h s e -> p (t h s e)")[:, 0:LH * LD * LD].rearrange(
            "p (h n) -> p h n", h=LH)
        zh = [sb(f"out_hi{i}", [P, KC, P], F32R) for i in range(2)]
        zl = [sb(f"out_lo{i}", [P, KC, P], F32R) for i in range(2)]

        straight = [ps(f"straight{i}", [P, TB]) for i in range(2)]
        swapped = [ps(f"swapped{i}", [P, TB]) for i in range(2)]
        mid = ps("mid", [P, 2, TB])
        v_ps = ps("v", [P, TPB, P])
        zt = swapped
        zs = straight

        loaded, w_loaded, wo_loaded = sem("loaded"), sem("w_loaded"), sem("wo_loaded")
        w_ready, wo_hi, wo_ready, w_hi = sem("w_ready"), sem("wo_hi"), sem("wo_ready"), sem("w_hi")
        made, turned, rotated, squared = sem("made"), sem("cos_sin_used"), sem("rotated"), sem("squared")
        mid_made, mid_stored, v_made, v_stored = sem("mid_made"), sem("mid_stored"), sem("v_made"), sem("v_stored")
        step, norm_ready, sd_ready, angle_ready, abs_ready, feat_ready = (
            sem("step"), sem("norm_ready"), sem("sd_ready"), sem("angle_ready"), sem("abs_ready"), sem("feat_ready"))
        pairs_ready, att_ready, outs_ready, o_ready = sem("pairs_ready"), sem("att_ready"), sem("outs_ready"), sem("o_ready")
        stored, back, ordered = sem("stored"), sem("back"), sem("ordered")
        z_turned, z_hi, z_lo, y_made, y_added = sem("z_turned"), sem("z_hi"), sem("z_lo"), sem("y_made"), sem("y_added")
        block = ctx.enter_context(nc.Block())
        units = [(b, u) for b in range(NB) for u in range(NU)]

        def order(copy, h0):
            return copy(zz[:, h0:h0 + LH // 2, :].rearrange("p h (i d) -> p h i d", d=LD),
                        z[:, :, h0:h0 + LH // 2, :].rearrange("p i h d -> p h i d"))

        @block.sync
        def _(sp):
            sp.dma_start(w[:, :, :, :], w_in).then_inc(w_loaded, 16)
            for dst, src in ((bias[:, :], bias_in), (bv[:, :], bv_in), (bo[:, :], bo_in), (cos[:, :], cos_in),
                             (sin[:, :], sin_in), (rand[:, :], rand_in), (ones[:, :], ones_in)):
                sp.dma_start(dst, src).then_inc(loaded, 16)
            sp.dma_start(wo[:, :, :], wo_in).then_inc(wo_loaded, 16)
            for b in range(NB):
                sp.wait_ge(o_ready, TPB * (b + 1))
                sp.dma_start(scratch[b * TB:(b + 1) * TB, :].rearrange("(t p) n -> p t n", p=P),
                             o[:, b * TPB:(b + 1) * TPB, :, :].rearrange("p t h d -> p t (h d)")).then_inc(stored, 16)
            sp.wait_ge(stored, 16 * NB)
            sp.dma_start(z[:, :, :, :].rearrange("p i h d -> p (i h d)"),
                         scratch.rearrange("(j i) n -> j (i n)", i=LD)).then_inc(back, 16)
            sp.wait_ge(back, 16)

        @block.gpsimd
        def _(pool):
            flat = lambda t: t[:, :, :].rearrange("p c n -> p (c n)")
            pool.wait_ge(wo_loaded, 16)
            pool.tensor_copy(flat(woh), flat(wo)).then_inc(wo_hi, 1)
            pool.wait_ge(wo_hi, 1)
            pool.tensor_tensor(flat(wol), flat(wo), fp(flat(woh)), ALU.subtract).then_inc(wo_ready, 1)
            for n in range(len(units)):
                pool.wait_ge(turned, n + 1)
                if n >= 2:
                    pool.wait_ge(mid_made, n - 1)
                pool.tensor_tensor(rot[n % 2][:, :], by_cos[n % 2][:, :], by_sin[n % 2][:, :], ALU.add).then_inc(rotated, 1)
            pool.wait_ge(feat_ready, 1)
            for t in range(NT):
                if t >= 2:
                    pool.wait_ge(att_ready, t - 1)
                f = feat[:, t, :, :, :].rearrange("p h s e -> p h (s e)")
                pool.tensor_tensor(pairs[t % 2][:, :, :, :],
                                   f[:, 0:LH, :].unsqueeze(2).broadcast_to([P, LH, LKV, LF]),
                                   f[:, LH:NHD, :].unsqueeze(1).broadcast_to([P, LH, LKV, LF]),
                                   ALU.mult).then_inc(pairs_ready, 1)

        @block.tensor
        def _(pe):
            def project(bank, tile_, b):
                for c in range(KC):
                    for k, (a, x) in enumerate(((wh, S.xh), (wh, S.xl), (wl, S.xh))):
                        mm = pe.matmul(bank, a[:, c, tile_, :], x[:, c, block_of(b)],
                                       start=(c == 0 and k == 0), stop=(c == KC - 1 and k == 2))
                return mm

            def middle(n):
                b, u = units[n]
                pe.wait_ge(rotated, n + 1)
                if u == 0 and b:
                    pe.wait_ge(mid_stored, b)
                for t in range(TPB):
                    at = mid[:, t // 2, (t % 2) * NU * HT * COLS + u * HT * COLS:]
                    pe.matmul(at[:, 0:MID], rot[n % 2][:, t * P:(t + 1) * P], rand[:, :], start=True, stop=True)
                pe.wait_ge(squared, n + 1)
                for t in range(TPB):
                    at = mid[:, t // 2, (t % 2) * NU * HT * COLS + u * HT * COLS:]
                    mm = pe.matmul(at[:, MID:MID + HT], square[n % 2][:, t * P:(t + 1) * P], ones[:, :], start=True, stop=True)
                mm.then_inc(mid_made, 1)

            pe.wait_ge(w_ready, 1)
            pe.wait_ge(loaded, 16 * 7)
            for n, (b, u) in enumerate(units):
                if n >= 2:
                    pe.wait_ge(turned, n - 1)
                project(straight[n % 2][:, :], u, b)
                project(swapped[n % 2][:, :], VT + 1 + u, b).then_inc(made, 1)
                if u == 0:
                    if b:
                        pe.wait_ge(v_stored, b)
                    for t in range(TPB):
                        cols = slice((b * TPB + t) * P, (b * TPB + t + 1) * P)
                        for c in range(KC):
                            for k, (x, a) in enumerate(((S.xh, wh), (S.xh, wl), (S.xl, wh))):
                                mm = pe.matmul(v_ps[:, t, :], x[:, c, cols], a[:, c, VT, :],
                                               start=(c == 0 and k == 0), stop=(c == KC - 1 and k == 2))
                    mm.then_inc(v_made, 1)
                if n:
                    middle(n - 1)
            middle(len(units) - 1)

            pe.wait_ge(ordered, 2)
            pe.wait_ge(wo_ready, 1)
            pe.wait_ge(v_stored, NB)

            def turn_head(h):
                if h >= 2:
                    pe.wait_ge(z_lo, h - 1)
                for c in range(KC):
                    mm = pe.transpose(zt[h % 2][:, c * P:(c + 1) * P], zz[:, h, c * P:(c + 1) * P], S.ident[:, :])
                mm.then_inc(z_turned, 1)

            turn_head(0)
            for h in range(LH):
                if h + 1 < LH:
                    turn_head(h + 1)
                pe.wait_ge(z_lo, h + 1)
                if h >= 2:
                    pe.wait_ge(y_added, h - 1)
                for c in range(KC):
                    for k, (a, ww) in enumerate(((zh, woh), (zh, wol), (zl, woh))):
                        mm = pe.matmul(zs[h % 2][:, 0:DM], a[h % 2][:, c, :], ww[:, c, :],
                                       start=(c == 0 and k == 0), stop=(c == KC - 1 and k == 2))
                mm.then_inc(y_made, 1)

        @block.scalar
        def _(act):
            flat = lambda t: t[:, :, :, :].rearrange("p c o n -> p (c o n)")
            act.wait_ge(w_loaded, 16)
            act.activation(flat(wh), flat(w), ACT.Copy).then_inc(w_hi, 1)
            for n, (b, u) in enumerate(units):
                act.wait_ge(rotated, n + 1)
                if n >= 2:
                    act.wait_ge(mid_made, n - 1)
                act.activation(square[n % 2][:, :], rot[n % 2][:, :], ACT.Square).then_inc(squared, 1)
                if u == NU - 1:
                    act.wait_ge(mid_made, n + 1)
                    for bank in range(2):
                        m = mid[:, bank, 0:2 * NU * HT * COLS].rearrange("p (t u n) -> p t u n", t=2, u=NU)
                        t = b * TPB + 2 * bank
                        act.activation(proj[:, t:t + 2, :].rearrange("p t (u n) -> p t u n", u=NU), m[:, :, :, 0:MID], ACT.Copy)
                        ins = act.activation(norm[:, t:t + 2, :].rearrange("p t (u n) -> p t u n", u=NU), m[:, :, :, MID:], ACT.Copy)
                    ins.then_inc(mid_stored, 1)
            act.wait_ge(norm_ready, 1)
            act.activation(sd[:, :, :], norm[:, :, :], ACT.Sqrt).then_inc(sd_ready, 1)
            act.wait_ge(angle_ready, 1)
            angles = proj[:, :, :].rearrange("p t (h e) -> p (t h) e", e=LE)
            place = lambda s: feat[:, :, :, s, :].rearrange("p t h e -> p (t h) e")
            act.activation(place(0), angles, ACT.Sin)
            act.activation(turns[:, :, :], proj[:, :, :], ACT.Abs).then_inc(abs_ready, 1)
            act.wait_ge(abs_ready, 1)
            act.activation(place(1), turns[:, :, :].rearrange("p t (h e) -> p (t h) e", e=LE), ACT.Sin,
                           scale=-1.0, bias=half_pi[:, :]).then_inc(feat_ready, 1)
            act.wait_ge(back, 16)
            act.wait_ge(att_ready, NT)
            order(lambda out, in_: act.activation(out, in_, ACT.Copy), 0).then_inc(ordered, 1)
            for h in range(LH):
                act.wait_ge(z_turned, h + 1)
                if h >= 2:
                    act.wait_ge(y_made, h - 1)
                act.activation(zh[h % 2][:, :, :].rearrange("p c n -> p (c n)"), zt[h % 2][:, 0:DM], ACT.Copy).then_inc(z_hi, 1)

        @block.vector
        def _(dve):
            done = 0

            def after(ins):
                nonlocal done
                done += 1
                ins.then_inc(step, 1)
                dve.wait_ge(step, done)

            flat = lambda t: t[:, :, :, :].rearrange("p c o n -> p (c o n)")
            dve.wait_ge(w_hi, 1)
            dve.tensor_tensor(flat(wl), flat(w), fp(flat(wh)), ALU.subtract).then_inc(w_ready, 1)
            dve.memset(half_pi[:, :], math.pi / 2)
            dve.wait_ge(loaded, 16 * 7)
            VS = (LH // LKV) / LF
            after(dve.tensor_scalar(bv[:, :], bv[:, :], VS, None, ALU.mult))
            for n, (b, u) in enumerate(units):
                i = n % 2
                dve.wait_ge(made, n + 1)
                if n >= 2:
                    dve.wait_ge(rotated, n - 1)
                dve.scalar_tensor_tensor(out=by_cos[i][:, :], in0=straight[i][:, :], scalar=bias[:, u:u + 1],
                                         in1=cos[:, block_of(b)], op0=ALU.add, op1=ALU.mult)
                dve.scalar_tensor_tensor(out=by_sin[i][:, :], in0=swapped[i][:, :], scalar=bias[:, VT + 1 + u:VT + 2 + u],
                                         in1=sin[:, block_of(b)], op0=ALU.add, op1=ALU.mult).then_inc(turned, 1)
                if u == 0:
                    dve.wait_ge(v_made, b + 1)
                    dve.scalar_tensor_tensor(out=v[:, b * TPB:(b + 1) * TPB, :], in0=v_ps[:, :, :], scalar=VS,
                                             in1=bv[:, :].unsqueeze(1).broadcast_to([P, TPB, P]),
                                             op0=ALU.mult, op1=ALU.add).then_inc(v_stored, 1)
            for t in range(NT):
                ins = dve.tensor_tensor(S.x[:, t, :], S.x[:, t, :], bo[:, :], ALU.add)
            dve.wait_ge(mid_stored, NB)
            dve.tensor_scalar(norm[:, :, :], norm[:, :, :], 1e-12, None, ALU.max).then_inc(norm_ready, 1)
            dve.wait_ge(sd_ready, 1)
            after(dve.reciprocal(sd[:, :, :], sd[:, :, :]))
            after(dve.tensor_tensor(r2[:, :, :], sd[:, :, :], sd[:, :, :], ALU.mult))
            after(dve.tensor_tensor(r2[:, :, :], r2[:, :, :], norm[:, :, :], ALU.mult))
            after(dve.tensor_scalar(r2[:, :, :], r2[:, :, :], -0.5, 1.5, ALU.mult, ALU.add))
            after(dve.tensor_tensor(sd[:, :, :], sd[:, :, :], r2[:, :, :], ALU.mult))
            p = proj[:, :, :]
            heads = p.rearrange("p t (h e) -> p (t h) e", e=LE)
            after(dve.tensor_tensor(heads, heads, sd[:, :, :].rearrange("p t h -> p (t h)").unsqueeze(2).broadcast_to(
                [P, NT * NHD, LE]), ALU.mult))
            tn = turns[:, :, :]
            after(dve.tensor_scalar(tn, p, 1 / (2 * math.pi), ROUND, ALU.mult, ALU.add))
            after(dve.tensor_scalar(tn, tn, ROUND, None, ALU.subtract))
            after(dve.scalar_tensor_tensor(out=p, in0=tn, scalar=-TWO_PI_HI, in1=p, op0=ALU.mult, op1=ALU.add))
            after(dve.scalar_tensor_tensor(out=p, in0=tn, scalar=-TWO_PI_LO, in1=p, op0=ALU.mult, op1=ALU.add))
            PI = float(np.nextafter(np.float32(math.pi), np.float32(0)))
            dve.tensor_scalar(p, p, PI, -PI, ALU.min, ALU.max).then_inc(angle_ready, 1)
            for t in range(NT):
                dve.wait_ge(pairs_ready, t + 1)
                dve.tensor_reduce(att[:, :, :], pairs[t % 2][:, :, :, :], AX.X, ALU.add).then_inc(att_ready, 1)
                dve.wait_ge(att_ready, t + 1)
                dve.tensor_tensor(outs[:, :, :, :], att[:, :, :].unsqueeze(2).broadcast_to([P, LH, LD, LKV]),
                                  v[:, t, :].rearrange("p (k d) -> p d k", d=LD).unsqueeze(1).broadcast_to([P, LH, LD, LKV]),
                                  ALU.mult).then_inc(outs_ready, 1)
                dve.wait_ge(outs_ready, t + 1)
                dve.tensor_reduce(o[:, t, :, :], outs[:, :, :, :], AX.X, ALU.add).then_inc(o_ready, 1)
            dve.wait_ge(back, 16)
            order(dve.tensor_copy, LH // 2).then_inc(ordered, 1)
            for h in range(LH):
                dve.wait_ge(z_hi, h + 1)
                one = lambda z_: z_[h % 2][:, :, :].rearrange("p c n -> p (c n)")
                dve.tensor_tensor(one(zl), zt[h % 2][:, 0:DM], fp(one(zh)), ALU.subtract).then_inc(z_lo, 1)
                if h >= 1:
                    dve.wait_ge(y_made, h)
                    dve.tensor_tensor(S.x[:, h - 1, :], S.x[:, h - 1, :], zs[(h - 1) % 2][:, 0:DM], ALU.add).then_inc(y_added, 1)
            dve.wait_ge(y_made, LH)
            dve.tensor_tensor(S.x[:, LH - 1, :], S.x[:, LH - 1, :], zs[(LH - 1) % 2][:, 0:DM], ALU.add).then_inc(y_added, 1)


def store_stage(nc, S, out):
    with ExitStack() as ctx:
        stored = S.sem("stored")
        block = ctx.enter_context(nc.Block())

        @block.sync
        def _(sp):
            sp.dma_start(out.rearrange("(t p) d -> p t d", p=P), S.x[:, :, :]).then_inc(stored, 16)
            sp.wait_ge(stored, 16)


def hybrid_block(nc, a, out):
    scratch = nc.dram_tensor("heads_by_token", (TOK, DM), FP32).ap()
    with ExitStack() as ctx:
        S = Shared(nc, ctx)
        load_stage(nc, S, a["x"], a["identity"])
        norm_stage(nc, S, "n1")
        attention_stage(nc, S, a["wqkv_codes"], a["wqkv_scales"], a["wo_codes"], a["wo_scales"], a["bo"])
        for i in range(2):
            if i == 1:
                clear_stage(nc, S, ("mn", "mr", "me"))
            norm_stage(nc, S, "mn", f"mn{i}")
            with ExitStack() as moe:
                combine = moe.enter_context(nc.sbuf_tensor(f"combine{i}", [NC * NE, TOK], BF16))
                route_stage(nc, S, "mr", f"mr{i}", a["gate_w"], a["similarity"], a["notdiag"], a["iota"], combine)
                experts_stage(nc, S, "me", f"me{i}", a["experts_w"], a["select"].bitcast(BF16), combine)
            if i == 0:
                norm_stage(nc, S, "n3")
                linear_stage(nc, S, a["lin_w"], a["lin_bias"], a["lin_bv"], a["lin_wo"], a["lin_bo"], a["cos"],
                             a["sin"], a["rand"], a["ones"], scratch)
        store_stage(nc, S, out)


def _arrays(d):
    A = lambda n: np.asarray(d["L0_attn_a_" + n])
    B = lambda n: np.asarray(d["L0_attn_b_" + n])
    F = lambda n: np.asarray(d["L0_ffn_" + n])
    f32 = np.float32
    out = {"x": A("x").reshape(TOK, DM), "identity": np.eye(P, dtype=f32)}

    def by_head(w):
        return w.reshape(KC, P, NH, HD).transpose(2, 1, 0, 3)

    def wrap(w, n):
        return np.concatenate([w, w[:n]], 0)

    codes = np.stack([by_head(A(f"w{m}_codes")) for m in "qkv"], 2).reshape(NH, P, -1)
    scales = np.stack([by_head(np.repeat(A(f"w{m}_scales"), 32, 0)) for m in "qkv"], 2).reshape(NH, P, -1)
    biases = np.stack([A("b" + m).reshape(NH, HD) for m in "qkv"], 2)
    out["wqkv_codes"] = wrap(np.concatenate([codes, biases], 2), 2)
    out["wqkv_scales"] = wrap(scales, 2)
    out["wo_codes"] = wrap(A("wo_codes").reshape(NH, HD, DM), 1)
    out["wo_scales"] = wrap(np.repeat(A("wo_scales"), 32, 0).reshape(NH, HD, DM), 1)
    out["bo"] = np.broadcast_to(A("bo"), (P, DM))

    gu = F("gate_up_proj")
    turn = lambda w: w.reshape(JT, P, KC, P).transpose(0, 3, 2, 1).reshape(JT, P, DM)
    gate, up = turn(gu[:, :FF].reshape(NF, DM)), turn(gu[:, FF:].reshape(NF, DM))
    down = F("down_proj").transpose(0, 2, 1).reshape(JT, P, DM)
    out["experts_w"] = np.concatenate([gate, up, down], 2)
    select = np.zeros((JT, NC, NE, P), np.uint16)
    for j in range(JT):
        for f in range(P):
            select[j, :, (j * P + f) // FF, f] = 0x3F80
    out["select"] = select.reshape(JT, NC * NE, P)
    out["gate_w"] = F("gate_weight").T.reshape(KC, P, NE).transpose(1, 0, 2)
    sim = np.zeros((P, P), f32)
    for s in range(SEC):
        sim[s * NE:(s + 1) * NE, s * NE:(s + 1) * NE] = F("similarity")
    out["similarity"] = sim
    out["notdiag"] = 1 - np.eye(P, dtype=f32)
    out["iota"] = np.broadcast_to(np.arange(NE, dtype=f32), (P, NE))

    def swap(w):
        w = w.reshape(-1, 2, LD // 2, *w.shape[1:])
        return w[:, ::-1].reshape(-1, *w.shape[3:])

    rows = lambda f: np.concatenate([B(f + "q"), B(f + "k"), B(f + "v"), swap(B(f + "q")), swap(B(f + "k"))], 0)
    out["lin_w"] = rows("W").reshape(7, P, KC, P).transpose(3, 2, 0, 1)
    out["lin_bias"] = rows("b").reshape(7, P).T
    out["lin_bv"] = np.broadcast_to(B("bv"), (P, P))
    out["lin_wo"] = B("Wo").T.reshape(KC, P, DM).transpose(1, 0, 2)
    out["lin_bo"] = np.broadcast_to(B("bo"), (P, DM))
    inv = (f32(1) / f32(10000.0) ** (np.arange(0, LD, 2, dtype=f32) / f32(LD))).astype(f32)
    angle = (np.arange(TOK, dtype=f32)[:, None] * inv[None, :]).astype(f32).astype(np.float64)
    sign = np.where(np.arange(P) % LD < LD // 2, -1.0, 1.0)[:, None]
    out["cos"] = np.cos(angle).T[np.arange(P) % (LD // 2)].astype(f32)
    out["sin"] = (np.sin(angle).T[np.arange(P) % (LD // 2)] * sign).astype(f32)
    rand, ones = np.zeros((P, 8, LE), f32), np.zeros((P, 8), f32)
    for h in range(8):
        rand[h * LD:(h + 1) * LD, h] = B("rand_matrix").T
        ones[h * LD:(h + 1) * LD, h] = 1
    out["rand"], out["ones"] = rand.reshape(P, -1), ones
    return {k: np.ascontiguousarray(v) for k, v in out.items()}


def kernel(**inputs):
    from concourse import bacc
    from concourse.bass_utils import run_bass_kernel_spmd

    nc = bacc.Bacc("TRN2", target_bir_lowering=False, num_devices=1)
    arrays = _arrays(inputs)
    args = {n: nc.dram_tensor("in_" + n, v.shape, mybir.dt.from_np(v.dtype), kind="ExternalInput").ap()
            for n, v in arrays.items()}
    out = nc.dram_tensor("out", (TOK, DM), FP32, kind="ExternalOutput").ap()
    hybrid_block(nc, args, out)
    r = run_bass_kernel_spmd(nc, [{"in_" + n: v for n, v in arrays.items()}], core_ids=[0])
    return r.results[0]["out"].reshape(1, TOK, DM)
```

```python
import math
from contextlib import ExitStack

import numpy as np

import concourse.bass as bass
from concourse import mybir

FP32 = mybir.dt.float32
F32R = mybir.dt.float32r
FP16 = mybir.dt.float16
BF16 = mybir.dt.bfloat16
U32 = mybir.dt.uint32
ALU = mybir.AluOpType
ACT = mybir.ActivationFunctionType
AX = mybir.AxisListType

P = 128
TOK = 2048
DM = 256
NT = TOK // P
NB = 4
TB = TOK // NB
TPB = NT // NB
KC = DM // P
NH = 16
HD = 128
EPS = 1e-5


def fp(ap):
    return ap.bitcast(FP32)


def block_of(b):
    return bass.ds(b * TB, TB)


class Shared:

    def __init__(self, nc, ctx):
        self.made = {}
        self.new_sem = lambda name: ctx.enter_context(nc.semaphore(name))
        sb = lambda name, shape, dt: ctx.enter_context(nc.sbuf_tensor(name, shape, dt))
        self.x = sb("residual", [P, NT, DM], FP32)
        self.xh = sb("normed_hi", [P, KC, TOK], F32R)
        self.xl = sb("normed_lo", [P, KC, TOK], F32R)
        self.ident = sb("identity_sb", [P, P], FP32)


    def sem(self, name):
        if name not in self.made:
            self.made[name] = self.new_sem(name)
        return self.made[name]


def clear_stage(nc, S, prefixes):
    block_ctx = ExitStack()
    with block_ctx:
        block = block_ctx.enter_context(nc.Block())

        @block.gpsimd
        def _(pool):
            for name, sem in S.made.items():
                if name.split("_")[0] in prefixes:
                    pool.sem_clear(sem)


def load_stage(nc, S, x_in, ident_in):
    with ExitStack() as ctx:
        loaded = S.sem("x_loaded")
        ident_loaded = S.sem("ident_loaded")
        block = ctx.enter_context(nc.Block())

        @block.sync
        def _(sp):
            sp.dma_start(S.x[:, :, :], x_in.rearrange("(t p) d -> p t d", p=P)).then_inc(loaded, 16)
            sp.dma_start(S.ident[:, :], ident_in).then_inc(ident_loaded, 16)
            sp.wait_ge(loaded, 16)
            sp.wait_ge(ident_loaded, 16)


def norm_stage(nc, S, name, places=None):
    places = places or name
    with ExitStack() as ctx:
        sb = lambda n, shape, dt: ctx.enter_context(nc.sbuf_tensor(f"{places}_{n}", shape, dt))
        sem = lambda n: S.sem(f"{name}_{n}")
        stats = sb("stats", [P, NT, 6], FP32)
        mv = sb("mean_var", [P, NT, 2], FP32)
        ve = sb("var_eps", [P, NT], FP32)
        sd = sb("sd", [P, NT], FP32)
        r = sb("rsd", [P, NT], FP32)
        r2 = sb("rsd_square", [P, NT], FP32)
        fix = sb("newton", [P, NT], FP32)
        xn = sb("normed", [P, NT, DM], FP32)
        turned = [ctx.enter_context(nc.psum_tensor(f"{places}_turned{i}", [P, TB], FP32)) for i in range(4)]
        stats_done, var_ready, sd_ready = sem("stats_done"), sem("var_ready"), sem("sd_ready")
        small, normed = sem("small"), sem("normed")
        turned_ready, hi_ready, lo_ready = sem("turned_ready"), sem("hi_ready"), sem("lo_ready")
        block = ctx.enter_context(nc.Block())

        @block.vector
        def _(dve):
            for t in range(NT):
                dve.bn_stats(stats[:, t, :], S.x[:, t, :]).then_inc(stats_done, 1)
            for t in range(NT):
                dve.wait_ge(stats_done, t + 1)
                dve.bn_aggr(mv[:, t, :], stats[:, t, :]).then_inc(small, 1)
            dve.wait_ge(small, NT)
            dve.tensor_scalar(ve[:, :], mv[:, :, 1], EPS, None, ALU.add).then_inc(var_ready, 1)
            dve.wait_ge(sd_ready, 1)
            dve.reciprocal(r[:, :], sd[:, :]).then_inc(small, 1)
            dve.wait_ge(small, NT + 1)
            dve.tensor_tensor(r2[:, :], r[:, :], r[:, :], ALU.mult).then_inc(small, 1)
            dve.wait_ge(small, NT + 2)
            dve.tensor_tensor(r2[:, :], r2[:, :], ve[:, :], ALU.mult).then_inc(small, 1)
            dve.wait_ge(small, NT + 3)
            dve.tensor_scalar(fix[:, :], r2[:, :], -0.5, 1.5, ALU.mult, ALU.add).then_inc(small, 1)
            dve.wait_ge(small, NT + 4)
            dve.tensor_tensor(r[:, :], r[:, :], fix[:, :], ALU.mult).then_inc(small, 1)
            dve.wait_ge(small, NT + 5)

            def lows(n):
                b, c = n // KC, n % KC
                dve.wait_ge(hi_ready, n + 1)
                dve.tensor_tensor(S.xl[:, c, block_of(b)], turned[n % 4][:, :],
                                  fp(S.xh[:, c, block_of(b)]), ALU.subtract).then_inc(lo_ready, 1)

            for t in range(NT):
                dve.tensor_scalar(xn[:, t, :], S.x[:, t, :], mv[:, t, 0:1], r[:, t:t + 1],
                                  ALU.subtract, ALU.mult).then_inc(normed, 1)
                if t % TPB == TPB - 1 and t >= 2 * TPB - 1:
                    lows(KC * (t // TPB) - 2)
                    lows(KC * (t // TPB) - 1)
            lows(KC * NB - 2)
            lows(KC * NB - 1)

        @block.tensor
        def _(pe):
            for b in range(NB):
                pe.wait_ge(normed, TPB * (b + 1))
                for c in range(KC):
                    n = b * KC + c
                    if n >= 4:
                        pe.wait_ge(lo_ready, n - 3)
                    for i in range(TPB):
                        mm = pe.transpose(turned[n % 4][:, i * P:(i + 1) * P],
                                          xn[:, b * TPB + i, c * P:(c + 1) * P], S.ident[:, :])
                    mm.then_inc(turned_ready, 1)

        @block.scalar
        def _(act):
            act.wait_ge(var_ready, 1)
            act.activation(sd[:, :], ve[:, :], ACT.Sqrt).then_inc(sd_ready, 1)
            for n in range(KC * NB):
                b, c = n // KC, n % KC
                act.wait_ge(turned_ready, n + 1)
                act.activation(S.xh[:, c, block_of(b)], turned[n % 4][:, :], ACT.Copy).then_inc(hi_ready, 1)


def attention_stage(nc, S, wqkv_codes, wqkv_scales, wo_codes, wo_scales, bo):
    SCALE = 1.0 / math.sqrt(HD)
    KT = TOK // P
    GK = 4
    NG = KT // GK
    PV_CUT = [[0, 0, 2, 5], [5, 6, 8, 11], [11, 11, 13, 16]]
    with ExitStack() as ctx:
        sb = lambda n, shape, dt: ctx.enter_context(nc.sbuf_tensor(f"a_{n}", shape, dt))
        sem = lambda n: S.sem(f"a_{n}")
        Kh = [sb(f"keys_hi{i}", [P, TOK], FP16) for i in range(2)]
        Kl = [sb(f"keys_lo{i}", [P, TOK], FP16) for i in range(2)]
        Vh = [sb(f"values_hi{i}", [P, KT, HD], FP16) for i in range(2)]
        Vl = [sb(f"values_lo{i}", [P, KT, HD], FP16) for i in range(2)]
        Qh = [sb(f"queries_hi{i}", [P, TB], FP16) for i in range(2)]
        Ql = [sb(f"queries_lo{i}", [P, TB], FP16) for i in range(2)]
        vft = sb("values_by_feature", [P, TB], FP32)
        E = [sb(f"exponentials{i}", [P, TOK], FP32) for i in range(2)]
        Th = [sb(f"turned_hi{i}", [P, KT, TB], FP16) for i in range(2)]
        Tl = [sb(f"turned_lo{i}", [P, KT, TB], FP16) for i in range(2)]
        Oh = sb("out_hi", [P, TB], F32R)
        Ol = sb("out_lo", [P, TB], F32R)
        Wh = [sb(f"wqkv_hi{i}", [P, 3, KC, HD], F32R) for i in range(2)]
        Wl = [sb(f"wqkv_lo{i}", [P, 3, KC, HD], F32R) for i in range(2)]
        WOh = [sb(f"wo_hi{i}", [P, DM], F32R) for i in range(2)]
        WOl = [sb(f"wo_lo{i}", [P, DM], F32R) for i in range(2)]
        bias = [sb(f"bias{i}", [P, 3], FP32) for i in range(2)]
        NW = 3 * KC * HD
        codes = sb("codes", [P, NW + 3], FP32)
        scales = sb("scales", [P, NW], FP32)
        ocodes = sb("out_codes", [P, DM], FP32)
        oscales = sb("out_scales", [P, DM], FP32)
        bo_sb = sb("bo", [P, DM], FP32)
        halfmax = sb("halfmax", [P, TPB, 2], FP32)
        negmax = sb("negmax", [P, TPB], FP32)
        rowsum = [sb(f"rowsum{i}", [P, TPB, 2], FP32) for i in range(2)]
        rsum = sb("rowsum_both", [P, TPB], FP32)
        rinv = sb("rowsum_inverse", [P, TPB], FP32)

        scores = ctx.enter_context(nc.psum_tensor("a_scores", [P, TOK], FP32))
        turned = [ctx.enter_context(nc.psum_tensor(f"a_turned{i}", [P, GK, P], FP32)) for i in range(2)]
        obank = ctx.enter_context(nc.psum_tensor("a_out", [P, TB], FP32))
        mbank = ctx.enter_context(nc.psum_tensor("a_proj", [P, TB], FP32))

        scores_half, exps_turned, pv_done = sem("scores_half"), sem("exps_turned"), sem("pv_done")
        v_made, v_turned, q_made, k_made = sem("v_made"), sem("v_turned"), sem("q_made"), sem("k_made")
        ya_made, yb_made = sem("ya_made"), sem("yb_made")
        exps_ready, turned_hi, v_stored = sem("exps_ready"), sem("turned_hi"), sem("v_stored")
        v_hi, q_hi, k_hi, o_hi = sem("v_hi"), sem("q_hi"), sem("k_hi"), sem("o_hi")
        half_ready, negmax_ready, turned_lo = sem("half_ready"), sem("negmax_ready"), sem("turned_lo")
        v_lo, q_lo, k_lo, o_lo = sem("v_lo"), sem("q_lo"), sem("k_lo"), sem("o_lo")
        ya_added, yb_added, rinv_ready = sem("ya_added"), sem("yb_added"), sem("rinv_ready")
        rsum_ready = sem("rsum_ready")
        w_raw, wo_raw, bo_raw = sem("w_raw"), sem("wo_raw"), sem("bo_raw")
        wqkv_step, wo_step = sem("wqkv_step"), sem("wo_step")
        w_split, wo_split = sem("w_split"), sem("wo_split")
        block = ctx.enter_context(nc.Block())
        Q, K, V = range(3)
        SPP = 2 * NB
        GS = TPB * NG
        CREDIT = 2

        def at(m):
            m %= SPP
            return m // NB, m % NB, m % 2

        def turned_to(T, m, t, g):
            qq = at(m if t else m - 1)[2]
            before = (t - 1) % TPB
            return T[qq][:, g * GK:(g + 1) * GK, before * P:(before + 1) * P]

        @block.sync
        def _(sp):
            sp.dma_start(bo_sb[:, :], bo).then_inc(bo_raw, 16)

            def load_qkv(h):
                sp.dma_start(codes[:, :], wqkv_codes[bass.ds(h, 1), :, :].rearrange("h p n -> (h p) n")).then_inc(w_raw, 16)
                sp.dma_start(scales[:, :], wqkv_scales[bass.ds(h, 1), :, :].rearrange("h p n -> (h p) n")).then_inc(w_raw, 16)

            def load_o(h):
                sp.dma_start(ocodes[:, :], wo_codes[bass.ds(h, 1), :, :].rearrange("h p n -> (h p) n")).then_inc(wo_raw, 16)
                sp.dma_start(oscales[:, :], wo_scales[bass.ds(h, 1), :, :].rearrange("h p n -> (h p) n")).then_inc(wo_raw, 16)

            load_qkv(0)
            load_o(0)
            sp.wait_ge(w_split, 1)
            load_qkv(1)
            with sp.Fori(0, NH) as h:
                sp.wait_ge(wo_split, h + 1)
                load_o(h + 1)
                sp.wait_ge(w_split, h + 2)
                load_qkv(h + 2)

        @block.gpsimd
        def _(pool):
            flat = lambda w: w[:, :, :, :].rearrange("p m c f -> p (m c f)")

            def split_qkv(h, i):
                pool.wait_ge(w_raw, h * 32 + 32)
                pool.tensor_tensor(flat(Wh[i]), codes[:, 0:NW], scales[:, :], ALU.mult)
                pool.tensor_tensor(codes[:, 0:NW], codes[:, 0:NW], scales[:, :], ALU.mult).then_inc(wqkv_step, 1)
                pool.tensor_copy(bias[i][:, :], codes[:, NW:NW + 3])
                pool.wait_ge(wqkv_step, h + 1)
                pool.tensor_tensor(flat(Wl[i]), codes[:, 0:NW], fp(flat(Wh[i])), ALU.subtract).then_inc(w_split, 1)

            def split_o(h, i):
                pool.wait_ge(wo_raw, h * 32 + 32)
                pool.tensor_tensor(WOh[i][:, :], ocodes[:, :], oscales[:, :], ALU.mult)
                pool.tensor_tensor(ocodes[:, :], ocodes[:, :], oscales[:, :], ALU.mult).then_inc(wo_step, 1)
                pool.wait_ge(wo_step, h + 1)
                pool.tensor_tensor(WOl[i][:, :], ocodes[:, :], fp(WOh[i][:, :]), ALU.subtract).then_inc(wo_split, 1)

            split_qkv(0, 0)
            split_o(0, 0)
            split_qkv(1, 1)
            with pool.Fori(0, NH // 2) as pair:
                for hh in range(2):
                    h = pair * 2 + hh
                    pool.wait_ge(yb_added, pair * SPP + (hh * NB + 2))
                    split_o(h + 1, 1 - hh)
                    pool.wait_ge(q_lo, pair * SPP + (hh * NB + 4))
                    split_qkv(h + 2, hh)

        @block.tensor
        def _(pe):
            def project(what, i, b, made):
                for c in range(KC):
                    for k, (w, x) in enumerate(((Wh, S.xh), (Wh, S.xl), (Wl, S.xh))):
                        mm = pe.matmul(mbank[:, :], w[i][:, what, c, :], x[:, c, block_of(b)],
                                       start=(c == 0 and k == 0), stop=(c == KC - 1 and k == 2))
                mm.then_inc(made, 1)

            def turn_values():
                for i in range(TPB):
                    mm = pe.transpose(mbank[:, i * P:(i + 1) * P], vft[:, i * P:(i + 1) * P], S.ident[:, :])
                mm.then_inc(v_turned, 1)

            def score(t, half, hh, qq):
                for c in range(2 * half, 2 * half + 2):
                    for q, k in ((Qh, Kh), (Qh, Kl), (Ql, Kh)):
                        mm = pe.matmul(scores[:, block_of(c)], q[qq][:, t * P:(t + 1) * P],
                                       k[hh][:, block_of(c)], start=(q is Qh and k is Kh), stop=(q is Ql))
                mm.then_inc(scores_half, 1)

            def values(n, k0, k1, hv, qv):
                for kt in range(k0, k1):
                    if kt == k0 or kt % GK == 0:
                        pe.wait_ge(turned_lo, n * GS + (kt // GK + 1 + CREDIT))
                    for v, e in ((Vh, Th), (Vh, Tl), (Vl, Th)):
                        mm = pe.matmul(obank[:, :], v[hv][:, kt, :], e[qv][:, kt, :],
                                       start=(kt == 0 and v is Vh and e is Th), stop=(kt == KT - 1 and v is Vl))
                if k1 == KT:
                    mm.then_inc(pv_done, 1)

            def turn(n, t, g):
                if g % (NG // 2) == 0:
                    pe.wait_ge(exps_ready, n * (2 * TPB) + (2 * t + CREDIT - 1 + g // (NG // 2)))
                pe.wait_ge(turned_lo, n * GS + (t * NG + g - 1 + CREDIT))
                for i in range(GK):
                    kt = g * GK + i
                    mm = pe.transpose(turned[g % 2][:, i, :], E[(t + 1) % 2][:, kt * P:(kt + 1) * P], S.ident[:, :])
                mm.then_inc(exps_turned, 1)

            def outputs(bank, a, ho, made):
                for i in range(2):
                    cols = slice((a + i) * P, (a + i + 1) * P)
                    for k, (o, w) in enumerate(((Oh, WOh), (Oh, WOl), (Ol, WOh))):
                        mm = pe.matmul(bank[:, i * DM:(i + 1) * DM], o[:, cols], w[ho][:, :],
                                       start=(k == 0), stop=(k == 2))
                mm.then_inc(made, 1)

            pe.wait_ge(w_split, 1)
            for b in range(NB):
                if b:
                    pe.wait_ge(k_lo, b)
                project(V, 0, b, v_made)
                pe.wait_ge(v_stored, b + 1)
                turn_values()
                pe.wait_ge(v_lo, b + 1)
                project(K, 0, b, k_made)
            pe.wait_ge(k_lo, NB)
            project(Q, 0, 0, q_made)

            def step(n, pair, m):
                hh, b, qq = at(m)
                h1, _, q1 = at(m - 1)
                if b == 0:
                    pe.wait_ge(w_split, pair * 2 + (hh + 2))
                if b == 1:
                    pe.wait_ge(wo_split, pair * 2 + (hh + 1))
                pe.wait_ge(q_lo, n + 1)
                pe.wait_ge(k_lo, n + NB)
                for t in range(TPB):
                    for half in range(2):
                        pe.wait_ge(exps_ready, n * (2 * TPB) + (2 * t + CREDIT - 1 + half))
                        score(t, half, hh, qq)
                        if t == 3 and half == 1:
                            pe.wait_ge(q_lo, n + 2)
                            project(K, 1 - hh, b, k_made)
                        turn(n, t, half)
                    if t == 0:
                        pe.wait_ge(yb_added, n + 1)
                        project(V, 1 - hh, b, v_made)
                    if t == 1:
                        pe.wait_ge(v_stored, n + NB + 1)
                        turn_values()
                        values(n, *PV_CUT[t][0:2], h1, q1)
                    if t == 2:
                        pe.wait_ge(v_lo, n + NB + 1)
                        h2, b2, _ = at(m + 1)
                        project(Q, h2, b2, q_made)
                    turn(n, t, 2)
                    if t == 0:
                        pe.wait_ge(ya_added, n + 1)
                    if t < 3:
                        values(n, *PV_CUT[t][1:3], h1, q1)
                    else:
                        pe.wait_ge(o_lo, n + 1)
                        outputs(obank, 0, h1, ya_made)
                    turn(n, t, 3)
                    if t < 3:
                        values(n, *PV_CUT[t][2:4], h1, q1)
                    else:
                        pe.wait_ge(k_lo, n + NB + 1)
                        outputs(mbank, 2, h1, yb_made)

            with pe.Fori(0, NH // 2) as pair:
                for m in range(SPP):
                    step(pair * SPP + m, pair, m)

            N = NH * NB
            hh, _, qq = at(SPP - 1)
            for g in range(NG):
                turn(N, 0, g)
            pe.wait_ge(ya_added, N + 1)
            values(N, 0, KT, hh, qq)
            pe.wait_ge(o_lo, N + 1)
            outputs(obank, 0, hh, ya_made)
            pe.wait_ge(yb_added, N + 1)
            outputs(mbank, 2, hh, yb_made)

        @block.scalar
        def _(act):
            def store_values(i, count):
                act.wait_ge(v_made, count)
                act.activation(vft[:, :], mbank[:, :], ACT.Identity, bias=bias[i][:, V:V + 1]).then_inc(v_stored, 1)

            def values_hi(i, b, count):
                act.wait_ge(v_turned, count)
                act.activation(Vh[i][:, b * TPB:(b + 1) * TPB, :].rearrange("p t d -> p (t d)"), mbank[:, :],
                               ACT.Copy).then_inc(v_hi, 1)

            def keys_hi(i, b, count):
                act.wait_ge(k_made, count)
                act.activation(Kh[i][:, block_of(b)], mbank[:, :], ACT.Identity, bias=bias[i][:, K:K + 1]).then_inc(k_hi, 1)

            def queries_hi(i, q, count):
                act.wait_ge(q_made, count)
                act.activation(Qh[q][:, :], mbank[:, :], ACT.Identity, bias=bias[i][:, Q:Q + 1]).then_inc(q_hi, 1)

            def out_hi(count):
                act.wait_ge(pv_done, count)
                act.activation(Oh[:, :], obank[:, :], ACT.Copy).then_inc(o_hi, 1)

            def exponentials(t, half, qq):
                keys = slice(half * (TOK // 2), (half + 1) * (TOK // 2))
                act.activation(E[t % 2][:, keys], scores[:, keys], ACT.Exp, bias=negmax[:, t:t + 1], scale=SCALE,
                               accum_out=rowsum[qq][:, t, half:half + 1]).then_inc(exps_ready, 1)

            def evacuate(n, t, g, m):
                dst = turned_to(Th, m, t, g)
                act.wait_ge(exps_turned, n * GS + (t * NG + g + 1))
                act.activation(dst, turned[g % 2][:, :, :], ACT.Copy).then_inc(turned_hi, 1)

            for b in range(NB):
                store_values(0, b + 1)
                values_hi(0, b, b + 1)
                keys_hi(0, b, b + 1)
            queries_hi(0, 0, 1)

            def step(n, pair, m):
                hh, b, qq = at(m)
                h2, _, q2 = at(m + 1)
                for t in range(TPB):
                    if t == 3:
                        out_hi(n + 1)
                    evacuate(n, t, 0, m)
                    if t == 3:
                        keys_hi(1 - hh, b, n + NB + 1)
                    evacuate(n, t, 1, m)
                    act.wait_ge(negmax_ready, n * TPB + (t + 1))
                    exponentials(t, 0, qq)
                    if t == 1:
                        values_hi(1 - hh, b, n + NB + 1)
                    evacuate(n, t, 2, m)
                    if t == 0:
                        store_values(1 - hh, n + NB + 1)
                    if t == 2:
                        queries_hi(h2, q2, n + 2)
                    exponentials(t, 1, qq)
                    evacuate(n, t, 3, m)

            with act.Fori(0, NH // 2) as pair:
                for m in range(SPP):
                    step(pair * SPP + m, pair, m)
            for g in range(NG):
                evacuate(NH * NB, 0, g, 0)
            out_hi(NH * NB + 1)

        @block.vector
        def _(dve):
            def values_lo(i, b, count):
                tiles = lambda v: v[i][:, b * TPB:(b + 1) * TPB, :].rearrange("p t d -> p (t d)")
                dve.wait_ge(v_hi, count)
                dve.tensor_tensor(tiles(Vl), mbank[:, :], tiles(Vh), ALU.subtract).then_inc(v_lo, 1)

            def keys_lo(i, b, count):
                dve.wait_ge(k_hi, count)
                dve.scalar_tensor_tensor(out=Kl[i][:, block_of(b)], in0=mbank[:, :], scalar=bias[i][:, K:K + 1],
                                         in1=Kh[i][:, block_of(b)], op0=ALU.add, op1=ALU.subtract).then_inc(k_lo, 1)

            def queries_lo(i, q, count):
                dve.wait_ge(q_hi, count)
                dve.scalar_tensor_tensor(out=Ql[q][:, :], in0=mbank[:, :], scalar=bias[i][:, Q:Q + 1],
                                         in1=Qh[q][:, :], op0=ALU.add, op1=ALU.subtract).then_inc(q_lo, 1)

            def out_lo(count):
                dve.wait_ge(o_hi, count)
                dve.tensor_tensor(Ol[:, :], obank[:, :], fp(Oh[:, :]), ALU.subtract).then_inc(o_lo, 1)

            def invert_sums(q, count):
                dve.tensor_tensor(rsum[:, :], rowsum[q][:, :, 0], rowsum[q][:, :, 1], ALU.add).then_inc(rsum_ready, 1)
                dve.wait_ge(rsum_ready, count)
                dve.reciprocal(rinv[:, :], rsum[:, :]).then_inc(rinv_ready, 1)
                dve.wait_ge(rinv_ready, count)

            def maximum(n, t, half):
                dve.wait_ge(scores_half, n * (2 * TPB) + (2 * t + half + 1))
                dve.tensor_reduce(halfmax[:, t, half:half + 1], scores[:, half * 2 * TB:(half + 1) * 2 * TB],
                                  AX.X, ALU.max).then_inc(half_ready, 1)

            def evacuate(n, t, g, m):
                dve.wait_ge(turned_hi, n * GS + (t * NG + g + 1))
                dve.tensor_tensor(turned_to(Tl, m, t, g), turned[g % 2][:, :, :], turned_to(Th, m, t, g),
                                  ALU.subtract).then_inc(turned_lo, 1)

            def add(bank, b, a):
                for i in range(2):
                    t = b * TPB + a + i
                    ins = dve.scalar_tensor_tensor(out=S.x[:, t, :], in0=bank[:, i * DM:(i + 1) * DM],
                                                   scalar=rinv[:, a + i:a + i + 1], in1=S.x[:, t, :],
                                                   op0=ALU.mult, op1=ALU.add)
                return ins

            for z in (Th[1], Tl[1], Vh[1], Vl[1]):
                dve.memset(z[:, :, :].bitcast(FP32), 0.0)
            dve.memset(rowsum[1][:, :, :], 1.0)
            for z in (WOh[1], WOl[1]):
                ins = dve.memset(fp(z[:, :]), 0.0)
            ins.then_inc(turned_lo, CREDIT)
            dve.memset(E[1][:, :], 0.0).then_inc(exps_ready, CREDIT)
            dve.wait_ge(bo_raw, 16)
            for t in range(NT):
                ins = dve.tensor_tensor(S.x[:, t, :], S.x[:, t, :], bo_sb[:, :], ALU.add)
            ins.then_inc(ya_added, 1)
            dve.wait_ge(ya_added, 1)
            dve.sem_inc(yb_added, 1)

            for b in range(NB):
                values_lo(0, b, b + 1)
                keys_lo(0, b, b + 1)
            queries_lo(0, 0, 1)

            def step(n, pair, m):
                hh, b, qq = at(m)
                h2, _, q2 = at(m + 1)
                _, b1, q1 = at(m - 1)
                for t in range(TPB):
                    if t == 3:
                        out_lo(n + 1)
                    maximum(n, t, 0)
                    evacuate(n, t, 0, m)
                    maximum(n, t, 1)
                    dve.wait_ge(half_ready, n * (2 * TPB) + (2 * t + 2))
                    dve.tensor_scalar(negmax[:, t:t + 1], halfmax[:, t, 0:1], halfmax[:, t, 1:2], -SCALE,
                                      ALU.max, ALU.mult).then_inc(negmax_ready, 1)
                    if t == 3:
                        keys_lo(1 - hh, b, n + NB + 1)
                    evacuate(n, t, 1, m)
                    if t == 3:
                        invert_sums(q1, n + 1)
                    evacuate(n, t, 2, m)
                    if t == 1:
                        values_lo(1 - hh, b, n + NB + 1)
                    if t == 2:
                        queries_lo(h2, q2, n + 2)
                    if t == 3:
                        dve.wait_ge(ya_made, n + 1)
                        add(obank, b1, 0).then_inc(ya_added, 1)
                    evacuate(n, t, 3, m)
                    if t == 3:
                        dve.wait_ge(yb_made, n + 1)
                        add(mbank, b1, 2).then_inc(yb_added, 1)

            with dve.Fori(0, NH // 2) as pair:
                for m in range(SPP):
                    step(pair * SPP + m, pair, m)

            N = NH * NB
            for g in range(NG):
                evacuate(N, 0, g, 0)
            out_lo(N + 1)
            invert_sums(at(SPP - 1)[2], N + 1)
            dve.wait_ge(ya_made, N + 1)
            add(obank, NB - 1, 0).then_inc(ya_added, 1)
            dve.wait_ge(yb_made, N + 1)
            add(mbank, NB - 1, 2).then_inc(yb_added, 1)


NE = 32
TOPK = 8
PRIM = 4
SEC = TOPK - PRIM
THRESHOLD = 0.5
FF = 96
NF = NE * FF
JT = NF // P
NC = 3


def route_stage(nc, S, name, places, gate_w, sim_in, notdiag_in, iota_in, combine):
    with ExitStack() as ctx:
        sb = lambda n, shape, dt: ctx.enter_context(nc.sbuf_tensor(f"{places}_{n}", shape, dt))
        sem = lambda n: S.sem(f"{name}_{n}")
        gate = sb("gate", [P, KC, NE], FP32)
        gh, gl = sb("gate_hi", [P, KC, NE], F32R), sb("gate_lo", [P, KC, NE], F32R)
        sim = sb("similarity", [P, P], FP32)
        notdiag = sb("notdiag", [P, P], FP32)
        iota = sb("iota", [P, NE], FP32)
        expo = sb("expo", [P, NT, NE], FP32)
        shifted = sb("shifted", [P, NT, NE], FP32)
        top_logit = sb("top_logit", [P, NT], FP32)
        total = sb("total", [P, NT], FP32)
        top = sb("top", [P, NT, TOPK], FP32)
        index = sb("index", [P, NT, TOPK], U32)
        indexf = sb("indexf", [P, NT, TOPK], FP32)
        topsum = sb("topsum", [P, NT], FP32)
        hot = sb("onehot", [P, NT, TOPK, NE], FP32)
        hotT = sb("onehot_turned", [P, TOK], FP32)
        product = sb("product", [P, NT, TOPK, NE], FP32)
        cand = sb("candidates", [P, NT, SEC, PRIM], FP32)
        best = sb("best", [P, NT, SEC], FP32)
        isbest = sb("isbest", [P, NT, SEC, PRIM], FP32)
        seen = sb("seen", [P, NT, SEC], FP32)
        reroute = sb("reroute", [P, NT, SEC], FP32)
        moved = sb("moved", [P, NT, SEC], FP32)
        gained = sb("gained", [P, NT, PRIM], FP32)
        coef = sb("coef", [P, NT, TOPK], FP32)
        comb = sb("comb", [P, NT, NE], FP32)
        parts = sb("comb_parts", [P, NT, NC, NE], BF16)
        identb = sb("identity_bf16", [P, P], BF16)
        logits = ctx.enter_context(nc.psum_tensor(f"{places}_logits", [P, NT, NE], FP32))
        hot_ps = ctx.enter_context(nc.psum_tensor(f"{places}_hot_ps", [P, TB], FP32))
        rows = ctx.enter_context(nc.psum_tensor(f"{places}_sim_rows", [P, NT, SEC, NE], FP32))
        comb_ps = ctx.enter_context(nc.psum_tensor(f"{places}_comb_ps", [P, TOK], BF16))
        loaded = sem("loaded")
        step = sem("dve_step")
        gate_ready, logits_ready, shifted_ready, expo_ready = sem("gate_ready"), sem("logits_ready"), sem("shifted_ready"), sem("expo_ready")
        hot_ready, hot_turned, hot_stored, rows_ready = sem("hot_ready"), sem("hot_turned"), sem("hot_stored"), sem("rows_ready")
        parts_ready, comb_turned, comb_stored = sem("parts_ready"), sem("comb_turned"), sem("comb_stored")
        block = ctx.enter_context(nc.Block())

        @block.sync
        def _(sp):
            sp.dma_start(gate[:, :, :], gate_w).then_inc(loaded, 16)
            sp.dma_start(sim[:, :], sim_in).then_inc(loaded, 16)
            sp.dma_start(notdiag[:, :], notdiag_in).then_inc(loaded, 16)
            sp.dma_start(iota[:, :], iota_in).then_inc(loaded, 16)

        @block.tensor
        def _(pe):
            pe.wait_ge(gate_ready, 1)
            for t in range(NT):
                for c in range(KC):
                    for k, (x, g) in enumerate(((S.xh, gh), (S.xh, gl), (S.xl, gh))):
                        mm = pe.matmul(logits[:, t, :], x[:, c, t * P:(t + 1) * P], g[:, c, :],
                                       start=(c == 0 and k == 0), stop=(c == KC - 1 and k == 2))
            mm.then_inc(logits_ready, 1)
            pe.wait_ge(hot_ready, 1)
            for b in range(NB):
                if b:
                    pe.wait_ge(hot_stored, b)
                for i in range(TPB):
                    mm = pe.transpose(hot_ps[:, i * P:(i + 1) * P],
                                      hot[:, b * TPB + i, PRIM:TOPK, :].rearrange("p s e -> p (s e)"), S.ident[:, :])
                mm.then_inc(hot_turned, 1)
            pe.wait_ge(hot_stored, NB)
            for t in range(NT):
                mm = pe.matmul(rows[:, t, :, :].rearrange("p s e -> p (s e)"), hotT[:, t * P:(t + 1) * P], sim[:, :],
                               start=True, stop=True)
            mm.then_inc(rows_ready, 1)
            pe.wait_ge(parts_ready, 1)
            for t in range(NT):
                mm = pe.transpose(comb_ps[0:NC * NE, t * P:(t + 1) * P],
                                  parts[:, t, :, :].rearrange("p c e -> p (c e)"), identb[:, :])
            mm.then_inc(comb_turned, 1)

        @block.scalar
        def _(act):
            act.wait_ge(shifted_ready, 1)
            act.activation(expo[:, :, :], shifted[:, :, :], ACT.Exp).then_inc(expo_ready, 1)
            for b in range(NB):
                act.wait_ge(hot_turned, b + 1)
                act.activation(hotT[:, block_of(b)], hot_ps[:, :], ACT.Copy).then_inc(hot_stored, 1)
            act.wait_ge(comb_turned, 1)
            act.activation(combine[:, :], comb_ps[0:NC * NE, :], ACT.Copy).then_inc(comb_stored, 1)

        @block.vector
        def _(dve):
            done = 0

            def after(ins):
                nonlocal done
                done += 1
                ins.then_inc(step, 1)
                dve.wait_ge(step, done)

            def over(ap, n, dim):
                a = ap.unsqueeze(dim)
                shape = list(a.shape)
                shape[dim] = n
                return a.broadcast_to(shape)

            dve.tensor_copy(identb[:, :], S.ident[:, :])
            dve.wait_ge(loaded, 64)
            dve.tensor_copy(gh[:, :, :], gate[:, :, :]).then_inc(step, 1)
            dve.wait_ge(step, 1)
            dve.tensor_tensor(gl[:, :, :], gate[:, :, :], fp(gh[:, :, :]), ALU.subtract).then_inc(gate_ready, 1)
            done = 1
            after(dve.tensor_tensor(sim[:, :], sim[:, :], notdiag[:, :], ALU.mult))
            after(dve.tensor_tensor(sim[:, :], sim[:, :], S.ident[:, :], ALU.add))

            dve.wait_ge(logits_ready, 1)
            after(dve.tensor_reduce(top_logit[:, :], logits[:, :, :], AX.X, ALU.max))
            dve.tensor_tensor(shifted[:, :, :], logits[:, :, :], over(top_logit[:, :], NE, 2), ALU.subtract).then_inc(shifted_ready, 1)
            dve.wait_ge(expo_ready, 1)
            after(dve.tensor_reduce(total[:, :], expo[:, :, :], AX.X, ALU.add))
            after(dve.reciprocal(total[:, :], total[:, :]))
            after(dve.tensor_tensor(expo[:, :, :], expo[:, :, :], over(total[:, :], NE, 2), ALU.mult))

            for t in range(NT):
                ins = dve.max(top[:, t, :], expo[:, t, :])
            after(ins)
            for t in range(NT):
                ins = dve.max_index(index[:, t, :], top[:, t, :], expo[:, t, :])
            after(ins)
            after(dve.tensor_copy(indexf[:, :, :], index[:, :, :]))
            dve.tensor_tensor(hot[:, :, :, :].rearrange("p t k e -> p (t k) e"),
                              over(indexf[:, :, :].rearrange("p t k -> p (t k)"), NE, 2),
                              over(iota[:, :], NT * TOPK, 1), ALU.is_equal).then_inc(hot_ready, 1)
            after(dve.tensor_reduce(topsum[:, :], top[:, :, :], AX.X, ALU.add))
            after(dve.tensor_scalar(topsum[:, :], topsum[:, :], 1e-12, None, ALU.max))
            after(dve.reciprocal(topsum[:, :], topsum[:, :]))
            after(dve.tensor_tensor(coef[:, :, :], top[:, :, :], over(topsum[:, :], TOPK, 2), ALU.mult))

            dve.wait_ge(rows_ready, 1)
            flat = product[:, :, :, :].rearrange("p t k e -> p (t k e)")
            for s in range(SEC):
                part = flat[:, (s % 2) * NT * PRIM * NE:(s % 2 + 1) * NT * PRIM * NE].rearrange(
                    "p (t k e) -> p t k e", k=PRIM, e=NE)
                after(dve.tensor_tensor(part, over(rows[:, :, s, :], PRIM, 2), hot[:, :, 0:PRIM, :], ALU.mult))
                ins = dve.tensor_reduce(cand[:, :, s, :], part, AX.X, ALU.add)
            after(ins)
            after(dve.tensor_reduce(best[:, :, :], cand[:, :, :, :], AX.X, ALU.max))
            after(dve.tensor_tensor(isbest[:, :, :, :], cand[:, :, :, :], over(best[:, :, :], PRIM, 3), ALU.is_equal))
            after(dve.tensor_copy(seen[:, :, :], isbest[:, :, :, 0]))
            for q in range(1, PRIM):
                after(dve.tensor_tensor(isbest[:, :, :, q], isbest[:, :, :, q], seen[:, :, :], ALU.is_gt))
                after(dve.tensor_tensor(seen[:, :, :], isbest[:, :, :, q], seen[:, :, :], ALU.max))
            after(dve.tensor_scalar(reroute[:, :, :], best[:, :, :], THRESHOLD, None, ALU.is_ge))
            after(dve.tensor_tensor(moved[:, :, :], coef[:, :, PRIM:TOPK], reroute[:, :, :], ALU.mult))
            after(dve.tensor_tensor(coef[:, :, PRIM:TOPK], coef[:, :, PRIM:TOPK], moved[:, :, :], ALU.subtract))
            after(dve.tensor_tensor(isbest[:, :, :, :], isbest[:, :, :, :], over(moved[:, :, :], PRIM, 3), ALU.mult))
            after(dve.tensor_reduce(gained[:, :, :], isbest[:, :, :, :].rearrange("p t s q -> p t q s"), AX.X, ALU.add))
            after(dve.tensor_tensor(coef[:, :, 0:PRIM], coef[:, :, 0:PRIM], gained[:, :, :], ALU.add))
            after(dve.tensor_tensor(product[:, :, :, :].rearrange("p t k e -> p (t k) e"),
                                    hot[:, :, :, :].rearrange("p t k e -> p (t k) e"),
                                    over(coef[:, :, :].rearrange("p t k -> p (t k)"), NE, 2), ALU.mult))
            after(dve.tensor_reduce(comb[:, :, :], product[:, :, :, :].rearrange("p t k e -> p t e k"), AX.X, ALU.add))
            for c in range(NC):
                ins = dve.tensor_copy(parts[:, :, c, :], comb[:, :, :])
                if c < NC - 1:
                    after(ins)
                    after(dve.tensor_tensor(comb[:, :, :], comb[:, :, :], parts[:, :, c, :], ALU.subtract))
            ins.then_inc(parts_ready, 1)


def experts_stage(nc, S, name, places, w_in, sel_in, combine):
    NWJ = 2 * KC * P + DM
    with ExitStack() as ctx:
        sb = lambda n, shape, dt: ctx.enter_context(nc.sbuf_tensor(f"{places}_{n}", shape, dt))
        sem = lambda n: S.sem(f"{name}_{n}")
        ps = lambda n, shape: ctx.enter_context(nc.psum_tensor(f"{places}_{n}", shape, FP32))
        raw = [sb(f"raw{i}", [P, NWJ], FP32) for i in range(2)]
        Wh = [sb(f"w_hi{i}", [P, NWJ], F32R) for i in range(2)]
        Wl = [sb(f"w_lo{i}", [P, NWJ], F32R) for i in range(2)]
        zeros = sb("zeros", [P, KC * P], FP32)
        sel = [sb(f"select{i}", [NC * NE, P], BF16) for i in range(2)]
        a = [sb(f"silu{i}", [P, TB], FP32) for i in range(2)]
        au = [sb(f"silu_up{i}", [P, TB], FP32) for i in range(2)]
        h = [sb(f"inner{i}", [P, TB], FP32) for i in range(2)]
        Hh = [sb(f"inner_hi{i}", [P, TB], F32R) for i in range(2)]
        Hl = [sb(f"inner_lo{i}", [P, TB], F32R) for i in range(2)]
        gate_ps = [ps(f"gate{i}", [P, TB]) for i in range(2)]
        up_ps = [ps(f"up{i}", [P, TB]) for i in range(2)]
        comb_ps = [ps(f"weight{i}", [P, TB]) for i in range(2)]
        out_ps = ps("out", [P, TPB, DM])
        raw_loaded = [sem(f"raw_loaded{i}") for i in range(2)]
        sel_loaded = [sem(f"select_loaded{i}") for i in range(2)]
        piece_hi, w_split, inner_lo = sem("piece_hi"), sem("w_split"), sem("inner_lo")
        gate_made, up_made, comb_made, out_made = sem("gate_made"), sem("up_made"), sem("weight_made"), sem("out_made")
        silu_ready, inner_hi = sem("silu_ready"), sem("inner_hi")
        up_used, inner_ready, out_added = sem("up_used"), sem("inner_ready"), sem("out_added")
        block = ctx.enter_context(nc.Block())
        SPL = 2 * NB
        LOOPS = JT // 2
        PIECES = 3
        DOWN = slice(2 * KC * P, NWJ)

        @block.sync
        def _(sp):
            def load(j, i):
                sp.dma_start(raw[i][:, :], w_in[bass.ds(j, 1), :, :].rearrange("j p n -> (j p) n")).then_inc(raw_loaded[i], 16)

            def load_sel(j, i):
                sp.dma_start(sel[i][:, :], sel_in[bass.ds(j, 1), :, :].rearrange("j p n -> (j p) n")).then_inc(sel_loaded[i], 16)

            for i in range(2):
                load(i, i)
                load_sel(i, i)
            with sp.Fori(0, LOOPS - 1) as l:
                for i in range(2):
                    sp.wait_ge(w_split, l * (2 * PIECES) + PIECES * (i + 1))
                    load(l * 2 + (i + 2), i)
                    sp.wait_ge(comb_made, l * SPL + NB * (i + 1))
                    load_sel(l * 2 + (i + 2), i)

        @block.gpsimd
        def _(pool):
            def split(piece, l, i):
                cols = slice(piece * KC * P, (piece + 1) * KC * P)
                count = l * (2 * PIECES) + (PIECES * i + piece + 1)
                if piece == 0:
                    pool.wait_ge(raw_loaded[i], l * 16 + 16)
                pool.tensor_tensor(Wh[i][:, cols], raw[i][:, cols], zeros[:, :], ALU.add).then_inc(piece_hi, 1)
                pool.wait_ge(piece_hi, count)
                pool.tensor_tensor(Wl[i][:, cols], raw[i][:, cols], fp(Wh[i][:, cols]), ALU.subtract).then_inc(w_split, 1)

            def low(n, q):
                pool.wait_ge(inner_hi, n + 1)
                pool.tensor_tensor(Hl[q][:, :], h[q][:, :], fp(Hh[q][:, :]), ALU.subtract).then_inc(inner_lo, 1)

            pool.memset(zeros[:, :], 0.0)
            for z in (Hh[1], Hl[1], Wh[1], Wl[1]):
                ins = pool.memset(fp(z[:, :]), 0.0)
            ins.then_inc(inner_lo, 1)
            pool.wait_ge(inner_lo, 1)
            for piece in range(PIECES):
                split(piece, 0, 0)

            def round_(l, last):
                for m in range(SPL):
                    i, b = m // NB, m % NB
                    low(l * SPL + m, m % 2)
                    if b < PIECES and not (last and i == 1):
                        if b == 0:
                            pool.wait_ge(out_made, l * SPL + (m + 1))
                        split(b, l + i, 1 - i)

            with pool.Fori(0, LOOPS - 1) as l:
                round_(l, False)
            round_(LOOPS - 1, True)

        @block.tensor
        def _(pe):
            def inner(n, l, m):
                i, b, q = m // NB, m % NB, m % 2
                if b == 0:
                    pe.wait_ge(w_split, l * (2 * PIECES) + (PIECES * i + 2))
                    pe.wait_ge(sel_loaded[i], l * 16 + 16)
                for half, bank, made in ((0, gate_ps, gate_made), (1, up_ps, up_made)):
                    for c in range(KC):
                        cols = slice((half * KC + c) * P, (half * KC + c + 1) * P)
                        for k, (w, x) in enumerate(((Wh, S.xh), (Wh, S.xl), (Wl, S.xh))):
                            mm = pe.matmul(bank[q][:, :], w[i][:, cols], x[:, c, block_of(b)],
                                           start=(c == 0 and k == 0), stop=(c == KC - 1 and k == 2))
                    mm.then_inc(made, 1)
                pe.matmul(comb_ps[q][:, :], sel[i][:, :], combine[:, block_of(b)], start=True, stop=True).then_inc(comb_made, 1)

            def outputs(n, m):
                m1 = (m - 1) % SPL
                i, q = m1 // NB, m1 % 2
                pe.wait_ge(inner_lo, n + 1)
                pe.wait_ge(out_added, n + 1)
                for t in range(TPB):
                    cols = slice(t * P, (t + 1) * P)
                    for k, (g, w) in enumerate(((Hh, Wh), (Hh, Wl), (Hl, Wh))):
                        mm = pe.matmul(out_ps[:, t, :], g[q][:, cols], w[i][:, DOWN], start=(k == 0), stop=(k == 2))
                mm.then_inc(out_made, 1)

            with pe.Fori(0, LOOPS) as l:
                for m in range(SPL):
                    n = l * SPL + m
                    inner(n, l, m)
                    if m % NB == 1:
                        pe.wait_ge(w_split, l * (2 * PIECES) + PIECES * (m // NB + 1))
                    outputs(n, m)
            outputs(LOOPS * SPL, 0)

        @block.scalar
        def _(act):
            with act.Fori(0, LOOPS) as l:
                for m in range(SPL):
                    n, q = l * SPL + m, m % 2
                    act.wait_ge(gate_made, n + 1)
                    act.activation(a[q][:, :], gate_ps[q][:, :], ACT.Silu).then_inc(silu_ready, 1)
                    act.wait_ge(inner_ready, n + 1)
                    act.activation(Hh[q][:, :], h[q][:, :], ACT.Copy).then_inc(inner_hi, 1)

        @block.vector
        def _(dve):
            def add(n, m):
                b = (m - 1) % NB
                dve.wait_ge(out_made, n + 1)
                x = S.x[:, b * TPB:(b + 1) * TPB, :]
                dve.tensor_tensor(x, x, out_ps[:, :, :], ALU.add).then_inc(out_added, 1)

            dve.sem_inc(out_added, 1)
            with dve.Fori(0, LOOPS) as l:
                for m in range(SPL):
                    n, q = l * SPL + m, m % 2
                    dve.wait_ge(silu_ready, n + 1)
                    dve.wait_ge(up_made, n + 1)
                    dve.tensor_tensor(au[q][:, :], a[q][:, :], up_ps[q][:, :], ALU.mult).then_inc(up_used, 1)
                    dve.wait_ge(up_used, n + 1)
                    dve.wait_ge(comb_made, n + 1)
                    dve.tensor_tensor(h[q][:, :], au[q][:, :], comb_ps[q][:, :], ALU.mult).then_inc(inner_ready, 1)
                    add(n, m)
            add(LOOPS * SPL, 0)


LH, LKV, LD = 16, 8, 16
LF = LD
LE = LF // 2
TWO_PI_HI = 6.28125
TWO_PI_LO = 2 * math.pi - TWO_PI_HI
ROUND = 1.5 * 2.0 ** 23


def linear_stage(nc, S, w_in, bias_in, bv_in, wo_in, bo_in, cos_in, sin_in, rand_in, ones_in, scratch):
    HT = 8
    NU = LH // HT + LKV // HT
    NHD = NU * HT
    COLS = LE + 1
    MID = HT * LE
    OUT = 7
    VT = 3
    with ExitStack() as ctx:
        sb = lambda n, shape, dt=FP32: ctx.enter_context(nc.sbuf_tensor(f"l_{n}", shape, dt))
        sem = lambda n: S.sem(f"l_{n}")
        ps = lambda n, shape: ctx.enter_context(nc.psum_tensor(f"l_{n}", shape, FP32))

        w = sb("w", [P, KC, OUT, P])
        wh, wl = sb("w_hi", [P, KC, OUT, P], F32R), sb("w_lo", [P, KC, OUT, P], F32R)
        wo = sb("wo", [P, KC, DM])
        woh, wol = sb("wo_hi", [P, KC, DM], F32R), sb("wo_lo", [P, KC, DM], F32R)
        bias = sb("bias", [P, OUT])
        bv = sb("bv", [P, P])
        bo = sb("bo", [P, DM])
        tables = sb("tables", [P, 2 * TOK])
        cos, sin = tables[:, 0:TOK], tables[:, TOK:2 * TOK]
        rand = sb("rand", [P, MID])
        ones = sb("ones", [P, HT])
        by_cos = [sb(f"by_cos{i}", [P, TB]) for i in range(2)]
        by_sin = [sb(f"by_sin{i}", [P, TB]) for i in range(2)]
        rot = [sb(f"rotated{i}", [P, TB]) for i in range(2)]
        square = [sb(f"square{i}", [P, TB]) for i in range(2)]
        proj = sb("projected", [P, NT, NHD * LE])
        norm = sb("square_norm", [P, NT, NHD])
        v = sb("values", [P, NT, LKV * LD])
        sd, r2 = sb("norm", [P, NT, NHD]), sb("newton", [P, NT, NHD])
        turns = sb("turns", [P, NT, NHD * LE])
        feat = sb("features", [P, NT, NHD, 2, LE])
        half_pi = sb("half_pi", [P, 1])
        att = [sb(f"pair_sums{i}", [P, LH, LKV]) for i in range(2)]
        pairs = [sb(f"pair_products{i}", [P, LF, LH, LKV]) for i in range(2)]
        outs = sb("out_products", [P, LH, LD, LKV])
        o = feat[:, :, :, :, :].rearrange("p t h s e -> p t (h s e)")[:, :, 0:LH * LD]
        z = tables[:, :].rearrange("p (i h d) -> p i h d", i=LD, h=LH)
        zz = feat[:, :, :, :, :].rearrange("p t h s e -> p (t h s e)")[:, 0:LH * LD * LD].rearrange(
            "p (h n) -> p h n", h=LH)
        zh = [sb(f"out_hi{i}", [P, KC, P], F32R) for i in range(2)]
        zl = [sb(f"out_lo{i}", [P, KC, P], F32R) for i in range(2)]

        straight = [ps(f"straight{i}", [P, TB]) for i in range(2)]
        swapped = [ps(f"swapped{i}", [P, TB]) for i in range(2)]
        mid = ps("mid", [P, 2, TB])
        v_ps = ps("v", [P, 2, 2 * P])
        att_ps = ps("pairs", [P, LH, LKV])
        zt = swapped
        zs = straight
        SUM_AFTER = 7

        loaded, w_loaded, wo_loaded = sem("loaded"), sem("w_loaded"), sem("wo_loaded")
        w_ready, wo_hi, wo_ready, w_hi = sem("w_ready"), sem("wo_hi"), sem("wo_ready"), sem("w_hi")
        made, turned, rotated, squared = sem("made"), sem("cos_sin_used"), sem("rotated"), sem("squared")
        mid_made, mid_stored, v_made, v_stored = sem("mid_made"), sem("mid_stored"), sem("v_made"), sem("v_stored")
        step, norm_ready, sd_ready, angle_ready, abs_ready, feat_ready = (
            sem("step"), sem("norm_ready"), sem("sd_ready"), sem("angle_ready"), sem("abs_ready"), sem("feat_ready"))
        pairs_ready, att_made, att_stored, outs_ready, o_ready = sem("pairs_ready"), sem("att_made"), sem("att_stored"), sem("outs_ready"), sem("o_ready")
        stored, back, ordered = sem("stored"), sem("back"), sem("ordered")
        z_turned, z_hi, z_lo, y_made, y_added = sem("z_turned"), sem("z_hi"), sem("z_lo"), sem("y_made"), sem("y_added")
        block = ctx.enter_context(nc.Block())
        units = [(b, u) for b in range(NB) for u in range(NU)]

        def order(copy, h0):
            return copy(zz[:, h0:h0 + LH // 2, :].rearrange("p h (i d) -> p h i d", d=LD),
                        z[:, :, h0:h0 + LH // 2, :].rearrange("p i h d -> p h i d"))

        @block.sync
        def _(sp):
            sp.dma_start(w[:, :, :, :], w_in).then_inc(w_loaded, 16)
            for dst, src in ((bias[:, :], bias_in), (bv[:, :], bv_in), (bo[:, :], bo_in), (cos[:, :], cos_in),
                             (sin[:, :], sin_in), (rand[:, :], rand_in), (ones[:, :], ones_in)):
                sp.dma_start(dst, src).then_inc(loaded, 16)
            sp.dma_start(wo[:, :, :], wo_in).then_inc(wo_loaded, 16)
            for b in range(NB):
                sp.wait_ge(o_ready, TPB * (b + 1))
                sp.dma_start(scratch[b * TB:(b + 1) * TB, :].rearrange("(t p) n -> p t n", p=P),
                             o[:, b * TPB:(b + 1) * TPB, :]).then_inc(stored, 16)
            sp.wait_ge(stored, 16 * NB)
            sp.dma_start(z[:, :, :, :].rearrange("p i h d -> p (i h d)"),
                         scratch.rearrange("(j i) n -> j (i n)", i=LD)).then_inc(back, 16)
            sp.wait_ge(back, 16)

        @block.gpsimd
        def _(pool):
            flat = lambda t: t[:, :, :].rearrange("p c n -> p (c n)")
            pool.wait_ge(wo_loaded, 16)
            pool.tensor_copy(flat(woh), flat(wo)).then_inc(wo_hi, 1)
            pool.wait_ge(wo_hi, 1)
            pool.tensor_tensor(flat(wol), flat(wo), fp(flat(woh)), ALU.subtract).then_inc(wo_ready, 1)
            def multiply(t):
                pool.wait_ge(feat_ready, t // TPB + 1)
                if t >= 2:
                    pool.wait_ge(att_made, t - 1)
                f = feat[:, t, :, :, :].rearrange("p h s e -> p h (s e)")
                pool.tensor_tensor(pairs[t % 2][:, :, :, :].rearrange("p f h k -> p h k f"),
                                   f[:, 0:LH, :].unsqueeze(2).broadcast_to([P, LH, LKV, LF]),
                                   f[:, LH:NHD, :].unsqueeze(1).broadcast_to([P, LH, LKV, LF]),
                                   ALU.mult).then_inc(pairs_ready, 1)

            for n in range(len(units)):
                pool.wait_ge(turned, n + 1)
                if n >= 2:
                    pool.wait_ge(mid_made, n - 1)
                pool.tensor_tensor(rot[n % 2][:, :], by_cos[n % 2][:, :], by_sin[n % 2][:, :], ALU.add).then_inc(rotated, 1)
                if n >= SUM_AFTER - 1:
                    multiply(n - (SUM_AFTER - 1))
            for t in range(len(units) - (SUM_AFTER - 1), NT):
                multiply(t)

        @block.tensor
        def _(pe):
            def project(bank, tile_, b):
                for c in range(KC):
                    for k, (a, x) in enumerate(((wh, S.xh), (wh, S.xl), (wl, S.xh))):
                        mm = pe.matmul(bank, a[:, c, tile_, :], x[:, c, block_of(b)],
                                       start=(c == 0 and k == 0), stop=(c == KC - 1 and k == 2))
                return mm

            def middle(n):
                b, u = units[n]
                pe.wait_ge(rotated, n + 1)
                if u == 0 and b:
                    pe.wait_ge(mid_stored, b)
                for t in range(TPB):
                    at = mid[:, t // 2, (t % 2) * NU * HT * COLS + u * HT * COLS:]
                    pe.matmul(at[:, 0:MID], rot[n % 2][:, t * P:(t + 1) * P], rand[:, :], start=True, stop=True)
                pe.wait_ge(squared, n + 1)
                for t in range(TPB):
                    at = mid[:, t // 2, (t % 2) * NU * HT * COLS + u * HT * COLS:]
                    mm = pe.matmul(at[:, MID:MID + HT], square[n % 2][:, t * P:(t + 1) * P], ones[:, :], start=True, stop=True)
                mm.then_inc(mid_made, 1)

            def add_pairs(t):
                pe.wait_ge(pairs_ready, t + 1)
                if t:
                    pe.wait_ge(att_stored, t)
                for f in range(LF):
                    mm = pe.matmul(att_ps[:, :, :].rearrange("p h k -> p (h k)"), S.ident[:, :],
                                   pairs[t % 2][:, f, :, :].rearrange("p h k -> p (h k)"), start=(f == 0), stop=(f == LF - 1))
                mm.then_inc(att_made, 1)

            pe.wait_ge(w_ready, 1)
            pe.wait_ge(loaded, 16 * 7)
            for n, (b, u) in enumerate(units):
                if n >= 2:
                    pe.wait_ge(turned, n - 1)
                project(straight[n % 2][:, :], u, b)
                project(swapped[n % 2][:, :], VT + 1 + u, b).then_inc(made, 1)
                if u < 2:
                    if b or u:
                        pe.wait_ge(v_stored, 2 * b + u)
                    for t in range(2):
                        cols = slice((b * TPB + 2 * u + t) * P, (b * TPB + 2 * u + t + 1) * P)
                        for c in range(KC):
                            for k, (x, a) in enumerate(((S.xh, wh), (S.xh, wl), (S.xl, wh))):
                                mm = pe.matmul(v_ps[:, t, :], x[:, c, cols], a[:, c, VT:VT + 2, :].rearrange("p o n -> p (o n)"),
                                               start=(c == 0 and k == 0), stop=(c == KC - 1 and k == 2))
                    mm.then_inc(v_made, 1)
                if n:
                    middle(n - 1)
                if n >= SUM_AFTER:
                    add_pairs(n - SUM_AFTER)
            middle(len(units) - 1)
            for t in range(len(units) - SUM_AFTER, NT):
                add_pairs(t)

            pe.wait_ge(ordered, 2)
            pe.wait_ge(wo_ready, 1)
            pe.wait_ge(v_stored, 2 * NB)

            def turn_head(h):
                if h >= 2:
                    pe.wait_ge(z_lo, h - 1)
                for c in range(KC):
                    mm = pe.transpose(zt[h % 2][:, c * P:(c + 1) * P], zz[:, h, c * P:(c + 1) * P], S.ident[:, :])
                mm.then_inc(z_turned, 1)

            turn_head(0)
            for h in range(LH):
                if h + 1 < LH:
                    turn_head(h + 1)
                pe.wait_ge(z_lo, h + 1)
                if h >= 2:
                    pe.wait_ge(y_added, h - 1)
                for c in range(KC):
                    for k, (a, ww) in enumerate(((zh, woh), (zh, wol), (zl, woh))):
                        mm = pe.matmul(zs[h % 2][:, 0:DM], a[h % 2][:, c, :], ww[:, c, :],
                                       start=(c == 0 and k == 0), stop=(c == KC - 1 and k == 2))
                mm.then_inc(y_made, 1)

        @block.scalar
        def _(act):
            flat = lambda t: t[:, :, :, :].rearrange("p c o n -> p (c o n)")
            act.wait_ge(w_loaded, 16)
            act.activation(flat(wh), flat(w), ACT.Copy).then_inc(w_hi, 1)
            def store_middle(b):
                act.wait_ge(mid_made, NU * (b + 1))
                for bank in range(2):
                    m = mid[:, bank, 0:2 * NU * HT * COLS].rearrange("p (t u n) -> p t u n", t=2, u=NU)
                    t = b * TPB + 2 * bank
                    act.activation(proj[:, t:t + 2, :].rearrange("p t (u n) -> p t u n", u=NU), m[:, :, :, 0:MID], ACT.Copy)
                    ins = act.activation(norm[:, t:t + 2, :].rearrange("p t (u n) -> p t u n", u=NU), m[:, :, :, MID:], ACT.Copy)
                ins.then_inc(mid_stored, 1)

            def norms(b):
                tiles = slice(b * TPB, (b + 1) * TPB)
                act.wait_ge(norm_ready, b + 1)
                act.activation(sd[:, tiles, :], norm[:, tiles, :], ACT.Sqrt).then_inc(sd_ready, 1)

            def features(b):
                tiles = slice(b * TPB, (b + 1) * TPB)
                act.wait_ge(angle_ready, b + 1)
                heads = lambda x: x[:, tiles, :].rearrange("p t (h e) -> p (t h) e", e=LE)
                place = lambda s: feat[:, tiles, :, s, :].rearrange("p t h e -> p (t h) e")
                act.activation(turns[:, tiles, :], proj[:, tiles, :], ACT.Abs).then_inc(abs_ready, 1)
                act.activation(place(0), heads(proj), ACT.Sin)
                act.wait_ge(abs_ready, b + 1)
                act.activation(place(1), heads(turns), ACT.Sin, scale=-1.0, bias=half_pi[:, :]).then_inc(feat_ready, 1)

            def store_sums(t):
                act.wait_ge(att_made, t + 1)
                if t >= 2:
                    act.wait_ge(outs_ready, t - 1)
                act.activation(att[t % 2][:, :, :], att_ps[:, :, :], ACT.Copy).then_inc(att_stored, 1)

            for n, (b, u) in enumerate(units):
                act.wait_ge(rotated, n + 1)
                if n >= 2:
                    act.wait_ge(mid_made, n - 1)
                act.activation(square[n % 2][:, :], rot[n % 2][:, :], ACT.Square).then_inc(squared, 1)
                if u == 0 and b:
                    norms(b - 1)
                if u == 2 and b:
                    features(b - 1)
                if u == NU - 1:
                    store_middle(b)
                if n >= SUM_AFTER:
                    store_sums(n - SUM_AFTER)
            norms(NB - 1)
            features(NB - 1)
            for t in range(len(units) - SUM_AFTER, NT):
                store_sums(t)
            act.wait_ge(back, 16)
            act.wait_ge(att_made, NT)
            order(lambda out, in_: act.activation(out, in_, ACT.Copy), 0).then_inc(ordered, 1)
            for h in range(LH):
                act.wait_ge(z_turned, h + 1)
                if h >= 2:
                    act.wait_ge(y_made, h - 1)
                act.activation(zh[h % 2][:, :, :].rearrange("p c n -> p (c n)"), zt[h % 2][:, 0:DM], ACT.Copy).then_inc(z_hi, 1)

        @block.vector
        def _(dve):
            done = 0

            def after(ins):
                nonlocal done
                done += 1
                ins.then_inc(step, 1)
                dve.wait_ge(step, done)

            flat = lambda t: t[:, :, :, :].rearrange("p c o n -> p (c o n)")
            dve.wait_ge(w_hi, 1)
            dve.tensor_tensor(flat(wl), flat(w), fp(flat(wh)), ALU.subtract).then_inc(w_ready, 1)
            dve.memset(half_pi[:, :], math.pi / 2)
            dve.wait_ge(loaded, 16 * 7)
            VS = (LH // LKV) / LF
            after(dve.tensor_scalar(bv[:, :], bv[:, :], VS, None, ALU.mult))

            def of_block(b):
                return (a[:, b * TPB:(b + 1) * TPB, :] for a in (sd, r2, norm, turns, proj))

            def limit_norms(b):
                sd_, r2_, norm_, tn, p = of_block(b)
                dve.wait_ge(mid_stored, b + 1)
                dve.tensor_scalar(norm_, norm_, 1e-12, None, ALU.max).then_inc(norm_ready, 1)

            def normalize(b):
                sd_, r2_, norm_, tn, p = of_block(b)
                dve.wait_ge(sd_ready, b + 1)
                after(dve.reciprocal(sd_, sd_))
                after(dve.tensor_tensor(r2_, sd_, sd_, ALU.mult))
                after(dve.tensor_tensor(r2_, r2_, norm_, ALU.mult))
                after(dve.tensor_scalar(r2_, r2_, -0.5, 1.5, ALU.mult, ALU.add))
                after(dve.tensor_tensor(sd_, sd_, r2_, ALU.mult))
                heads = p.rearrange("p t (h e) -> p (t h) e", e=LE)
                after(dve.tensor_tensor(heads, heads, sd_.rearrange("p t h -> p (t h)").unsqueeze(2).broadcast_to(
                    [P, TPB * NHD, LE]), ALU.mult))

            def angles(b):
                sd_, r2_, norm_, tn, p = of_block(b)
                after(dve.tensor_scalar(tn, p, 1 / (2 * math.pi), ROUND, ALU.mult, ALU.add))
                after(dve.tensor_scalar(tn, tn, ROUND, None, ALU.subtract))
                after(dve.scalar_tensor_tensor(out=p, in0=tn, scalar=-TWO_PI_HI, in1=p, op0=ALU.mult, op1=ALU.add))
                after(dve.scalar_tensor_tensor(out=p, in0=tn, scalar=-TWO_PI_LO, in1=p, op0=ALU.mult, op1=ALU.add))
                PI = float(np.nextafter(np.float32(math.pi), np.float32(0)))
                dve.tensor_scalar(p, p, PI, -PI, ALU.min, ALU.max).then_inc(angle_ready, 1)

            def outputs(t):
                dve.wait_ge(att_stored, t + 1)
                if t:
                    dve.wait_ge(o_ready, t)
                dve.tensor_tensor(outs[:, :, :, :], att[t % 2][:, :, :].unsqueeze(2).broadcast_to([P, LH, LD, LKV]),
                                  v[:, t, :].rearrange("p (k d) -> p d k", d=LD).unsqueeze(1).broadcast_to([P, LH, LD, LKV]),
                                  ALU.mult).then_inc(outs_ready, 1)
                dve.wait_ge(outs_ready, t + 1)
                dve.tensor_reduce(o[:, t, :].rearrange("p (h d) -> p h d", d=LD), outs[:, :, :, :], AX.X, ALU.add).then_inc(o_ready, 1)

            for n, (b, u) in enumerate(units):
                i = n % 2
                dve.wait_ge(made, n + 1)
                if n >= 2:
                    dve.wait_ge(rotated, n - 1)
                dve.scalar_tensor_tensor(out=by_cos[i][:, :], in0=straight[i][:, :], scalar=bias[:, u:u + 1],
                                         in1=cos[:, block_of(b)], op0=ALU.add, op1=ALU.mult)
                dve.scalar_tensor_tensor(out=by_sin[i][:, :], in0=swapped[i][:, :], scalar=bias[:, VT + 1 + u:VT + 2 + u],
                                         in1=sin[:, block_of(b)], op0=ALU.add, op1=ALU.mult).then_inc(turned, 1)
                if u < 2:
                    t = b * TPB + 2 * u
                    dve.wait_ge(v_made, 2 * b + u + 1)
                    dve.scalar_tensor_tensor(out=v[:, t:t + 2, :], in0=v_ps[:, :, 0:P], scalar=VS,
                                             in1=bv[:, :].unsqueeze(1).broadcast_to([P, 2, P]),
                                             op0=ALU.mult, op1=ALU.add).then_inc(v_stored, 1)
                if b:
                    (limit_norms, normalize, angles)[u](b - 1)
                if n >= SUM_AFTER + 1:
                    outputs(n - (SUM_AFTER + 1))
            for part in (limit_norms, normalize, angles):
                part(NB - 1)
            for t in range(len(units) - (SUM_AFTER + 1), NT):
                outputs(t)
            for t in range(NT):
                ins = dve.tensor_tensor(S.x[:, t, :], S.x[:, t, :], bo[:, :], ALU.add)
            dve.wait_ge(back, 16)
            order(dve.tensor_copy, LH // 2).then_inc(ordered, 1)
            for h in range(LH):
                dve.wait_ge(z_hi, h + 1)
                one = lambda z_: z_[h % 2][:, :, :].rearrange("p c n -> p (c n)")
                dve.tensor_tensor(one(zl), zt[h % 2][:, 0:DM], fp(one(zh)), ALU.subtract).then_inc(z_lo, 1)
                if h >= 1:
                    dve.wait_ge(y_made, h)
                    dve.tensor_tensor(S.x[:, h - 1, :], S.x[:, h - 1, :], zs[(h - 1) % 2][:, 0:DM], ALU.add).then_inc(y_added, 1)
            dve.wait_ge(y_made, LH)
            dve.tensor_tensor(S.x[:, LH - 1, :], S.x[:, LH - 1, :], zs[(LH - 1) % 2][:, 0:DM], ALU.add).then_inc(y_added, 1)


def store_stage(nc, S, out):
    with ExitStack() as ctx:
        stored = S.sem("stored")
        block = ctx.enter_context(nc.Block())

        @block.sync
        def _(sp):
            sp.dma_start(out.rearrange("(t p) d -> p t d", p=P), S.x[:, :, :]).then_inc(stored, 16)
            sp.wait_ge(stored, 16)


def hybrid_block(nc, a, out):
    scratch = nc.dram_tensor("heads_by_token", (TOK, DM), FP32).ap()
    with ExitStack() as ctx:
        S = Shared(nc, ctx)
        load_stage(nc, S, a["x"], a["identity"])
        norm_stage(nc, S, "n1")
        attention_stage(nc, S, a["wqkv_codes"], a["wqkv_scales"], a["wo_codes"], a["wo_scales"], a["bo"])
        for i in range(2):
            if i == 1:
                clear_stage(nc, S, ("mn", "mr", "me"))
            norm_stage(nc, S, "mn", f"mn{i}")
            with ExitStack() as moe:
                combine = moe.enter_context(nc.sbuf_tensor(f"combine{i}", [NC * NE, TOK], BF16))
                route_stage(nc, S, "mr", f"mr{i}", a["gate_w"], a["similarity"], a["notdiag"], a["iota"], combine)
                experts_stage(nc, S, "me", f"me{i}", a["experts_w"], a["select"].bitcast(BF16), combine)
            if i == 0:
                norm_stage(nc, S, "n3")
                linear_stage(nc, S, a["lin_w"], a["lin_bias"], a["lin_bv"], a["lin_wo"], a["lin_bo"], a["cos"],
                             a["sin"], a["rand"], a["ones"], scratch)
        store_stage(nc, S, out)


def _arrays(d):
    A = lambda n: np.asarray(d["L0_attn_a_" + n])
    B = lambda n: np.asarray(d["L0_attn_b_" + n])
    F = lambda n: np.asarray(d["L0_ffn_" + n])
    f32 = np.float32
    out = {"x": A("x").reshape(TOK, DM), "identity": np.eye(P, dtype=f32)}

    def by_head(w):
        return w.reshape(KC, P, NH, HD).transpose(2, 1, 0, 3)

    def wrap(w, n):
        return np.concatenate([w, w[:n]], 0)

    codes = np.stack([by_head(A(f"w{m}_codes")) for m in "qkv"], 2).reshape(NH, P, -1)
    scales = np.stack([by_head(np.repeat(A(f"w{m}_scales"), 32, 0)) for m in "qkv"], 2).reshape(NH, P, -1)
    biases = np.stack([A("b" + m).reshape(NH, HD) for m in "qkv"], 2)
    out["wqkv_codes"] = wrap(np.concatenate([codes, biases], 2), 2)
    out["wqkv_scales"] = wrap(scales, 2)
    out["wo_codes"] = wrap(A("wo_codes").reshape(NH, HD, DM), 1)
    out["wo_scales"] = wrap(np.repeat(A("wo_scales"), 32, 0).reshape(NH, HD, DM), 1)
    out["bo"] = np.broadcast_to(A("bo"), (P, DM))

    gu = F("gate_up_proj")
    turn = lambda w: w.reshape(JT, P, KC, P).transpose(0, 3, 2, 1).reshape(JT, P, DM)
    gate, up = turn(gu[:, :FF].reshape(NF, DM)), turn(gu[:, FF:].reshape(NF, DM))
    down = F("down_proj").transpose(0, 2, 1).reshape(JT, P, DM)
    out["experts_w"] = np.concatenate([gate, up, down], 2)
    select = np.zeros((JT, NC, NE, P), np.uint16)
    for j in range(JT):
        for f in range(P):
            select[j, :, (j * P + f) // FF, f] = 0x3F80
    out["select"] = select.reshape(JT, NC * NE, P)
    out["gate_w"] = F("gate_weight").T.reshape(KC, P, NE).transpose(1, 0, 2)
    sim = np.zeros((P, P), f32)
    for s in range(SEC):
        sim[s * NE:(s + 1) * NE, s * NE:(s + 1) * NE] = F("similarity")
    out["similarity"] = sim
    out["notdiag"] = 1 - np.eye(P, dtype=f32)
    out["iota"] = np.broadcast_to(np.arange(NE, dtype=f32), (P, NE))

    def swap(w):
        w = w.reshape(-1, 2, LD // 2, *w.shape[1:])
        return w[:, ::-1].reshape(-1, *w.shape[3:])

    rows = lambda f: np.concatenate([B(f + "q"), B(f + "k"), B(f + "v"), swap(B(f + "q")), swap(B(f + "k"))], 0)
    out["lin_w"] = rows("W").reshape(7, P, KC, P).transpose(3, 2, 0, 1)
    out["lin_bias"] = rows("b").reshape(7, P).T
    out["lin_bv"] = np.broadcast_to(B("bv"), (P, P))
    out["lin_wo"] = B("Wo").T.reshape(KC, P, DM).transpose(1, 0, 2)
    out["lin_bo"] = np.broadcast_to(B("bo"), (P, DM))
    inv = (f32(1) / f32(10000.0) ** (np.arange(0, LD, 2, dtype=f32) / f32(LD))).astype(f32)
    angle = (np.arange(TOK, dtype=f32)[:, None] * inv[None, :]).astype(f32).astype(np.float64)
    sign = np.where(np.arange(P) % LD < LD // 2, -1.0, 1.0)[:, None]
    out["cos"] = np.cos(angle).T[np.arange(P) % (LD // 2)].astype(f32)
    out["sin"] = (np.sin(angle).T[np.arange(P) % (LD // 2)] * sign).astype(f32)
    rand, ones = np.zeros((P, 8, LE), f32), np.zeros((P, 8), f32)
    for h in range(8):
        rand[h * LD:(h + 1) * LD, h] = B("rand_matrix").T
        ones[h * LD:(h + 1) * LD, h] = 1
    out["rand"], out["ones"] = rand.reshape(P, -1), ones
    return {k: np.ascontiguousarray(v) for k, v in out.items()}


def kernel(**inputs):
    from concourse import bacc
    from concourse.bass_utils import run_bass_kernel_spmd

    nc = bacc.Bacc("TRN2", target_bir_lowering=False, num_devices=1)
    arrays = _arrays(inputs)
    args = {n: nc.dram_tensor("in_" + n, v.shape, mybir.dt.from_np(v.dtype), kind="ExternalInput").ap()
            for n, v in arrays.items()}
    out = nc.dram_tensor("out", (TOK, DM), FP32, kind="ExternalOutput").ap()
    hybrid_block(nc, args, out)
    r = run_bass_kernel_spmd(nc, [{"in_" + n: v for n, v in arrays.items()}], core_ids=[0])
    return r.results[0]["out"].reshape(1, TOK, DM)
```

```python
import math
from contextlib import ExitStack

import numpy as np

import concourse.bass as bass
from concourse import mybir

FP32 = mybir.dt.float32
F32R = mybir.dt.float32r
FP16 = mybir.dt.float16
BF16 = mybir.dt.bfloat16
U32 = mybir.dt.uint32
ALU = mybir.AluOpType
ACT = mybir.ActivationFunctionType
AX = mybir.AxisListType

P = 128
TOK = 2048
DM = 256
NT = TOK // P
NB = 4
TB = TOK // NB
TPB = NT // NB
KC = DM // P
NH = 16
HD = 128
EPS = 1e-5


def fp(ap):
    return ap.bitcast(FP32)


def block_of(b):
    return bass.ds(b * TB, TB)


class Shared:

    def __init__(self, nc, ctx):
        self.made = {}
        self.new_sem = lambda name: ctx.enter_context(nc.semaphore(name))
        sb = lambda name, shape, dt: ctx.enter_context(nc.sbuf_tensor(name, shape, dt))
        self.x = sb("residual", [P, NT, DM], FP32)
        self.xh = sb("normed_hi", [P, KC, TOK], F32R)
        self.xl = sb("normed_lo", [P, KC, TOK], F32R)
        self.ident = sb("identity_sb", [P, P], FP32)

    def sem(self, name):
        if name not in self.made:
            self.made[name] = self.new_sem(name)
        return self.made[name]


def clear_stage(nc, S, prefixes):
    block_ctx = ExitStack()
    with block_ctx:
        block = block_ctx.enter_context(nc.Block())

        @block.gpsimd
        def _(pool):
            for name, sem in S.made.items():
                if name.split("_")[0] in prefixes:
                    pool.sem_clear(sem)


class Norm:

    def __init__(self, nc, S, ctx, name, places, xn, banks, loads=None):
        sb = lambda n, shape, dt: ctx.enter_context(nc.sbuf_tensor(f"{places}_{n}", shape, dt))
        sem = lambda n: S.sem(f"{name}_{n}")
        stats = sb("stats", [P, NT, 6], FP32)
        mv = sb("mean_var", [P, NT, 2], FP32)
        ve = sb("var_eps", [P, NT], FP32)
        sd = sb("sd", [P, NT], FP32)
        r = sb("rsd", [P, NT], FP32)
        r2 = sb("rsd_square", [P, NT], FP32)
        fix = sb("newton", [P, NT], FP32)
        shift = sb("shift", [P, NT], FP32)
        turned = banks
        stats_done, var_ready, sd_ready = sem("stats_done"), sem("var_ready"), sem("sd_ready")
        small, r_ready, normed, normed_act = sem("small"), sem("r_ready"), sem("normed"), sem("normed_act")
        turned_ready, hi_ready, lo_ready = sem("turned_ready"), sem("hi_ready"), sem("lo_ready")
        HALF, HB = NT // 2, NB // 2
        OWN = TPB // 2

        def ready(engine, b):
            engine.wait_ge(lo_ready, KC * (b + 1))

        def done(engine):
            engine.wait_ge(lo_ready, KC * NB)

        def vector(dve):
            count = 0

            def after(ins):
                nonlocal count
                count += 1
                ins.then_inc(small, 1)
                dve.wait_ge(small, count)

            def statistics(h):
                for t in range(h * HALF, (h + 1) * HALF):
                    if loads and t % TPB == 0:
                        dve.wait_ge(loads[t // TPB], 16)
                    dve.bn_stats(stats[:, t, :], S.x[:, t, :]).then_inc(stats_done, 1)
                for t in range(h * HALF, (h + 1) * HALF):
                    dve.wait_ge(stats_done, t + 1)
                    ins = dve.bn_aggr(mv[:, t, :], stats[:, t, :])
                after(ins)
                tiles = slice(h * HALF, (h + 1) * HALF)
                dve.tensor_scalar(ve[:, tiles], mv[:, tiles, 1], EPS, None, ALU.add).then_inc(var_ready, 1)

            def factors(h):
                tiles = slice(h * HALF, (h + 1) * HALF)
                dve.wait_ge(sd_ready, h + 1)
                after(dve.reciprocal(r[:, tiles], sd[:, tiles]))
                after(dve.tensor_tensor(r2[:, tiles], r[:, tiles], r[:, tiles], ALU.mult))
                after(dve.tensor_tensor(r2[:, tiles], r2[:, tiles], ve[:, tiles], ALU.mult))
                after(dve.tensor_scalar(fix[:, tiles], r2[:, tiles], -0.5, 1.5, ALU.mult, ALU.add))
                after(dve.tensor_tensor(r[:, tiles], r[:, tiles], fix[:, tiles], ALU.mult))
                dve.scalar_tensor_tensor(out=shift[:, tiles], in0=mv[:, tiles, 0], scalar=-1.0, in1=r[:, tiles],
                                         op0=ALU.mult, op1=ALU.mult).then_inc(r_ready, 1)

            def tiles_of(b):
                for t in range(b * TPB + OWN, (b + 1) * TPB):
                    dve.tensor_scalar(xn[:, t, :], S.x[:, t, :], mv[:, t, 0:1], r[:, t:t + 1],
                                      ALU.subtract, ALU.mult).then_inc(normed, 1)

            def lows(b):
                for c in range(KC):
                    n = b * KC + c
                    dve.wait_ge(hi_ready, n + 1)
                    dve.tensor_tensor(S.xl[:, c, block_of(b)], turned[n % 4],
                                      fp(S.xh[:, c, block_of(b)]), ALU.subtract).then_inc(lo_ready, 1)

            statistics(0)
            statistics(1)
            factors(0)
            for b in range(HB):
                tiles_of(b)
            factors(1)
            for b in range(NB):
                if HB + b < NB:
                    tiles_of(HB + b)
                lows(b)

        def tensor(pe):
            for b in range(NB):
                pe.wait_ge(normed, (TPB - OWN) * (b + 1))
                pe.wait_ge(normed_act, OWN * (b + 1))
                for c in range(KC):
                    n = b * KC + c
                    if n >= 4:
                        pe.wait_ge(lo_ready, n - 3)
                    for i in range(TPB):
                        mm = pe.transpose(turned[n % 4][:, i * P:(i + 1) * P],
                                          xn[:, b * TPB + i, c * P:(c + 1) * P], S.ident[:, :])
                    mm.then_inc(turned_ready, 1)

        def scalar(act):
            def tiles_of(b):
                for t in range(b * TPB, b * TPB + OWN):
                    act.activation(xn[:, t, :], S.x[:, t, :], ACT.Identity, bias=shift[:, t:t + 1],
                                   scale=r[:, t:t + 1]).then_inc(normed_act, 1)

            def highs(b):
                for c in range(KC):
                    n = b * KC + c
                    act.wait_ge(turned_ready, n + 1)
                    act.activation(S.xh[:, c, block_of(b)], turned[n % 4], ACT.Copy).then_inc(hi_ready, 1)

            for h in range(2):
                tiles = slice(h * HALF, (h + 1) * HALF)
                act.wait_ge(var_ready, h + 1)
                act.activation(sd[:, tiles], ve[:, tiles], ACT.Sqrt).then_inc(sd_ready, 1)
            act.wait_ge(r_ready, 1)
            for b in range(HB):
                tiles_of(b)
            act.wait_ge(r_ready, 2)
            for b in range(NB):
                if HB + b < NB:
                    tiles_of(HB + b)
                highs(b)

        self.ready, self.done, self.vector, self.tensor, self.scalar = ready, done, vector, tensor, scalar


def attention_stage(nc, S, x_in, ident_in, wqkv_codes, wqkv_scales, wo_codes, wo_scales, bo):
    SCALE = 1.0 / math.sqrt(HD)
    KT = TOK // P
    GK = 4
    NG = KT // GK
    PV_CUT = [[0, 0, 2, 5], [5, 7, 9, 11], [11, 11, 13, 16]]
    with ExitStack() as ctx:
        sb = lambda n, shape, dt: ctx.enter_context(nc.sbuf_tensor(f"a_{n}", shape, dt))
        sem = lambda n: S.sem(f"a_{n}")
        Kh = [sb(f"keys_hi{i}", [P, TOK], FP16) for i in range(2)]
        Kl = [sb(f"keys_lo{i}", [P, TOK], FP16) for i in range(2)]
        Vh = [sb(f"values_hi{i}", [P, KT, HD], FP16) for i in range(2)]
        Vl = [sb(f"values_lo{i}", [P, KT, HD], FP16) for i in range(2)]
        Qh = [sb(f"queries_hi{i}", [P, TB], FP16) for i in range(2)]
        Ql = [sb(f"queries_lo{i}", [P, TB], FP16) for i in range(2)]
        vft = sb("values_by_feature", [P, TB], FP32)
        E = [sb(f"exponentials{i}", [P, TOK], FP32) for i in range(2)]
        Th = [sb(f"turned_hi{i}", [P, KT, TB], FP16) for i in range(2)]
        Tl = [sb(f"turned_lo{i}", [P, KT, TB], FP16) for i in range(2)]
        Oh = sb("out_hi", [P, TB], F32R)
        Ol = sb("out_lo", [P, TB], F32R)
        Wh = [sb(f"wqkv_hi{i}", [P, 3, KC, HD], F32R) for i in range(2)]
        Wl = [sb(f"wqkv_lo{i}", [P, 3, KC, HD], F32R) for i in range(2)]
        WOh = [sb(f"wo_hi{i}", [P, DM], F32R) for i in range(2)]
        WOl = [sb(f"wo_lo{i}", [P, DM], F32R) for i in range(2)]
        bias = [sb(f"bias{i}", [P, 3], FP32) for i in range(2)]
        NW = 3 * KC * HD
        codes = sb("codes", [P, NW + 3], FP32)
        scales = sb("scales", [P, NW], FP32)
        ocodes = sb("out_codes", [P, DM], FP32)
        oscales = sb("out_scales", [P, DM], FP32)
        bo_sb = sb("bo", [P, DM], FP32)
        halfmax = sb("halfmax", [P, TPB, 2], FP32)
        negmax = sb("negmax", [P, TPB], FP32)
        rowsum = [sb(f"rowsum{i}", [P, TPB, 2], FP32) for i in range(2)]
        rsum = sb("rowsum_both", [P, TPB], FP32)
        rinv = sb("rowsum_inverse", [P, TPB], FP32)

        scores = ctx.enter_context(nc.psum_tensor("a_scores", [P, TOK], FP32))
        turned = [ctx.enter_context(nc.psum_tensor(f"a_turned{i}", [P, GK, P], FP32)) for i in range(2)]
        obank = ctx.enter_context(nc.psum_tensor("a_out", [P, TB], FP32))
        mbank = ctx.enter_context(nc.psum_tensor("a_proj", [P, TB], FP32))

        scores_half, exps_turned, pv_done = sem("scores_half"), sem("exps_turned"), sem("pv_done")
        v_made, v_turned, q_made, k_made = sem("v_made"), sem("v_turned"), sem("q_made"), sem("k_made")
        ya_made, yb_made = sem("ya_made"), sem("yb_made")
        exps_ready, turned_hi, v_stored = sem("exps_ready"), sem("turned_hi"), sem("v_stored")
        v_hi, q_hi, k_hi, o_hi = sem("v_hi"), sem("q_hi"), sem("k_hi"), sem("o_hi")
        half_ready, negmax_ready, turned_lo = sem("half_ready"), sem("negmax_ready"), sem("turned_lo")
        v_lo, q_lo, k_lo, o_lo = sem("v_lo"), sem("q_lo"), sem("k_lo"), sem("o_lo")
        ya_added, yb_added, rinv_ready = sem("ya_added"), sem("yb_added"), sem("rinv_ready")
        rsum_ready = sem("rsum_ready")
        w_raw, wo_raw, bo_raw = sem("w_raw"), sem("wo_raw"), sem("bo_raw")
        wqkv_step, wo_step = sem("wqkv_step"), sem("wo_step")
        w_split, wo_split = sem("w_split"), sem("wo_split")
        x_loaded = [sem(f"x_loaded{b}") for b in range(NB)]
        ident_loaded = sem("ident_loaded")
        norm = Norm(nc, S, ctx, "n1", "n1", Th[0][:, :, :].bitcast(FP32), [scores[:, block_of(b)] for b in range(NB)], x_loaded)
        block = ctx.enter_context(nc.Block())
        Q, K, V = range(3)
        SPP = 2 * NB
        GS = TPB * NG
        CREDIT = 2

        def at(m):
            m %= SPP
            return m // NB, m % NB, m % 2

        def turned_to(T, m, t, g):
            qq = at(m if t else m - 1)[2]
            before = (t - 1) % TPB
            return T[qq][:, g * GK:(g + 1) * GK, before * P:(before + 1) * P]

        @block.sync
        def _(sp):
            for b in range(NB):
                sp.dma_start(S.x[:, b * TPB:(b + 1) * TPB, :],
                             x_in[b * TB:(b + 1) * TB, :].rearrange("(t p) d -> p t d", p=P)).then_inc(x_loaded[b], 16)
            sp.dma_start(S.ident[:, :], ident_in).then_inc(ident_loaded, 16)

            def load_qkv(h):
                sp.dma_start(codes[:, :], wqkv_codes[bass.ds(h, 1), :, :].rearrange("h p n -> (h p) n")).then_inc(w_raw, 16)
                sp.dma_start(scales[:, :], wqkv_scales[bass.ds(h, 1), :, :].rearrange("h p n -> (h p) n")).then_inc(w_raw, 16)

            def load_o(h):
                sp.dma_start(ocodes[:, :], wo_codes[bass.ds(h, 1), :, :].rearrange("h p n -> (h p) n")).then_inc(wo_raw, 16)
                sp.dma_start(oscales[:, :], wo_scales[bass.ds(h, 1), :, :].rearrange("h p n -> (h p) n")).then_inc(wo_raw, 16)

            load_qkv(0)
            load_o(0)
            sp.dma_start(bo_sb[:, :], bo).then_inc(bo_raw, 16)
            sp.wait_ge(w_split, 1)
            load_qkv(1)
            with sp.Fori(0, NH) as h:
                sp.wait_ge(wo_split, h + 1)
                load_o(h + 1)
                sp.wait_ge(w_split, h + 2)
                load_qkv(h + 2)

        @block.gpsimd
        def _(pool):
            flat = lambda w: w[:, :, :, :].rearrange("p m c f -> p (m c f)")

            def split_qkv(h, i):
                pool.wait_ge(w_raw, h * 32 + 32)
                pool.tensor_tensor(flat(Wh[i]), codes[:, 0:NW], scales[:, :], ALU.mult)
                pool.tensor_tensor(codes[:, 0:NW], codes[:, 0:NW], scales[:, :], ALU.mult).then_inc(wqkv_step, 1)
                pool.tensor_copy(bias[i][:, :], codes[:, NW:NW + 3])
                pool.wait_ge(wqkv_step, h + 1)
                pool.tensor_tensor(flat(Wl[i]), codes[:, 0:NW], fp(flat(Wh[i])), ALU.subtract).then_inc(w_split, 1)

            def split_o(h, i):
                pool.wait_ge(wo_raw, h * 32 + 32)
                pool.tensor_tensor(WOh[i][:, :], ocodes[:, :], oscales[:, :], ALU.mult)
                pool.tensor_tensor(ocodes[:, :], ocodes[:, :], oscales[:, :], ALU.mult).then_inc(wo_step, 1)
                pool.wait_ge(wo_step, h + 1)
                pool.tensor_tensor(WOl[i][:, :], ocodes[:, :], fp(WOh[i][:, :]), ALU.subtract).then_inc(wo_split, 1)

            split_qkv(0, 0)
            for z in (Th[1], Tl[1], Vh[1], Vl[1]):
                pool.memset(z[:, :, :].bitcast(FP32), 0.0)
            pool.memset(rowsum[1][:, :, :], 1.0)
            for z in (WOh[1], WOl[1]):
                ins = pool.memset(fp(z[:, :]), 0.0)
            ins.then_inc(turned_lo, CREDIT)
            pool.memset(E[1][:, :], 0.0).then_inc(exps_ready, CREDIT)
            split_o(0, 0)
            split_qkv(1, 1)
            with pool.Fori(0, NH // 2) as pair:
                for hh in range(2):
                    h = pair * 2 + hh
                    pool.wait_ge(yb_added, pair * SPP + (hh * NB + 2))
                    split_o(h + 1, 1 - hh)
                    pool.wait_ge(q_lo, pair * SPP + (hh * NB + 4))
                    split_qkv(h + 2, hh)

        @block.tensor
        def _(pe):
            def project(what, i, b, made, bank=mbank):
                for c in range(KC):
                    for k, (w, x) in enumerate(((Wh, S.xh), (Wh, S.xl), (Wl, S.xh))):
                        mm = pe.matmul(bank[:, :], w[i][:, what, c, :], x[:, c, block_of(b)],
                                       start=(c == 0 and k == 0), stop=(c == KC - 1 and k == 2))
                mm.then_inc(made, 1)

            def turn_values(bank=mbank):
                for i in range(TPB):
                    mm = pe.transpose(bank[:, i * P:(i + 1) * P], vft[:, i * P:(i + 1) * P], S.ident[:, :])
                mm.then_inc(v_turned, 1)

            def score(t, half, hh, qq):
                for c in range(2 * half, 2 * half + 2):
                    for q, k in ((Qh, Kh), (Qh, Kl), (Ql, Kh)):
                        mm = pe.matmul(scores[:, block_of(c)], q[qq][:, t * P:(t + 1) * P],
                                       k[hh][:, block_of(c)], start=(q is Qh and k is Kh), stop=(q is Ql))
                mm.then_inc(scores_half, 1)

            def values(n, k0, k1, hv, qv):
                for kt in range(k0, k1):
                    if kt == k0 or kt % GK == 0:
                        pe.wait_ge(turned_lo, n * GS + (kt // GK + 1 + CREDIT))
                    for v, e in ((Vh, Th), (Vh, Tl), (Vl, Th)):
                        mm = pe.matmul(obank[:, :], v[hv][:, kt, :], e[qv][:, kt, :],
                                       start=(kt == 0 and v is Vh and e is Th), stop=(kt == KT - 1 and v is Vl))
                if k1 == KT:
                    mm.then_inc(pv_done, 1)

            def turn(n, t, g):
                if g % (NG // 2) == 0:
                    pe.wait_ge(exps_ready, n * (2 * TPB) + (2 * t + CREDIT - 1 + g // (NG // 2)))
                pe.wait_ge(turned_lo, n * GS + (t * NG + g - 1 + CREDIT))
                for i in range(GK):
                    kt = g * GK + i
                    mm = pe.transpose(turned[g % 2][:, i, :], E[(t + 1) % 2][:, kt * P:(kt + 1) * P], S.ident[:, :])
                mm.then_inc(exps_turned, 1)

            def outputs(bank, a, ho, made):
                for i in range(2):
                    cols = slice((a + i) * P, (a + i + 1) * P)
                    for k, (o, w) in enumerate(((Oh, WOh), (Oh, WOl), (Ol, WOh))):
                        mm = pe.matmul(bank[:, i * DM:(i + 1) * DM], o[:, cols], w[ho][:, :],
                                       start=(k == 0), stop=(k == 2))
                mm.then_inc(made, 1)

            pe.wait_ge(ident_loaded, 16)
            norm.tensor(pe)
            norm.done(pe)
            pe.wait_ge(w_split, 1)
            for b in range(NB):
                if b:
                    pe.wait_ge(v_stored, b)
                project(V, 0, b, v_made)
                project(K, 0, b, k_made, scores[:, block_of(b)])
                pe.wait_ge(v_stored, b + 1)
                if b:
                    pe.wait_ge(v_lo, b)
                turn_values(obank)
            project(Q, 0, 0, q_made)
            pe.wait_ge(k_lo, NB)
            pe.wait_ge(v_lo, NB)

            def step(n, pair, m):
                hh, b, qq = at(m)
                h1, _, q1 = at(m - 1)
                if b == 0:
                    pe.wait_ge(w_split, pair * 2 + (hh + 2))
                if b == 1:
                    pe.wait_ge(wo_split, pair * 2 + (hh + 1))
                pe.wait_ge(q_lo, n + 1)
                pe.wait_ge(k_lo, n + NB)
                for t in range(TPB):
                    for half in range(2):
                        pe.wait_ge(exps_ready, n * (2 * TPB) + (2 * t + CREDIT - 1 + half))
                        score(t, half, hh, qq)
                        turn(n, t, half)
                    if t == 0:
                        pe.wait_ge(yb_added, n + 1)
                        project(V, 1 - hh, b, v_made)
                    if t == 1:
                        pe.wait_ge(v_stored, n + NB + 1)
                        turn_values()
                        values(n, *PV_CUT[t][0:2], h1, q1)
                    if t == 2:
                        pe.wait_ge(v_lo, n + NB + 1)
                        h2, b2, _ = at(m + 1)
                        project(Q, h2, b2, q_made)
                    if t == 3:
                        pe.wait_ge(q_lo, n + 2)
                        project(K, 1 - hh, b, k_made)
                        pe.wait_ge(o_lo, n + 1)
                        outputs(obank, 0, h1, ya_made)
                    turn(n, t, 2)
                    if t == 0:
                        pe.wait_ge(ya_added, n + 1)
                    if t < 3:
                        values(n, *PV_CUT[t][1:3], h1, q1)
                    turn(n, t, 3)
                    if t < 3:
                        values(n, *PV_CUT[t][2:4], h1, q1)
                    else:
                        pe.wait_ge(k_lo, n + NB + 1)
                        outputs(mbank, 2, h1, yb_made)

            with pe.Fori(0, NH // 2) as pair:
                for m in range(SPP):
                    step(pair * SPP + m, pair, m)

            N = NH * NB
            hh, _, qq = at(SPP - 1)
            for g in range(NG):
                turn(N, 0, g)
            pe.wait_ge(ya_added, N + 1)
            values(N, 0, KT, hh, qq)
            pe.wait_ge(o_lo, N + 1)
            outputs(obank, 0, hh, ya_made)
            pe.wait_ge(yb_added, N + 1)
            outputs(mbank, 2, hh, yb_made)

        @block.scalar
        def _(act):
            def store_values(i, count):
                act.wait_ge(v_made, count)
                act.activation(vft[:, :], mbank[:, :], ACT.Identity, bias=bias[i][:, V:V + 1]).then_inc(v_stored, 1)

            def values_hi(i, b, count, bank=mbank):
                act.wait_ge(v_turned, count)
                act.activation(Vh[i][:, b * TPB:(b + 1) * TPB, :].rearrange("p t d -> p (t d)"), bank[:, :],
                               ACT.Copy).then_inc(v_hi, 1)

            def keys_hi(i, b, count, bank=mbank):
                act.wait_ge(k_made, count)
                act.activation(Kh[i][:, block_of(b)], bank[:, :], ACT.Identity, bias=bias[i][:, K:K + 1]).then_inc(k_hi, 1)

            def queries_hi(i, q, count):
                act.wait_ge(q_made, count)
                act.activation(Qh[q][:, :], mbank[:, :], ACT.Identity, bias=bias[i][:, Q:Q + 1]).then_inc(q_hi, 1)

            def out_hi(count):
                act.wait_ge(pv_done, count)
                act.activation(Oh[:, :], obank[:, :], ACT.Copy).then_inc(o_hi, 1)

            def exponentials(t, half, qq):
                keys = slice(half * (TOK // 2), (half + 1) * (TOK // 2))
                act.activation(E[t % 2][:, keys], scores[:, keys], ACT.Exp, bias=negmax[:, t:t + 1], scale=SCALE,
                               accum_out=rowsum[qq][:, t, half:half + 1]).then_inc(exps_ready, 1)

            def evacuate(n, t, g, m):
                dst = turned_to(Th, m, t, g)
                act.wait_ge(exps_turned, n * GS + (t * NG + g + 1))
                act.activation(dst, turned[g % 2][:, :, :], ACT.Copy).then_inc(turned_hi, 1)

            norm.scalar(act)
            act.wait_ge(w_split, 1)
            for b in range(NB):
                store_values(0, b + 1)
                keys_hi(0, b, b + 1, scores[:, block_of(b)])
                values_hi(0, b, b + 1, obank)
            queries_hi(0, 0, 1)

            def step(n, pair, m):
                hh, b, qq = at(m)
                h2, _, q2 = at(m + 1)
                for t in range(TPB):
                    if t == 3:
                        out_hi(n + 1)
                    evacuate(n, t, 0, m)
                    evacuate(n, t, 1, m)
                    if t == 3:
                        keys_hi(1 - hh, b, n + NB + 1)
                    act.wait_ge(negmax_ready, n * TPB + (t + 1))
                    exponentials(t, 0, qq)
                    if t == 1:
                        values_hi(1 - hh, b, n + NB + 1)
                    evacuate(n, t, 2, m)
                    if t == 0:
                        store_values(1 - hh, n + NB + 1)
                    if t == 2:
                        queries_hi(h2, q2, n + 2)
                    exponentials(t, 1, qq)
                    evacuate(n, t, 3, m)

            with act.Fori(0, NH // 2) as pair:
                for m in range(SPP):
                    step(pair * SPP + m, pair, m)
            for g in range(NG):
                evacuate(NH * NB, 0, g, 0)
            out_hi(NH * NB + 1)

        @block.vector
        def _(dve):
            def values_lo(i, b, count, bank=mbank):
                tiles = lambda v: v[i][:, b * TPB:(b + 1) * TPB, :].rearrange("p t d -> p (t d)")
                dve.wait_ge(v_hi, count)
                dve.tensor_tensor(tiles(Vl), bank[:, :], tiles(Vh), ALU.subtract).then_inc(v_lo, 1)

            def keys_lo(i, b, count, bank=mbank):
                dve.wait_ge(k_hi, count)
                dve.scalar_tensor_tensor(out=Kl[i][:, block_of(b)], in0=bank[:, :], scalar=bias[i][:, K:K + 1],
                                         in1=Kh[i][:, block_of(b)], op0=ALU.add, op1=ALU.subtract).then_inc(k_lo, 1)

            def queries_lo(i, q, count):
                dve.wait_ge(q_hi, count)
                dve.scalar_tensor_tensor(out=Ql[q][:, :], in0=mbank[:, :], scalar=bias[i][:, Q:Q + 1],
                                         in1=Qh[q][:, :], op0=ALU.add, op1=ALU.subtract).then_inc(q_lo, 1)

            def out_lo(count):
                dve.wait_ge(o_hi, count)
                dve.tensor_tensor(Ol[:, :], obank[:, :], fp(Oh[:, :]), ALU.subtract).then_inc(o_lo, 1)

            def invert_sums(q, count):
                dve.tensor_tensor(rsum[:, :], rowsum[q][:, :, 0], rowsum[q][:, :, 1], ALU.add).then_inc(rsum_ready, 1)
                dve.wait_ge(rsum_ready, count)
                dve.reciprocal(rinv[:, :], rsum[:, :]).then_inc(rinv_ready, 1)
                dve.wait_ge(rinv_ready, count)

            def maximum(n, t, half):
                dve.wait_ge(scores_half, n * (2 * TPB) + (2 * t + half + 1))
                dve.tensor_reduce(halfmax[:, t, half:half + 1], scores[:, half * 2 * TB:(half + 1) * 2 * TB],
                                  AX.X, ALU.max).then_inc(half_ready, 1)

            def evacuate(n, t, g, m):
                dve.wait_ge(turned_hi, n * GS + (t * NG + g + 1))
                dve.tensor_tensor(turned_to(Tl, m, t, g), turned[g % 2][:, :, :], turned_to(Th, m, t, g),
                                  ALU.subtract).then_inc(turned_lo, 1)

            def add(bank, b, a):
                for i in range(2):
                    t = b * TPB + a + i
                    ins = dve.scalar_tensor_tensor(out=S.x[:, t, :], in0=bank[:, i * DM:(i + 1) * DM],
                                                   scalar=rinv[:, a + i:a + i + 1], in1=S.x[:, t, :],
                                                   op0=ALU.mult, op1=ALU.add)
                return ins

            norm.vector(dve)
            for b in range(NB):
                keys_lo(0, b, b + 1, scores[:, block_of(b)])
                values_lo(0, b, b + 1, obank)
            queries_lo(0, 0, 1)
            dve.wait_ge(bo_raw, 16)
            for t in range(NT):
                ins = dve.tensor_tensor(S.x[:, t, :], S.x[:, t, :], bo_sb[:, :], ALU.add)
            ins.then_inc(ya_added, 1)
            dve.wait_ge(ya_added, 1)
            dve.sem_inc(yb_added, 1)

            def step(n, pair, m):
                hh, b, qq = at(m)
                h2, _, q2 = at(m + 1)
                _, b1, q1 = at(m - 1)
                for t in range(TPB):
                    if t == 3:
                        out_lo(n + 1)
                    first = (evacuate, maximum) if t == 0 else (maximum, evacuate)
                    for half in range(2):
                        for work in first:
                            if work is maximum:
                                maximum(n, t, half)
                            elif half == 0 or t == 0:
                                evacuate(n, t, half, m)
                    dve.wait_ge(half_ready, n * (2 * TPB) + (2 * t + 2))
                    dve.tensor_scalar(negmax[:, t:t + 1], halfmax[:, t, 0:1], halfmax[:, t, 1:2], -SCALE,
                                      ALU.max, ALU.mult).then_inc(negmax_ready, 1)
                    if t:
                        evacuate(n, t, 1, m)
                    if t == 3:
                        keys_lo(1 - hh, b, n + NB + 1)
                        invert_sums(q1, n + 1)
                    evacuate(n, t, 2, m)
                    if t == 1:
                        values_lo(1 - hh, b, n + NB + 1)
                    if t == 2:
                        queries_lo(h2, q2, n + 2)
                    if t == 3:
                        dve.wait_ge(ya_made, n + 1)
                        add(obank, b1, 0).then_inc(ya_added, 1)
                    evacuate(n, t, 3, m)
                    if t == 3:
                        dve.wait_ge(yb_made, n + 1)
                        add(mbank, b1, 2).then_inc(yb_added, 1)

            with dve.Fori(0, NH // 2) as pair:
                for m in range(SPP):
                    step(pair * SPP + m, pair, m)

            N = NH * NB
            for g in range(NG):
                evacuate(N, 0, g, 0)
            out_lo(N + 1)
            invert_sums(at(SPP - 1)[2], N + 1)
            dve.wait_ge(ya_made, N + 1)
            add(obank, NB - 1, 0).then_inc(ya_added, 1)
            dve.wait_ge(yb_made, N + 1)
            add(mbank, NB - 1, 2).then_inc(yb_added, 1)


NE = 32
TOPK = 8
PRIM = 4
SEC = TOPK - PRIM
THRESHOLD = 0.5
FF = 96
NF = NE * FF
JT = NF // P
NC = 3


class Experts:

    PIECES = 3

    def __init__(self, nc, S, ctx, name, places, w_in, sel_in):
        sb = lambda n, shape, dt: ctx.enter_context(nc.sbuf_tensor(f"{places}_{n}", shape, dt))
        sem = lambda n: S.sem(f"{name}_{n}")
        NWJ = 2 * KC * P + DM
        self.DOWN = slice(2 * KC * P, NWJ)
        self.raw = raw = [sb(f"raw{i}", [P, NWJ], FP32) for i in range(2)]
        self.Wh = Wh = [sb(f"w_hi{i}", [P, NWJ], F32R) for i in range(2)]
        self.Wl = Wl = [sb(f"w_lo{i}", [P, NWJ], F32R) for i in range(2)]
        self.zeros = zeros = sb("zeros", [P, KC * P], FP32)
        self.sel = sel = [sb(f"select{i}", [NC * NE, P], BF16) for i in range(2)]
        self.Hh = Hh = [sb(f"inner_hi{i}", [P, TB], F32R) for i in range(2)]
        self.Hl = Hl = [sb(f"inner_lo{i}", [P, TB], F32R) for i in range(2)]
        self.raw_loaded = raw_loaded = [sem(f"raw_loaded{i}") for i in range(2)]
        self.sel_loaded = sel_loaded = [sem(f"select_loaded{i}") for i in range(2)]
        self.piece_hi, self.w_split, self.inner_lo = piece_hi, w_split, inner_lo = sem("piece_hi"), sem("w_split"), sem("inner_lo")
        PIECES = self.PIECES

        def load(sp, j, i):
            sp.dma_start(raw[i][:, :], w_in[bass.ds(j, 1), :, :].rearrange("j p n -> (j p) n")).then_inc(raw_loaded[i], 16)

        def load_sel(sp, j, i):
            sp.dma_start(sel[i][:, :], sel_in[bass.ds(j, 1), :, :].rearrange("j p n -> (j p) n")).then_inc(sel_loaded[i], 16)

        def split(pool, piece, l, i):
            cols = slice(piece * KC * P, (piece + 1) * KC * P)
            count = l * (2 * PIECES) + (PIECES * i + piece + 1)
            if piece == 0:
                pool.wait_ge(raw_loaded[i], l * 16 + 16)
            pool.tensor_tensor(Wh[i][:, cols], raw[i][:, cols], zeros[:, :], ALU.add).then_inc(piece_hi, 1)
            pool.wait_ge(piece_hi, count)
            pool.tensor_tensor(Wl[i][:, cols], raw[i][:, cols], fp(Wh[i][:, cols]), ALU.subtract).then_inc(w_split, 1)

        def prefetch(sp):
            for i in range(2):
                load(sp, i, i)
                load_sel(sp, i, i)

        def prepare(pool):
            pool.memset(zeros[:, :], 0.0)
            for z in (Hh[1], Hl[1], Wh[1], Wl[1]):
                ins = pool.memset(fp(z[:, :]), 0.0)
            ins.then_inc(inner_lo, 1)
            pool.wait_ge(inner_lo, 1)
            for piece in range(PIECES):
                split(pool, piece, 0, 0)

        self.load, self.load_sel, self.split = load, load_sel, split
        self.prefetch, self.prepare = prefetch, prepare


class ExpertsPrograms:

    def __init__(self, nc, S, ctx, name, places, E, combine, result, banks):
        sb = lambda n, shape, dt: ctx.enter_context(nc.sbuf_tensor(f"{places}_{n}", shape, dt))
        sem = lambda n: S.sem(f"{name}_{n}")
        Wh, Wl, sel, Hh, Hl, DOWN, PIECES = E.Wh, E.Wl, E.sel, E.Hh, E.Hl, E.DOWN, E.PIECES
        sel_loaded, w_split, inner_lo = E.sel_loaded, E.w_split, E.inner_lo
        a = [sb(f"silu{i}", [P, TB], FP32) for i in range(2)]
        au = [sb(f"silu_up{i}", [P, TB], FP32) for i in range(2)]
        h = [sb(f"inner{i}", [P, TB], FP32) for i in range(2)]
        gate_ps, up_ps, comb_ps = banks[0:2], banks[2:4], banks[4:6]
        out_ps = banks[6].rearrange("p (t d) -> p t d", d=DM)
        gate_made, up_made, comb_made, out_made = sem("gate_made"), sem("up_made"), sem("weight_made"), sem("out_made")
        silu_ready, inner_hi = sem("silu_ready"), sem("inner_hi")
        up_used, inner_ready, out_added = sem("up_used"), sem("inner_ready"), sem("out_added")
        result_stored = sem("result_stored")
        SPL = 2 * NB
        LOOPS = JT // 2
        EARLY = 2

        def sync(sp):
            with sp.Fori(0, LOOPS - 1) as l:
                for i in range(2):
                    sp.wait_ge(w_split, l * (2 * PIECES) + PIECES * (i + 1))
                    E.load(sp, l * 2 + (i + 2), i)
                    sp.wait_ge(comb_made, l * SPL + NB * (i + 1))
                    E.load_sel(sp, l * 2 + (i + 2), i)
            if result is not None:
                for b in range(NB):
                    sp.wait_ge(out_added, LOOPS * SPL - NB + (b + 3))
                    sp.dma_start(result[b * TB:(b + 1) * TB, :].rearrange("(t p) d -> p t d", p=P),
                                 S.x[:, b * TPB:(b + 1) * TPB, :]).then_inc(result_stored, 16)
                sp.wait_ge(result_stored, 16 * NB)

        def gpsimd(pool):
            def low(n, q):
                pool.wait_ge(inner_hi, n + 1)
                pool.tensor_tensor(Hl[q][:, :], h[q][:, :], fp(Hh[q][:, :]), ALU.subtract).then_inc(inner_lo, 1)

            def round_(l, last):
                for m in range(SPL):
                    i, b = m // NB, m % NB
                    low(l * SPL + m, m % 2)
                    if b < PIECES and not (last and i == 1):
                        if b == 0:
                            pool.wait_ge(out_made, l * SPL + (m + 1))
                        E.split(pool, b, l + i, 1 - i)

            with pool.Fori(0, LOOPS - 1) as l:
                round_(l, False)
            round_(LOOPS - 1, True)

        def gate_and_up(pe, l, m):
            i, b, q = m // NB, m % NB, m % 2
            if b == 0:
                pe.wait_ge(w_split, l * (2 * PIECES) + (PIECES * i + 2))
            for half, bank, made in ((0, gate_ps, gate_made), (1, up_ps, up_made)):
                for c in range(KC):
                    cols = slice((half * KC + c) * P, (half * KC + c + 1) * P)
                    for k, (w, x) in enumerate(((Wh, S.xh), (Wh, S.xl), (Wl, S.xh))):
                        mm = pe.matmul(bank[q], w[i][:, cols], x[:, c, block_of(b)],
                                       start=(c == 0 and k == 0), stop=(c == KC - 1 and k == 2))
                mm.then_inc(made, 1)

        def tensor_early(pe):
            for m in range(EARLY):
                gate_and_up(pe, 0, m)

        def tensor(pe):
            def weights(l, m):
                i, b, q = m // NB, m % NB, m % 2
                if b == 0:
                    pe.wait_ge(sel_loaded[i], l * 16 + 16)
                pe.matmul(comb_ps[q], sel[i][:, :], combine[:, block_of(b)], start=True, stop=True).then_inc(comb_made, 1)

            def outputs(n, m):
                m1 = (m - 1) % SPL
                i, q = m1 // NB, m1 % 2
                pe.wait_ge(inner_lo, n + 1)
                pe.wait_ge(out_added, n + 1)
                for t in range(TPB):
                    cols = slice(t * P, (t + 1) * P)
                    for k, (g, w) in enumerate(((Hh, Wh), (Hh, Wl), (Hl, Wh))):
                        mm = pe.matmul(out_ps[:, t, :], g[q][:, cols], w[i][:, DOWN], start=(k == 0), stop=(k == 2))
                mm.then_inc(out_made, 1)

            def round_(l, early):
                for m in range(SPL):
                    n = l * SPL + m
                    if m >= early:
                        gate_and_up(pe, l, m)
                    weights(l, m)
                    if m % NB == 1:
                        pe.wait_ge(w_split, l * (2 * PIECES) + PIECES * (m // NB + 1))
                    outputs(n, m)

            round_(0, EARLY)
            with pe.Fori(1, LOOPS) as l:
                round_(l, 0)
            outputs(LOOPS * SPL, 0)

        def silu(act, n, q):
            act.wait_ge(gate_made, n + 1)
            act.activation(a[q][:, :], gate_ps[q], ACT.Silu).then_inc(silu_ready, 1)

        def scalar_early(act):
            for m in range(EARLY):
                silu(act, m, m % 2)

        def scalar(act):
            def round_(l, early):
                for m in range(SPL):
                    n, q = l * SPL + m, m % 2
                    if m >= early:
                        silu(act, n, q)
                    act.wait_ge(inner_ready, n + 1)
                    act.activation(Hh[q][:, :], h[q][:, :], ACT.Copy).then_inc(inner_hi, 1)

            round_(0, EARLY)
            with act.Fori(1, LOOPS) as l:
                round_(l, 0)

        def vector(dve):
            def add(n, m):
                b = (m - 1) % NB
                dve.wait_ge(out_made, n + 1)
                x = S.x[:, b * TPB:(b + 1) * TPB, :]
                dve.tensor_tensor(x, x, out_ps[:, :, :], ALU.add).then_inc(out_added, 1)

            dve.sem_inc(out_added, 1)
            with dve.Fori(0, LOOPS) as l:
                for m in range(SPL):
                    n, q = l * SPL + m, m % 2
                    dve.wait_ge(silu_ready, n + 1)
                    dve.wait_ge(up_made, n + 1)
                    dve.tensor_tensor(au[q][:, :], a[q][:, :], up_ps[q], ALU.mult).then_inc(up_used, 1)
                    dve.wait_ge(up_used, n + 1)
                    dve.wait_ge(comb_made, n + 1)
                    dve.tensor_tensor(h[q][:, :], au[q][:, :], comb_ps[q], ALU.mult).then_inc(inner_ready, 1)
                    add(n, m)
            add(LOOPS * SPL, 0)

        self.sync, self.gpsimd, self.scalar, self.vector = sync, gpsimd, scalar, vector
        self.tensor_early, self.tensor, self.scalar_early = tensor_early, tensor, scalar_early


def moe_stage(nc, S, name, places, gate_w, sim_in, notdiag_in, iota_in, combine, experts, result):
    HALF = NT // 2
    with ExitStack() as ctx:
        sb = lambda n, shape, dt: ctx.enter_context(nc.sbuf_tensor(f"{places}_{n}", shape, dt))
        sem = lambda n: S.sem(f"{name}_{n}")
        gate = sb("gate", [P, KC, P], FP32)
        gh, gl = sb("gate_hi", [P, KC, P], F32R), sb("gate_lo", [P, KC, P], F32R)
        by_expert = sb("logits_by_expert", [NE, TOK], FP32)
        sim = sb("similarity", [P, P], FP32)
        simp = sb("similarity_parts", [P, NC, P], BF16)
        notdiag = sb("notdiag", [P, P], FP32)
        iota = sb("iota", [P, NE], FP32)
        expo = sb("expo", [P, NT, NE], FP32)
        shifted = sb("shifted", [P, NT, NE], FP32)
        top_logit = sb("top_logit", [P, NT], FP32)
        total = sb("total", [P, NT], FP32)
        top = sb("top", [P, NT, TOPK], FP32)
        index = sb("index", [P, NT, TOPK], U32)
        indexf = sb("indexf", [P, NT, TOPK], FP32)
        topsum = sb("topsum", [P, NT], FP32)
        hot = sb("onehot", [P, NT, TOPK, NE], BF16)
        hotT = sb("onehot_turned", [P, TOK], BF16)
        product = sb("product", [P, NT * TOPK * NE], FP32)
        product2 = sb("product2", [P, NT * TOPK * NE], FP32)
        cand = sb("candidates", [P, SEC, NT, PRIM], FP32)
        best = sb("best", [P, SEC, NT], FP32)
        isbest = sb("isbest", [P, SEC, NT, PRIM], FP32)
        seen = sb("seen", [P, SEC, NT], FP32)
        reroute = sb("reroute", [P, SEC, NT], FP32)
        moved = sb("moved", [P, SEC, NT], FP32)
        gained = sb("gained", [P, NT, PRIM], FP32)
        coef = sb("coef", [P, NT, TOPK], FP32)
        comb = sb("comb", [P, NT, NE], FP32)
        parts = sb("comb_parts", [P, NT, NC, NE], BF16)
        identb = sb("identity_bf16", [P, P], BF16)
        logits = ctx.enter_context(nc.psum_tensor(f"{places}_logits", [P, NT, NE], FP32))
        rows = ctx.enter_context(nc.psum_tensor(f"{places}_sim_rows", [P, NT, SEC, NE], FP32))
        hot_ps = ctx.enter_context(nc.psum_tensor(f"{places}_hot_ps", [P, HALF * P], BF16))
        two = ctx.enter_context(nc.psum_tensor(f"{places}_comb_ps", [P, 2 * TB], FP32))
        lt_ps = [two[:, i * TB:(i + 1) * TB] for i in range(2)]
        comb_ps = two[:, :].bitcast(BF16)
        cand_ps = logits[:, :, :].rearrange("p t e -> p (t e)")[:, 0:SEC * HALF * PRIM]
        comb0_ps = rows[:, 0:2, :, :].rearrange("p t s e -> p (t s e)")
        turned_hot = [hot_ps[:, :], comb_ps[:, 0:HALF * P]]
        norm = Norm(nc, S, ctx, "mn", f"{places}_n", product[:, :].rearrange("p (t d) -> p t d", d=DM),
                    [rows[:, b * TPB:(b + 1) * TPB, :, :].rearrange("p t s e -> p (t s e)") for b in range(NB)])
        gate_loaded, loaded = sem("gate_loaded"), sem("loaded")
        step = sem("dve_step")
        gate_ready, lt_made, lt_stored = sem("gate_ready"), sem("lt_made"), sem("lt_stored")
        logits_ready, shifted_ready, expo_ready = sem("logits_ready"), sem("shifted_ready"), sem("expo_ready")
        hot_ready, hot_turned, hot_stored, rows_ready = sem("hot_ready"), sem("hot_turned"), sem("hot_stored"), sem("rows_ready")
        parts_ready, comb_turned, comb_stored = sem("parts_ready"), sem("comb_turned"), sem("comb_stored")
        sim_ready, similar_ready, cand_made = sem("sim_ready"), sem("similar_ready"), sem("cand_made")
        weighted_ready, comb0_made = sem("weighted_ready"), sem("comb0_made")
        cand_used = sem("cand_used")
        flat_rows = rows[:, :, :, :].rearrange("p t s e -> p (t s e)")
        row_bank = lambda i: flat_rows[:, i * TB:(i + 1) * TB]
        work = ExpertsPrograms(nc, S, ctx, "me", f"{places}_e", experts, combine, result,
                               [row_bank(2), row_bank(1), row_bank(3), logits[:, :, :].rearrange("p t e -> p (t e)"),
                                hot_ps[:, :].bitcast(FP32), row_bank(0), two[:, :]])
        block = ctx.enter_context(nc.Block())
        tiles = lambda h: slice(h * HALF, (h + 1) * HALF)
        by_sec = [a[:, :].rearrange("p (s t k e) -> p s t k e", s=SEC, k=PRIM, e=NE) for a in (product, product2)]
        weighted = [a[:, 0:HALF * TOPK * NE].rearrange("p (t k e) -> p t k e", k=TOPK, e=NE) for a in (product, product2)]

        @block.sync
        def _(sp):
            sp.dma_start(gate[:, :, :], gate_w).then_inc(gate_loaded, 16)
            sp.dma_start(sim[:, :], sim_in).then_inc(loaded, 16)
            sp.dma_start(notdiag[:, :], notdiag_in).then_inc(loaded, 16)
            sp.dma_start(iota[:, :], iota_in).then_inc(loaded, 16)
            experts.prefetch(sp)
            work.sync(sp)

        @block.gpsimd
        def _(pool):
            pool.wait_ge(gate_loaded, 16)
            pool.tensor_copy(gh[:, :, :], gate[:, :, :]).then_inc(gate_ready, 1)
            pool.wait_ge(gate_ready, 1)
            pool.tensor_tensor(gl[:, :, :], gate[:, :, :], fp(gh[:, :, :]), ALU.subtract).then_inc(gate_ready, 1)
            experts.prepare(pool)
            work.gpsimd(pool)

        @block.tensor
        def _(pe):
            def turn_logits(b):
                pe.wait_ge(lt_stored, b + 1)
                for t in range(b * TPB, (b + 1) * TPB):
                    mm = pe.transpose(logits[:, t, :], by_expert[:, t * P:(t + 1) * P], S.ident[0:NE, 0:NE])
                return mm

            norm.tensor(pe)
            pe.wait_ge(gate_ready, 2)
            for b in range(NB):
                norm.ready(pe, b)
                if b >= 2:
                    pe.wait_ge(lt_stored, b - 1)
                for c in range(KC):
                    for k, (g, x) in enumerate(((gh, S.xh), (gh, S.xl), (gl, S.xh))):
                        mm = pe.matmul(lt_ps[b % 2], g[:, c, :], x[:, c, block_of(b)],
                                       start=(c == 0 and k == 0), stop=(c == KC - 1 and k == 2))
                mm.then_inc(lt_made, 1)
                if b:
                    turn_logits(b - 1)
            turn_logits(NB - 1).then_inc(logits_ready, 1)
            pe.wait_ge(sim_ready, 1)
            for h in range(2):
                pe.wait_ge(hot_ready, h + 1)
                for i in range(HALF):
                    mm = pe.transpose(turned_hot[h][:, i * P:(i + 1) * P],
                                      hot[:, h * HALF + i, PRIM:TOPK, :].rearrange("p s e -> p (s e)"), identb[:, :])
                mm.then_inc(hot_turned, 1)
            for h in range(2):
                pe.wait_ge(hot_stored, h + 1)
                for t in range(h * HALF, (h + 1) * HALF):
                    for c in range(NC):
                        mm = pe.matmul(rows[:, t, :, :].rearrange("p s e -> p (s e)"), hotT[:, t * P:(t + 1) * P],
                                       simp[:, c, :], start=(c == 0), stop=(c == NC - 1))
                    if t % TPB == TPB - 1:
                        mm.then_inc(rows_ready, 1)
            pe.wait_ge(similar_ready, 1)
            for e in range(NE):
                mm = pe.matmul(cand_ps, S.ident[:, :], by_sec[0].rearrange("p s t k e -> p (s t k) e")[:, :, e],
                               start=(e == 0), stop=(e == NE - 1))
            mm.then_inc(cand_made, 1)
            pe.wait_ge(cand_used, 1)
            work.tensor_early(pe)
            pe.wait_ge(weighted_ready, 1)
            for k in range(TOPK):
                mm = pe.matmul(comb0_ps, S.ident[:, :], weighted[0][:, :, k, :], start=(k == 0), stop=(k == TOPK - 1))
            mm.then_inc(comb0_made, 1)
            for i, h in enumerate((1, 0)):
                pe.wait_ge(parts_ready, i + 1)
                for t in range(h * HALF, (h + 1) * HALF):
                    mm = pe.transpose(comb_ps[0:NC * NE, t * P:(t + 1) * P],
                                      parts[:, t, :, :].rearrange("p c e -> p (c e)"), identb[:, :])
                mm.then_inc(comb_turned, 1)
            pe.wait_ge(comb_stored, 2)
            work.tensor(pe)

        @block.scalar
        def _(act):
            norm.scalar(act)
            for b in range(NB):
                act.wait_ge(lt_made, b + 1)
                act.activation(by_expert[:, block_of(b)], lt_ps[b % 2][0:NE, :], ACT.Copy).then_inc(lt_stored, 1)
            act.wait_ge(shifted_ready, 1)
            act.activation(expo[:, :, :], shifted[:, :, :], ACT.Exp).then_inc(expo_ready, 1)
            for h in range(2):
                act.wait_ge(hot_turned, h + 1)
                act.activation(hotT[:, h * HALF * P:(h + 1) * HALF * P], turned_hot[h], ACT.Copy).then_inc(hot_stored, 1)
            work.scalar_early(act)
            for i, h in enumerate((1, 0)):
                cols = slice(h * HALF * P, (h + 1) * HALF * P)
                act.wait_ge(comb_turned, i + 1)
                act.activation(combine[:, cols], comb_ps[0:NC * NE, cols], ACT.Copy).then_inc(comb_stored, 1)
            work.scalar(act)

        @block.vector
        def _(dve):
            done = 0

            def after(ins):
                nonlocal done
                done += 1
                ins.then_inc(step, 1)
                dve.wait_ge(step, done)

            def over(ap, n, dim):
                a = ap.unsqueeze(dim)
                shape = list(a.shape)
                shape[dim] = n
                return a.broadcast_to(shape)

            norm.vector(dve)
            dve.tensor_copy(identb[:, :], S.ident[:, :])
            dve.wait_ge(loaded, 48)
            after(dve.tensor_tensor(sim[:, :], sim[:, :], notdiag[:, :], ALU.mult))
            after(dve.tensor_tensor(sim[:, :], sim[:, :], S.ident[:, :], ALU.add))
            for c in range(NC):
                ins = dve.tensor_copy(simp[:, c, :], sim[:, :])
                if c < NC - 1:
                    after(ins)
                    after(dve.tensor_tensor(sim[:, :], sim[:, :], simp[:, c, :], ALU.subtract))
            ins.then_inc(sim_ready, 1)

            dve.wait_ge(logits_ready, 1)
            after(dve.tensor_reduce(top_logit[:, :], logits[:, :, :], AX.X, ALU.max))
            dve.tensor_tensor(shifted[:, :, :], logits[:, :, :], over(top_logit[:, :], NE, 2), ALU.subtract).then_inc(shifted_ready, 1)
            dve.wait_ge(expo_ready, 1)
            after(dve.tensor_reduce(total[:, :], expo[:, :, :], AX.X, ALU.add))
            after(dve.reciprocal(total[:, :], total[:, :]))
            after(dve.tensor_tensor(expo[:, :, :], expo[:, :, :], over(total[:, :], NE, 2), ALU.mult))

            for t in range(NT):
                ins = dve.max(top[:, t, :], expo[:, t, :])
            after(ins)
            for t in range(NT):
                ins = dve.max_index(index[:, t, :], top[:, t, :], expo[:, t, :])
            after(ins)
            after(dve.tensor_copy(indexf[:, :, :], index[:, :, :]))
            for h in range(2):
                dve.tensor_tensor(hot[:, tiles(h), :, :].rearrange("p t k e -> p (t k) e"),
                                  over(indexf[:, tiles(h), :].rearrange("p t k -> p (t k)"), NE, 2),
                                  over(iota[:, :], HALF * TOPK, 1), ALU.is_equal).then_inc(hot_ready, 1)
            after(dve.tensor_reduce(topsum[:, :], top[:, :, :], AX.X, ALU.add))
            after(dve.tensor_scalar(topsum[:, :], topsum[:, :], 1e-12, None, ALU.max))
            after(dve.reciprocal(topsum[:, :], topsum[:, :]))
            after(dve.tensor_tensor(coef[:, :, :], top[:, :, :], over(topsum[:, :], TOPK, 2), ALU.mult))

            dve.wait_ge(hot_ready, 2)
            for h in range(2):
                for b in range(h * NB // 2, (h + 1) * NB // 2):
                    dve.wait_ge(rows_ready, b + 1)
                    four = slice(b * TPB, (b + 1) * TPB)
                    at = slice((b * TPB) % HALF, (b * TPB) % HALF + TPB)
                    for s in range(SEC):
                        ins = dve.tensor_tensor(by_sec[h][:, s, at, :, :], over(rows[:, four, s, :], PRIM, 2),
                                                hot[:, four, 0:PRIM, :], ALU.mult)
                if h == 0:
                    ins.then_inc(similar_ready, 1)
            after(ins)
            after(dve.tensor_reduce(cand[:, :, tiles(1), :].rearrange("p s t k -> p s (t k)"),
                                    by_sec[1].rearrange("p s t k e -> p s (t k) e"), AX.X, ALU.add))
            dve.wait_ge(cand_made, 1)
            dve.tensor_copy(cand[:, :, tiles(0), :].rearrange("p s t k -> p s (t k)"),
                            cand_ps.rearrange("p (s n) -> p s n", s=SEC)).then_inc(cand_used, 1)
            dve.wait_ge(cand_used, 1)
            sec = coef[:, :, PRIM:TOPK].rearrange("p t s -> p s t")
            after(dve.tensor_reduce(best[:, :, :], cand[:, :, :, :], AX.X, ALU.max))
            after(dve.tensor_tensor(isbest[:, :, :, :], cand[:, :, :, :], over(best[:, :, :], PRIM, 3), ALU.is_equal))
            after(dve.tensor_copy(seen[:, :, :], isbest[:, :, :, 0]))
            for q in range(1, PRIM):
                after(dve.tensor_tensor(isbest[:, :, :, q], isbest[:, :, :, q], seen[:, :, :], ALU.is_gt))
                after(dve.tensor_tensor(seen[:, :, :], isbest[:, :, :, q], seen[:, :, :], ALU.max))
            after(dve.tensor_scalar(reroute[:, :, :], best[:, :, :], THRESHOLD, None, ALU.is_ge))
            after(dve.tensor_tensor(moved[:, :, :], sec, reroute[:, :, :], ALU.mult))
            after(dve.tensor_tensor(sec, sec, moved[:, :, :], ALU.subtract))
            after(dve.tensor_tensor(isbest[:, :, :, :], isbest[:, :, :, :], over(moved[:, :, :], PRIM, 3), ALU.mult))
            after(dve.tensor_reduce(gained[:, :, :], isbest[:, :, :, :].rearrange("p s t q -> p t q s"), AX.X, ALU.add))
            after(dve.tensor_tensor(coef[:, :, 0:PRIM], coef[:, :, 0:PRIM], gained[:, :, :], ALU.add))
            for h in range(2):
                ins = dve.tensor_tensor(weighted[h].rearrange("p t k e -> p (t k) e"),
                                        hot[:, tiles(h), :, :].rearrange("p t k e -> p (t k) e"),
                                        over(coef[:, tiles(h), :].rearrange("p t k -> p (t k)"), NE, 2), ALU.mult)
                if h == 0:
                    ins.then_inc(weighted_ready, 1)
            after(ins)
            for h in (1, 0):
                if h == 1:
                    after(dve.tensor_reduce(comb[:, tiles(1), :], weighted[1].rearrange("p t k e -> p t e k"), AX.X, ALU.add))
                else:
                    dve.wait_ge(comb0_made, 1)
                    after(dve.tensor_copy(comb[:, tiles(0), :].rearrange("p t e -> p (t e)"), comb0_ps))
                for c in range(NC):
                    ins = dve.tensor_copy(parts[:, tiles(h), c, :], comb[:, tiles(h), :])
                    if c < NC - 1:
                        after(ins)
                        after(dve.tensor_tensor(comb[:, tiles(h), :], comb[:, tiles(h), :], parts[:, tiles(h), c, :], ALU.subtract))
                ins.then_inc(parts_ready, 1)
            work.vector(dve)


LH, LKV, LD = 16, 8, 16
LF = LD
LE = LF // 2
TWO_PI_HI = 6.28125
TWO_PI_LO = 2 * math.pi - TWO_PI_HI
ROUND = 1.5 * 2.0 ** 23


def linear_stage(nc, S, w_in, bias_in, bv_in, wo_in, bo_in, cos_in, sin_in, rand_in, ones_in, scratch):
    HT = 8
    NU = LH // HT + LKV // HT
    NHD = NU * HT
    COLS = LE + 1
    MID = HT * LE
    OUT = 7
    VT = 3
    with ExitStack() as ctx:
        sb = lambda n, shape, dt=FP32: ctx.enter_context(nc.sbuf_tensor(f"l_{n}", shape, dt))
        sem = lambda n: S.sem(f"l_{n}")
        ps = lambda n, shape: ctx.enter_context(nc.psum_tensor(f"l_{n}", shape, FP32))

        w = sb("w", [P, KC, OUT, P])
        wh, wl = sb("w_hi", [P, KC, OUT, P], F32R), sb("w_lo", [P, KC, OUT, P], F32R)
        wo = sb("wo", [P, KC, DM])
        woh, wol = sb("wo_hi", [P, KC, DM], F32R), sb("wo_lo", [P, KC, DM], F32R)
        bias = sb("bias", [P, OUT])
        bv = sb("bv", [P, P])
        bo = sb("bo", [P, DM])
        tables = sb("tables", [P, 2 * TOK])
        cos, sin = tables[:, 0:TOK], tables[:, TOK:2 * TOK]
        rand = sb("rand", [P, MID])
        ones = sb("ones", [P, HT])
        by_cos = [sb(f"by_cos{i}", [P, TB]) for i in range(2)]
        by_sin = [sb(f"by_sin{i}", [P, TB]) for i in range(2)]
        rot = [sb(f"rotated{i}", [P, TB]) for i in range(2)]
        square = [sb(f"square{i}", [P, TB]) for i in range(2)]
        proj = sb("projected", [P, NT, NHD * LE])
        norms = sb("square_norm", [P, NT, NHD])
        v = sb("values", [P, NT, LKV * LD])
        sd, r2 = sb("norm", [P, NT, NHD]), sb("newton", [P, NT, NHD])
        turns = sb("turns", [P, NT, NHD * LE])
        feat = sb("features", [P, NT, NHD, 2, LE])
        half_pi = sb("half_pi", [P, 1])
        att = [sb(f"pair_sums{i}", [P, LH, LKV]) for i in range(2)]
        pairs = [sb(f"pair_products{i}", [P, LF, LH, LKV]) for i in range(2)]
        outs = sb("out_products", [P, LH, LD, LKV])
        o = feat[:, :, :, :, :].rearrange("p t h s e -> p t (h s e)")[:, :, 0:LH * LD]
        z = tables[:, :].rearrange("p (i h d) -> p i h d", i=LD, h=LH)
        zz = feat[:, :, :, :, :].rearrange("p t h s e -> p (t h s e)")[:, 0:LH * LD * LD].rearrange(
            "p (h n) -> p h n", h=LH)
        zh = [sb(f"out_hi{i}", [P, KC, P], F32R) for i in range(2)]
        zl = [sb(f"out_lo{i}", [P, KC, P], F32R) for i in range(2)]

        straight = [ps(f"straight{i}", [P, TB]) for i in range(2)]
        swapped = [ps(f"swapped{i}", [P, TB]) for i in range(2)]
        mid = ps("mid", [P, 2, TB])
        v_ps = ps("v", [P, 2, 2 * P])
        att_ps = ps("pairs", [P, LH, LKV])
        zt = swapped
        zs = straight
        norm = Norm(nc, S, ctx, "n3", "n3", feat[:, :, :, :, :].rearrange("p t h s e -> p (t h s e)")[:, 0:NT * DM].rearrange(
            "p (t d) -> p t d", d=DM), [b_[:, :] for b_ in straight + swapped])
        SUM_AFTER = 7

        loaded, w_loaded, wo_loaded = sem("loaded"), sem("w_loaded"), sem("wo_loaded")
        w_ready, wo_hi, wo_ready, w_hi = sem("w_ready"), sem("wo_hi"), sem("wo_ready"), sem("w_hi")
        made, turned, rotated, squared = sem("made"), sem("cos_sin_used"), sem("rotated"), sem("squared")
        mid_made, mid_stored, v_made, v_stored = sem("mid_made"), sem("mid_stored"), sem("v_made"), sem("v_stored")
        step, norm_ready, sd_ready, angle_ready, abs_ready, feat_ready = (
            sem("step"), sem("norm_ready"), sem("sd_ready"), sem("angle_ready"), sem("abs_ready"), sem("feat_ready"))
        pairs_ready, att_made, att_stored, outs_ready, o_ready = sem("pairs_ready"), sem("att_made"), sem("att_stored"), sem("outs_ready"), sem("o_ready")
        stored, back, ordered = sem("stored"), sem("back"), sem("ordered")
        z_turned, z_hi, z_lo, y_made, y_added = sem("z_turned"), sem("z_hi"), sem("z_lo"), sem("y_made"), sem("y_added")
        block = ctx.enter_context(nc.Block())
        units = [(b, u) for b in range(NB) for u in range(NU)]

        def order(copy, h0):
            return copy(zz[:, h0:h0 + LH // 2, :].rearrange("p h (i d) -> p h i d", d=LD),
                        z[:, :, h0:h0 + LH // 2, :].rearrange("p i h d -> p h i d"))

        @block.sync
        def _(sp):
            sp.dma_start(w[:, :, :, :], w_in).then_inc(w_loaded, 16)
            for dst, src in ((bias[:, :], bias_in), (bv[:, :], bv_in), (bo[:, :], bo_in), (cos[:, :], cos_in),
                             (sin[:, :], sin_in), (rand[:, :], rand_in), (ones[:, :], ones_in)):
                sp.dma_start(dst, src).then_inc(loaded, 16)
            sp.dma_start(wo[:, :, :], wo_in).then_inc(wo_loaded, 16)
            for b in range(NB):
                sp.wait_ge(o_ready, TPB * (b + 1))
                sp.dma_start(scratch[b * TB:(b + 1) * TB, :].rearrange("(t p) n -> p t n", p=P),
                             o[:, b * TPB:(b + 1) * TPB, :]).then_inc(stored, 16)
                sp.wait_ge(stored, 16 * (b + 1))
                sp.wait_ge(turned, len(units))
                sp.dma_start(z[b * TB // LD:(b + 1) * TB // LD, :, :, :].rearrange("p i h d -> p (i h d)"),
                             scratch[b * TB:(b + 1) * TB, :].rearrange("(j i) n -> j (i n)", i=LD)).then_inc(back, 16)
            sp.wait_ge(back, 16 * NB)

        @block.gpsimd
        def _(pool):
            flat = lambda t: t[:, :, :, :].rearrange("p c o n -> p (c o n)")
            pool.wait_ge(w_loaded, 16)
            pool.tensor_copy(flat(wh), flat(w)).then_inc(w_hi, 1)
            pool.wait_ge(w_hi, 1)
            pool.tensor_tensor(flat(wl), flat(w), fp(flat(wh)), ALU.subtract).then_inc(w_ready, 1)
            flat = lambda t: t[:, :, :].rearrange("p c n -> p (c n)")
            pool.wait_ge(wo_loaded, 16)
            pool.tensor_copy(flat(woh), flat(wo)).then_inc(wo_hi, 1)
            pool.wait_ge(wo_hi, 1)
            pool.tensor_tensor(flat(wol), flat(wo), fp(flat(woh)), ALU.subtract).then_inc(wo_ready, 1)
            def multiply(t):
                pool.wait_ge(feat_ready, t // TPB + 1)
                if t >= 2:
                    pool.wait_ge(att_made, t - 1)
                f = feat[:, t, :, :, :].rearrange("p h s e -> p h (s e)")
                pool.tensor_tensor(pairs[t % 2][:, :, :, :].rearrange("p f h k -> p h k f"),
                                   f[:, 0:LH, :].unsqueeze(2).broadcast_to([P, LH, LKV, LF]),
                                   f[:, LH:NHD, :].unsqueeze(1).broadcast_to([P, LH, LKV, LF]),
                                   ALU.mult).then_inc(pairs_ready, 1)

            for n in range(len(units)):
                pool.wait_ge(turned, n + 1)
                if n >= 2:
                    pool.wait_ge(mid_made, n - 1)
                pool.tensor_tensor(rot[n % 2][:, :], by_cos[n % 2][:, :], by_sin[n % 2][:, :], ALU.add).then_inc(rotated, 1)
                if n >= SUM_AFTER - 1:
                    multiply(n - (SUM_AFTER - 1))
            for t in range(len(units) - (SUM_AFTER - 1), NT):
                multiply(t)

        @block.tensor
        def _(pe):
            def project(bank, tile_, b):
                for c in range(KC):
                    for k, (a, x) in enumerate(((wh, S.xh), (wh, S.xl), (wl, S.xh))):
                        mm = pe.matmul(bank, a[:, c, tile_, :], x[:, c, block_of(b)],
                                       start=(c == 0 and k == 0), stop=(c == KC - 1 and k == 2))
                return mm

            def middle(n):
                b, u = units[n]
                pe.wait_ge(rotated, n + 1)
                if u == 0 and b:
                    pe.wait_ge(mid_stored, b)
                for t in range(TPB):
                    at = mid[:, t // 2, (t % 2) * NU * HT * COLS + u * HT * COLS:]
                    pe.matmul(at[:, 0:MID], rot[n % 2][:, t * P:(t + 1) * P], rand[:, :], start=True, stop=True)
                pe.wait_ge(squared, n + 1)
                for t in range(TPB):
                    at = mid[:, t // 2, (t % 2) * NU * HT * COLS + u * HT * COLS:]
                    mm = pe.matmul(at[:, MID:MID + HT], square[n % 2][:, t * P:(t + 1) * P], ones[:, :], start=True, stop=True)
                mm.then_inc(mid_made, 1)

            def add_pairs(t):
                pe.wait_ge(pairs_ready, t + 1)
                if t:
                    pe.wait_ge(att_stored, t)
                for f in range(LF):
                    mm = pe.matmul(att_ps[:, :, :].rearrange("p h k -> p (h k)"), S.ident[:, :],
                                   pairs[t % 2][:, f, :, :].rearrange("p h k -> p (h k)"), start=(f == 0), stop=(f == LF - 1))
                mm.then_inc(att_made, 1)

            norm.tensor(pe)
            norm.done(pe)
            pe.wait_ge(w_ready, 1)
            pe.wait_ge(loaded, 16 * 7)
            for n, (b, u) in enumerate(units):
                if n >= 2:
                    pe.wait_ge(turned, n - 1)
                project(straight[n % 2][:, :], u, b)
                project(swapped[n % 2][:, :], VT + 1 + u, b).then_inc(made, 1)
                if u < 2:
                    if b or u:
                        pe.wait_ge(v_stored, 2 * b + u)
                    for t in range(2):
                        cols = slice((b * TPB + 2 * u + t) * P, (b * TPB + 2 * u + t + 1) * P)
                        for c in range(KC):
                            for k, (x, a) in enumerate(((S.xh, wh), (S.xh, wl), (S.xl, wh))):
                                mm = pe.matmul(v_ps[:, t, :], x[:, c, cols], a[:, c, VT:VT + 2, :].rearrange("p o n -> p (o n)"),
                                               start=(c == 0 and k == 0), stop=(c == KC - 1 and k == 2))
                    mm.then_inc(v_made, 1)
                if n:
                    middle(n - 1)
                if n >= SUM_AFTER:
                    add_pairs(n - SUM_AFTER)
            middle(len(units) - 1)
            for t in range(len(units) - SUM_AFTER, NT):
                add_pairs(t)

            pe.wait_ge(ordered, 2)
            pe.wait_ge(wo_ready, 1)
            pe.wait_ge(v_stored, 2 * NB)

            def turn_head(h):
                if h >= 2:
                    pe.wait_ge(z_lo, h - 1)
                for c in range(KC):
                    mm = pe.transpose(zt[h % 2][:, c * P:(c + 1) * P], zz[:, h, c * P:(c + 1) * P], S.ident[:, :])
                mm.then_inc(z_turned, 1)

            turn_head(0)
            for h in range(LH):
                if h + 1 < LH:
                    turn_head(h + 1)
                pe.wait_ge(z_lo, h + 1)
                if h >= 2:
                    pe.wait_ge(y_added, h - 1)
                for c in range(KC):
                    for k, (a, ww) in enumerate(((zh, woh), (zh, wol), (zl, woh))):
                        mm = pe.matmul(zs[h % 2][:, 0:DM], a[h % 2][:, c, :], ww[:, c, :],
                                       start=(c == 0 and k == 0), stop=(c == KC - 1 and k == 2))
                mm.then_inc(y_made, 1)

        @block.scalar
        def _(act):
            norm.scalar(act)
            def store_middle(b):
                act.wait_ge(mid_made, NU * (b + 1))
                for bank in range(2):
                    m = mid[:, bank, 0:2 * NU * HT * COLS].rearrange("p (t u n) -> p t u n", t=2, u=NU)
                    t = b * TPB + 2 * bank
                    act.activation(proj[:, t:t + 2, :].rearrange("p t (u n) -> p t u n", u=NU), m[:, :, :, 0:MID], ACT.Copy)
                    ins = act.activation(norms[:, t:t + 2, :].rearrange("p t (u n) -> p t u n", u=NU), m[:, :, :, MID:], ACT.Copy)
                ins.then_inc(mid_stored, 1)

            def norm_roots(b):
                tiles = slice(b * TPB, (b + 1) * TPB)
                act.wait_ge(norm_ready, b + 1)
                act.activation(sd[:, tiles, :], norms[:, tiles, :], ACT.Sqrt).then_inc(sd_ready, 1)

            def features(b):
                tiles = slice(b * TPB, (b + 1) * TPB)
                act.wait_ge(angle_ready, b + 1)
                heads = lambda x: x[:, tiles, :].rearrange("p t (h e) -> p (t h) e", e=LE)
                place = lambda s: feat[:, tiles, :, s, :].rearrange("p t h e -> p (t h) e")
                act.activation(turns[:, tiles, :], proj[:, tiles, :], ACT.Abs).then_inc(abs_ready, 1)
                act.activation(place(0), heads(proj), ACT.Sin)
                act.wait_ge(abs_ready, b + 1)
                act.activation(place(1), heads(turns), ACT.Sin, scale=-1.0, bias=half_pi[:, :]).then_inc(feat_ready, 1)

            def store_sums(t):
                act.wait_ge(att_made, t + 1)
                if t >= 2:
                    act.wait_ge(outs_ready, t - 1)
                act.activation(att[t % 2][:, :, :], att_ps[:, :, :], ACT.Copy).then_inc(att_stored, 1)

            for n, (b, u) in enumerate(units):
                act.wait_ge(rotated, n + 1)
                if n >= 2:
                    act.wait_ge(mid_made, n - 1)
                act.activation(square[n % 2][:, :], rot[n % 2][:, :], ACT.Square).then_inc(squared, 1)
                if u == 0 and b:
                    norm_roots(b - 1)
                if u == 2 and b:
                    features(b - 1)
                if u == NU - 1:
                    store_middle(b)
                if n >= SUM_AFTER:
                    store_sums(n - SUM_AFTER)
            norm_roots(NB - 1)
            features(NB - 1)
            for t in range(len(units) - SUM_AFTER, NT):
                store_sums(t)
            act.wait_ge(back, 16 * NB)
            act.wait_ge(att_made, NT)
            order(lambda out, in_: act.activation(out, in_, ACT.Copy), 0).then_inc(ordered, 1)
            for h in range(LH):
                act.wait_ge(z_turned, h + 1)
                if h >= 2:
                    act.wait_ge(y_made, h - 1)
                act.activation(zh[h % 2][:, :, :].rearrange("p c n -> p (c n)"), zt[h % 2][:, 0:DM], ACT.Copy).then_inc(z_hi, 1)

        @block.vector
        def _(dve):
            done = 0

            def after(ins):
                nonlocal done
                done += 1
                ins.then_inc(step, 1)
                dve.wait_ge(step, done)

            norm.vector(dve)
            dve.memset(half_pi[:, :], math.pi / 2)
            dve.wait_ge(loaded, 16 * 7)
            VS = (LH // LKV) / LF
            after(dve.tensor_scalar(bv[:, :], bv[:, :], VS, None, ALU.mult))

            def of_block(b):
                return (a[:, b * TPB:(b + 1) * TPB, :] for a in (sd, r2, norms, turns, proj))

            def limit_norms(b):
                sd_, r2_, norm_, tn, p = of_block(b)
                dve.wait_ge(mid_stored, b + 1)
                dve.tensor_scalar(norm_, norm_, 1e-12, None, ALU.max).then_inc(norm_ready, 1)

            def normalize(b):
                sd_, r2_, norm_, tn, p = of_block(b)
                dve.wait_ge(sd_ready, b + 1)
                after(dve.reciprocal(sd_, sd_))
                after(dve.tensor_tensor(r2_, sd_, sd_, ALU.mult))
                after(dve.tensor_tensor(r2_, r2_, norm_, ALU.mult))
                after(dve.tensor_scalar(r2_, r2_, -0.5, 1.5, ALU.mult, ALU.add))
                after(dve.tensor_tensor(sd_, sd_, r2_, ALU.mult))
                heads = p.rearrange("p t (h e) -> p (t h) e", e=LE)
                after(dve.tensor_tensor(heads, heads, sd_.rearrange("p t h -> p (t h)").unsqueeze(2).broadcast_to(
                    [P, TPB * NHD, LE]), ALU.mult))

            def angles(b):
                sd_, r2_, norm_, tn, p = of_block(b)
                after(dve.tensor_scalar(tn, p, 1 / (2 * math.pi), ROUND, ALU.mult, ALU.add))
                after(dve.tensor_scalar(tn, tn, ROUND, None, ALU.subtract))
                after(dve.scalar_tensor_tensor(out=p, in0=tn, scalar=-TWO_PI_HI, in1=p, op0=ALU.mult, op1=ALU.add))
                after(dve.scalar_tensor_tensor(out=p, in0=tn, scalar=-TWO_PI_LO, in1=p, op0=ALU.mult, op1=ALU.add))
                PI = float(np.nextafter(np.float32(math.pi), np.float32(0)))
                dve.tensor_scalar(p, p, PI, -PI, ALU.min, ALU.max).then_inc(angle_ready, 1)

            def outputs(t):
                dve.wait_ge(att_stored, t + 1)
                if t:
                    dve.wait_ge(o_ready, t)
                dve.tensor_tensor(outs[:, :, :, :], att[t % 2][:, :, :].unsqueeze(2).broadcast_to([P, LH, LD, LKV]),
                                  v[:, t, :].rearrange("p (k d) -> p d k", d=LD).unsqueeze(1).broadcast_to([P, LH, LD, LKV]),
                                  ALU.mult).then_inc(outs_ready, 1)
                dve.wait_ge(outs_ready, t + 1)
                dve.tensor_reduce(o[:, t, :].rearrange("p (h d) -> p h d", d=LD), outs[:, :, :, :], AX.X, ALU.add).then_inc(o_ready, 1)

            for n, (b, u) in enumerate(units):
                i = n % 2
                dve.wait_ge(made, n + 1)
                if n >= 2:
                    dve.wait_ge(rotated, n - 1)
                dve.scalar_tensor_tensor(out=by_cos[i][:, :], in0=straight[i][:, :], scalar=bias[:, u:u + 1],
                                         in1=cos[:, block_of(b)], op0=ALU.add, op1=ALU.mult)
                dve.scalar_tensor_tensor(out=by_sin[i][:, :], in0=swapped[i][:, :], scalar=bias[:, VT + 1 + u:VT + 2 + u],
                                         in1=sin[:, block_of(b)], op0=ALU.add, op1=ALU.mult).then_inc(turned, 1)
                if u < 2:
                    t = b * TPB + 2 * u
                    dve.wait_ge(v_made, 2 * b + u + 1)
                    dve.scalar_tensor_tensor(out=v[:, t:t + 2, :], in0=v_ps[:, :, 0:P], scalar=VS,
                                             in1=bv[:, :].unsqueeze(1).broadcast_to([P, 2, P]),
                                             op0=ALU.mult, op1=ALU.add).then_inc(v_stored, 1)
                if b:
                    (limit_norms, normalize, angles)[u](b - 1)
                if n >= SUM_AFTER + 1:
                    outputs(n - (SUM_AFTER + 1))
            for part in (limit_norms, normalize, angles):
                part(NB - 1)
            for t in range(len(units) - (SUM_AFTER + 1), NT):
                outputs(t)
            for t in range(NT):
                ins = dve.tensor_tensor(S.x[:, t, :], S.x[:, t, :], bo[:, :], ALU.add)
            dve.wait_ge(back, 16 * NB)
            order(dve.tensor_copy, LH // 2).then_inc(ordered, 1)
            for h in range(LH):
                dve.wait_ge(z_hi, h + 1)
                one = lambda z_: z_[h % 2][:, :, :].rearrange("p c n -> p (c n)")
                dve.tensor_tensor(one(zl), zt[h % 2][:, 0:DM], fp(one(zh)), ALU.subtract).then_inc(z_lo, 1)
                if h >= 1:
                    dve.wait_ge(y_made, h)
                    dve.tensor_tensor(S.x[:, h - 1, :], S.x[:, h - 1, :], zs[(h - 1) % 2][:, 0:DM], ALU.add).then_inc(y_added, 1)
            dve.wait_ge(y_made, LH)
            dve.tensor_tensor(S.x[:, LH - 1, :], S.x[:, LH - 1, :], zs[(LH - 1) % 2][:, 0:DM], ALU.add).then_inc(y_added, 1)


def hybrid_block(nc, a, out):
    scratch = nc.dram_tensor("heads_by_token", (TOK, DM), FP32).ap()
    with ExitStack() as ctx:
        S = Shared(nc, ctx)
        attention_stage(nc, S, a["x"], a["identity"], a["wqkv_codes"], a["wqkv_scales"], a["wo_codes"], a["wo_scales"], a["bo"])
        for i in range(2):
            if i == 1:
                clear_stage(nc, S, ("mn", "mr", "me"))
            with ExitStack() as moe:
                combine = moe.enter_context(nc.sbuf_tensor(f"combine{i}", [NC * NE, TOK], BF16))
                experts = Experts(nc, S, moe, "me", f"me{i}", a["experts_w"], a["select"].bitcast(BF16))
                moe_stage(nc, S, "mr", f"mr{i}", a["gate_w"], a["similarity"], a["notdiag"], a["iota"], combine, experts,
                          out if i else None)
            if i == 0:
                linear_stage(nc, S, a["lin_w"], a["lin_bias"], a["lin_bv"], a["lin_wo"], a["lin_bo"], a["cos"],
                             a["sin"], a["rand"], a["ones"], scratch)


def _arrays(d):
    A = lambda n: np.asarray(d["L0_attn_a_" + n])
    B = lambda n: np.asarray(d["L0_attn_b_" + n])
    F = lambda n: np.asarray(d["L0_ffn_" + n])
    f32 = np.float32
    out = {"x": A("x").reshape(TOK, DM), "identity": np.eye(P, dtype=f32)}

    def by_head(w):
        return w.reshape(KC, P, NH, HD).transpose(2, 1, 0, 3)

    def wrap(w, n):
        return np.concatenate([w, w[:n]], 0)

    codes = np.stack([by_head(A(f"w{m}_codes")) for m in "qkv"], 2).reshape(NH, P, -1)
    scales = np.stack([by_head(np.repeat(A(f"w{m}_scales"), 32, 0)) for m in "qkv"], 2).reshape(NH, P, -1)
    biases = np.stack([A("b" + m).reshape(NH, HD) for m in "qkv"], 2)
    out["wqkv_codes"] = wrap(np.concatenate([codes, biases], 2), 2)
    out["wqkv_scales"] = wrap(scales, 2)
    out["wo_codes"] = wrap(A("wo_codes").reshape(NH, HD, DM), 1)
    out["wo_scales"] = wrap(np.repeat(A("wo_scales"), 32, 0).reshape(NH, HD, DM), 1)
    out["bo"] = np.broadcast_to(A("bo"), (P, DM))

    gu = F("gate_up_proj")
    turn = lambda w: w.reshape(JT, P, KC, P).transpose(0, 3, 2, 1).reshape(JT, P, DM)
    gate, up = turn(gu[:, :FF].reshape(NF, DM)), turn(gu[:, FF:].reshape(NF, DM))
    down = F("down_proj").transpose(0, 2, 1).reshape(JT, P, DM)
    out["experts_w"] = np.concatenate([gate, up, down], 2)
    select = np.zeros((JT, NC, NE, P), np.uint16)
    for j in range(JT):
        for f in range(P):
            select[j, :, (j * P + f) // FF, f] = 0x3F80
    out["select"] = select.reshape(JT, NC * NE, P)
    out["gate_w"] = np.zeros((P, KC, P), f32)
    out["gate_w"][:, :, 0:NE] = F("gate_weight").T.reshape(KC, P, NE).transpose(1, 0, 2)
    sim = np.zeros((P, P), f32)
    for s in range(SEC):
        sim[s * NE:(s + 1) * NE, s * NE:(s + 1) * NE] = F("similarity")
    out["similarity"] = sim
    out["notdiag"] = 1 - np.eye(P, dtype=f32)
    out["iota"] = np.broadcast_to(np.arange(NE, dtype=f32), (P, NE))

    def swap(w):
        w = w.reshape(-1, 2, LD // 2, *w.shape[1:])
        return w[:, ::-1].reshape(-1, *w.shape[3:])

    rows = lambda f: np.concatenate([B(f + "q"), B(f + "k"), B(f + "v"), swap(B(f + "q")), swap(B(f + "k"))], 0)
    out["lin_w"] = rows("W").reshape(7, P, KC, P).transpose(3, 2, 0, 1)
    out["lin_bias"] = rows("b").reshape(7, P).T
    out["lin_bv"] = np.broadcast_to(B("bv"), (P, P))
    out["lin_wo"] = B("Wo").T.reshape(KC, P, DM).transpose(1, 0, 2)
    out["lin_bo"] = np.broadcast_to(B("bo"), (P, DM))
    inv = (f32(1) / f32(10000.0) ** (np.arange(0, LD, 2, dtype=f32) / f32(LD))).astype(f32)
    angle = (np.arange(TOK, dtype=f32)[:, None] * inv[None, :]).astype(f32).astype(np.float64)
    sign = np.where(np.arange(P) % LD < LD // 2, -1.0, 1.0)[:, None]
    out["cos"] = np.cos(angle).T[np.arange(P) % (LD // 2)].astype(f32)
    out["sin"] = (np.sin(angle).T[np.arange(P) % (LD // 2)] * sign).astype(f32)
    rand, ones = np.zeros((P, 8, LE), f32), np.zeros((P, 8), f32)
    for h in range(8):
        rand[h * LD:(h + 1) * LD, h] = B("rand_matrix").T
        ones[h * LD:(h + 1) * LD, h] = 1
    out["rand"], out["ones"] = rand.reshape(P, -1), ones
    return {k: np.ascontiguousarray(v) for k, v in out.items()}


def kernel(**inputs):
    from concourse import bacc
    from concourse.bass_utils import run_bass_kernel_spmd

    nc = bacc.Bacc("TRN2", target_bir_lowering=False, num_devices=1)
    arrays = _arrays(inputs)
    args = {n: nc.dram_tensor("in_" + n, v.shape, mybir.dt.from_np(v.dtype), kind="ExternalInput").ap()
            for n, v in arrays.items()}
    out = nc.dram_tensor("out", (TOK, DM), FP32, kind="ExternalOutput").ap()
    hybrid_block(nc, args, out)
    r = run_bass_kernel_spmd(nc, [{"in_" + n: v for n, v in arrays.items()}], core_ids=[0])
    return r.results[0]["out"].reshape(1, TOK, DM)
```
